# Optimizing a Trainium2 kernel written in Bass

```python
import numpy as np
import jax
import jax.numpy as jnp

def _softmax(x, axis=-1):
    return jax.nn.softmax(x, axis=axis)

def _gelu(x):
    return jax.nn.gelu(x, approximate=True)

def _silu(x):
    return jax.nn.silu(x)

def _sigmoid(x):
    return jax.nn.sigmoid(x)

def _layernorm(x, axis=-1, eps=1e-05):
    m = jnp.mean(x, axis=axis, keepdims=True)
    v = jnp.var(x, axis=axis, keepdims=True)
    return (x - m) / jnp.sqrt(v + eps)

def _scatter_add(tgt, idx, src, axis=0):
    return tgt.at[idx].add(src)

def _segment_sum(src, seg, n):
    return jax.ops.segment_sum(src, seg, n)
kernel_name = 'mk_decoder_postln_d2_seqx_r4_657943'

def setup_inputs(seed: int=0):
    np.random.seed(seed)
    _w = jnp.asarray

    def _rec_inputs():
        import jax
        import jax.numpy as jnp
        _rk = jax.random.key(seed)
        x = -0.0002928 + 1 * jax.random.normal(jax.random.fold_in(_rk, 1), (16, 100, 256), jnp.float32)
        _lenS = 100 - jax.random.randint(jax.random.fold_in(_rk, 7), (16,), 0, max(1, 100 // 4) + 1, jnp.int32)
        _lenS2 = 361 - jax.random.randint(jax.random.fold_in(_rk, 8), (16,), 0, max(1, 361 // 4) + 1, jnp.int32)
        _ctx_768P = jax.random.normal(jax.random.fold_in(_rk, 11), (16, 16, 192), jnp.float32)
        _ctx_768c = jax.random.dirichlet(jax.random.fold_in(_rk, 511), 0.3 * jnp.ones((16,), jnp.float32), (16, 361))
        _ctx_768t = jnp.einsum('bsk,bkd->bsd', _ctx_768c, _ctx_768P)
        _ctx_768t = _ctx_768t * jax.lax.rsqrt(jnp.mean(jnp.square(_ctx_768t)) + 1e-12) * 0.953939
        ctx_768 = -8.43904e-05 + 0.999875 * (_ctx_768t + 0.3 * jax.random.normal(jax.random.fold_in(_rk, 611), (16, 361, 192), jnp.float32))
        _validS = jnp.arange(100)[None, :] < _lenS[:, None]
        _validS2 = jnp.arange(361)[None, :] < _lenS2[:, None]
        _causal = jnp.tril(jnp.ones((100, 100), dtype=bool))
        mask_BxS2_bf1 = jnp.ones((16, 361), dtype=bool)
        return (x, ctx_768, mask_BxS2_bf1)
    x, ctx_768, mask_BxS2_bf1 = _rec_inputs()

    def _L0_attn_setup():
        import math
        import jax, jax.numpy as jnp
        import numpy as np
        HEADS = 16
        REL_WINDOW = 128
        key = jax.random.key(seed)
        k1, k2, k3, k4, k5 = jax.random.split(key, 5)
        b, s, d = (2, 512, 256)
        hd = d // HEADS
        R = 2 * REL_WINDOW + 1
        return {'x': jax.random.normal(k1, (b, s, d), dtype=jnp.float32), 'Wqkv': jax.random.normal(k2, (3 * d, d), dtype=jnp.float32) * (1.0 / math.sqrt(d)), 'bqkv': jax.random.normal(k3, (3 * d,), dtype=jnp.float32) * 0.02, 'Wr': jax.random.normal(k4, (R, hd), dtype=jnp.float32) * (1.0 / math.sqrt(hd)), 'br': jax.random.normal(k5, (R,), dtype=jnp.float32) * 0.02}
    _L0_attn_all = _L0_attn_setup()
    _L0_attn_in = {k: v for k, v in _L0_attn_all.items() if k in ('Wqkv', 'bqkv', 'Wr', 'br')}
    del _L0_attn_all

    def _L0_xattn_setup():
        import jax, jax.numpy as jnp
        import numpy as np
        LATENT_CH = 256
        INPUT_CH = 192
        QK_CH = 256
        V_CH = 256
        OUT_CH = 256
        NHEADS = 8
        EPS = 1e-05

        def layer_norm(x, gamma, beta):
            mu = jnp.mean(x, axis=-1, keepdims=True)
            var = jnp.var(x, axis=-1, keepdims=True)
            return (x - mu) * jax.lax.rsqrt(var + EPS) * gamma + beta
        key = jax.random.key(seed)
        ks = jax.random.split(key, 6)
        B, Lq, Lkv = (8, 128, 4096)
        latent_q = jax.random.normal(ks[0], (B, Lq, LATENT_CH), dtype=jnp.float32)
        input_kv = jax.random.normal(ks[1], (B, Lkv, INPUT_CH), dtype=jnp.float32)
        W_Q = jax.random.normal(ks[2], (LATENT_CH, QK_CH), dtype=jnp.float32) / np.sqrt(LATENT_CH)
        W_K = jax.random.normal(ks[3], (INPUT_CH, QK_CH), dtype=jnp.float32) / np.sqrt(INPUT_CH)
        W_V = jax.random.normal(ks[4], (INPUT_CH, V_CH), dtype=jnp.float32) / np.sqrt(INPUT_CH)
        W_O = jax.random.normal(ks[5], (V_CH, OUT_CH), dtype=jnp.float32) / np.sqrt(V_CH)
        ln_lat_g = jnp.ones((LATENT_CH,), jnp.float32)
        ln_lat_b = jnp.zeros((LATENT_CH,), jnp.float32)
        ln_in_g = jnp.ones((INPUT_CH,), jnp.float32)
        ln_in_b = jnp.zeros((INPUT_CH,), jnp.float32)
        return dict(latent_q=latent_q, input_kv=input_kv, W_Q=W_Q, W_K=W_K, W_V=W_V, W_O=W_O, ln_lat_g=ln_lat_g, ln_lat_b=ln_lat_b, ln_in_g=ln_in_g, ln_in_b=ln_in_b)
    _L0_xattn_all = _L0_xattn_setup()
    _L0_xattn_in = {k: v for k, v in _L0_xattn_all.items() if k in ('W_Q', 'W_K', 'W_V', 'W_O', 'ln_lat_g', 'ln_lat_b', 'ln_in_g', 'ln_in_b')}
    del _L0_xattn_all

    def _L0_ffn_setup():
        import jax, jax.numpy as jnp
        import numpy as np
        D_MODEL, D_FF, RANK = (256, 1024, 64)
        B, S = (4, 1024)
        key = jax.random.key(seed)
        ks = jax.random.split(key, 7)
        return {'x': jax.random.normal(ks[0], (B, S, D_MODEL), dtype=jnp.float32), 'U1': jax.random.normal(ks[1], (D_MODEL, RANK), dtype=jnp.float32) * 0.02, 'V1': jax.random.normal(ks[2], (RANK, D_FF), dtype=jnp.float32) * 0.02, 'b1': jnp.zeros((D_FF,), dtype=jnp.float32), 'U2': jax.random.normal(ks[3], (D_FF, RANK), dtype=jnp.float32) * 0.02, 'V2': jax.random.normal(ks[4], (RANK, D_MODEL), dtype=jnp.float32) * 0.02, 'b2': jnp.zeros((D_MODEL,), dtype=jnp.float32)}
    _L0_ffn_all = _L0_ffn_setup()
    _L0_ffn_in = {k: v for k, v in _L0_ffn_all.items() if k in ('U1', 'V1', 'b1', 'U2', 'V2', 'b2')}
    del _L0_ffn_all

    def _L1_attn_setup():
        import jax, jax.numpy as jnp
        import numpy as np
        D_MODEL = 256
        N_HEADS = 16
        D_HEAD = D_MODEL // N_HEADS
        M_SLOPE = 0.5
        BATCH = 2
        SEQ = 512

        def _alibi_bias(n_heads, seq_len, m, dtype):
            slopes = m ** jnp.arange(n_heads, dtype=dtype)
            pos = jnp.arange(seq_len, dtype=dtype)
            dist = jnp.abs(pos[:, None] - pos[None, :])
            return -dist[None, :, :] * slopes[:, None, None]
        key = jax.random.key(seed)
        k1, k2, k3 = jax.random.split(key, 3)
        x = jax.random.normal(k1, (BATCH, SEQ, D_MODEL), dtype=jnp.float32)
        qkv_w = jax.random.normal(k2, (3 * D_MODEL, D_MODEL), dtype=jnp.float32) * (1.0 / np.sqrt(D_MODEL))
        qkv_b = jnp.zeros((3 * D_MODEL,), dtype=jnp.float32)
        out_w = jax.random.normal(k3, (D_MODEL, D_MODEL), dtype=jnp.float32) * (1.0 / np.sqrt(D_MODEL))
        out_b = jnp.zeros((D_MODEL,), dtype=jnp.float32)
        return {'x': x, 'qkv_w': qkv_w, 'qkv_b': qkv_b, 'out_w': out_w, 'out_b': out_b}
    _L1_attn_all = _L1_attn_setup()
    _L1_attn_in = {k: v for k, v in _L1_attn_all.items() if k in ('qkv_w', 'qkv_b', 'out_w', 'out_b')}
    del _L1_attn_all

    def _L1_xattn_setup():
        import jax, jax.numpy as jnp
        import numpy as np
        DIM = 256
        CTX_DIM = 192
        HEADS = 16
        key = jax.random.key(seed)
        ks = jax.random.split(key, 7)
        B, N, M = (4, 1024, 64)
        x = jax.random.normal(ks[0], (B, N, DIM), dtype=jnp.float32)
        context = jax.random.normal(ks[1], (B, M, CTX_DIM), dtype=jnp.float32)
        context_mask = jnp.ones((B, M), dtype=bool)
        s_d = 1.0 / np.sqrt(DIM)
        s_c = 1.0 / np.sqrt(CTX_DIM)
        Wq = jax.random.normal(ks[2], (DIM, DIM), dtype=jnp.float32) * s_d
        Wk = jax.random.normal(ks[3], (CTX_DIM, DIM), dtype=jnp.float32) * s_c
        Wv = jax.random.normal(ks[4], (CTX_DIM, DIM), dtype=jnp.float32) * s_c
        Wo = jax.random.normal(ks[5], (DIM, DIM), dtype=jnp.float32) * s_d
        return {'x': x, 'context': context, 'context_mask': context_mask, 'Wq': Wq, 'Wk': Wk, 'Wv': Wv, 'Wo': Wo}
    _L1_xattn_all = _L1_xattn_setup()
    _L1_xattn_in = {k: v for k, v in _L1_xattn_all.items() if k in ('Wq', 'Wk', 'Wv', 'Wo')}
    del _L1_xattn_all

    def _L1_ffn_setup():
        import jax, jax.numpy as jnp
        import numpy as np
        QMAX = 127.0

        def _quant_dequant(w):
            scale = jnp.max(jnp.abs(w), axis=-1, keepdims=True) / QMAX
            scale = jnp.maximum(scale, 1e-08)
            q = jnp.clip(jnp.round(w / scale), -QMAX, QMAX)
            return q * scale
        key = jax.random.key(seed)
        ks = jax.random.split(key, 7)
        B, S, D, F, E, NS = (2, 512, 256, 512, 8, 1)
        std = 1.0 / np.sqrt(D)
        x = jax.random.normal(ks[0], (B, S, D), dtype=jnp.float32)
        router_w = _quant_dequant(jax.random.normal(ks[1], (E, D), dtype=jnp.float32) * std)
        router_b = jnp.zeros((E,), dtype=jnp.float32)
        w_up = _quant_dequant(jax.random.normal(ks[2], (E, F, D), dtype=jnp.float32) * std)
        w_down = _quant_dequant(jax.random.normal(ks[3], (E, D, F), dtype=jnp.float32) / np.sqrt(F))
        shared_w_up = _quant_dequant(jax.random.normal(ks[4], (NS, F, D), dtype=jnp.float32) * std)
        shared_w_down = _quant_dequant(jax.random.normal(ks[5], (NS, D, F), dtype=jnp.float32) / np.sqrt(F))
        return {'x': x, 'router_w': router_w, 'router_b': router_b, 'w_up': w_up, 'w_down': w_down, 'shared_w_up': shared_w_up, 'shared_w_down': shared_w_down}
    _L1_ffn_all = _L1_ffn_setup()
    _L1_ffn_in = {k: v for k, v in _L1_ffn_all.items() if k in ('router_w', 'router_b', 'w_up', 'w_down', 'shared_w_up', 'shared_w_down')}
    del _L1_ffn_all
    return {'x': x, 'ctx_768': ctx_768, 'mask_BxS2_bf1': mask_BxS2_bf1, 'L0_attn_Wqkv': _L0_attn_in['Wqkv'], 'L0_attn_bqkv': _L0_attn_in['bqkv'], 'L0_attn_Wr': _L0_attn_in['Wr'], 'L0_attn_br': _L0_attn_in['br'], 'L0_xattn_W_Q': _L0_xattn_in['W_Q'], 'L0_xattn_W_K': _L0_xattn_in['W_K'], 'L0_xattn_W_V': _L0_xattn_in['W_V'], 'L0_xattn_W_O': _L0_xattn_in['W_O'], 'L0_xattn_ln_lat_g': _L0_xattn_in['ln_lat_g'], 'L0_xattn_ln_lat_b': _L0_xattn_in['ln_lat_b'], 'L0_xattn_ln_in_g': _L0_xattn_in['ln_in_g'], 'L0_xattn_ln_in_b': _L0_xattn_in['ln_in_b'], 'L0_ffn_U1': _L0_ffn_in['U1'], 'L0_ffn_V1': _L0_ffn_in['V1'], 'L0_ffn_b1': _L0_ffn_in['b1'], 'L0_ffn_U2': _L0_ffn_in['U2'], 'L0_ffn_V2': _L0_ffn_in['V2'], 'L0_ffn_b2': _L0_ffn_in['b2'], 'L1_attn_qkv_w': _L1_attn_in['qkv_w'], 'L1_attn_qkv_b': _L1_attn_in['qkv_b'], 'L1_attn_out_w': _L1_attn_in['out_w'], 'L1_attn_out_b': _L1_attn_in['out_b'], 'L1_xattn_Wq': _L1_xattn_in['Wq'], 'L1_xattn_Wk': _L1_xattn_in['Wk'], 'L1_xattn_Wv': _L1_xattn_in['Wv'], 'L1_xattn_Wo': _L1_xattn_in['Wo'], 'L1_ffn_router_w': _L1_ffn_in['router_w'], 'L1_ffn_router_b': _L1_ffn_in['router_b'], 'L1_ffn_w_up': _L1_ffn_in['w_up'], 'L1_ffn_w_down': _L1_ffn_in['w_down'], 'L1_ffn_shared_w_up': _L1_ffn_in['shared_w_up'], 'L1_ffn_shared_w_down': _L1_ffn_in['shared_w_down']}

def reference(x, ctx_768, mask_BxS2_bf1, L0_attn_Wqkv, L0_attn_bqkv, L0_attn_Wr, L0_attn_br, L0_xattn_W_Q, L0_xattn_W_K, L0_xattn_W_V, L0_xattn_W_O, L0_xattn_ln_lat_g, L0_xattn_ln_lat_b, L0_xattn_ln_in_g, L0_xattn_ln_in_b, L0_ffn_U1, L0_ffn_V1, L0_ffn_b1, L0_ffn_U2, L0_ffn_V2, L0_ffn_b2, L1_attn_qkv_w, L1_attn_qkv_b, L1_attn_out_w, L1_attn_out_b, L1_xattn_Wq, L1_xattn_Wk, L1_xattn_Wv, L1_xattn_Wo, L1_ffn_router_w, L1_ffn_router_b, L1_ffn_w_up, L1_ffn_w_down, L1_ffn_shared_w_up, L1_ffn_shared_w_down):
    import jax
    import jax.numpy as jnp

    def _L0_attn_ref(x, Wqkv, bqkv, Wr, br):
        import math
        import jax, jax.numpy as jnp
        import numpy as np
        HEADS = 16
        REL_WINDOW = 128
        b, s, d = x.shape
        h = HEADS
        hd = d // h
        w = REL_WINDOW
        scale = math.sqrt(d / h)
        qkv = (x @ Wqkv.T + bqkv).reshape(b, s, h, 3 * hd)
        q, k, v = jnp.split(qkv, 3, axis=-1)
        q = q.transpose(0, 2, 1, 3)
        k = k.transpose(0, 2, 1, 3)
        v = v.transpose(0, 2, 1, 3)
        content = jnp.einsum('bhik,bhjk->bhij', q, k) / scale
        idx = jnp.arange(s)
        offsets = jnp.clip(idx[None, :] - idx[:, None], -w, w) + w
        rp = jnp.einsum('bhik,rk->bhir', q, Wr) + br
        pos = jnp.take_along_axis(rp, jnp.broadcast_to(offsets, (b, h, s, s)), axis=-1)
        attn = jax.nn.softmax(content + pos, axis=-1)
        out = jnp.einsum('bhij,bhjk->bhik', attn, v)
        return out.transpose(0, 2, 1, 3).reshape(b, s, d)

    def _L0_xattn_ref(latent_q, input_kv, W_Q, W_K, W_V, W_O, ln_lat_g, ln_lat_b, ln_in_g, ln_in_b):
        import jax, jax.numpy as jnp
        import numpy as np
        LATENT_CH = 256
        INPUT_CH = 192
        QK_CH = 256
        V_CH = 256
        OUT_CH = 256
        NHEADS = 8
        EPS = 1e-05

        def layer_norm(x, gamma, beta):
            mu = jnp.mean(x, axis=-1, keepdims=True)
            var = jnp.var(x, axis=-1, keepdims=True)
            return (x - mu) * jax.lax.rsqrt(var + EPS) * gamma + beta
        B, Lq, _ = latent_q.shape
        _, Lkv, _ = input_kv.shape
        H = NHEADS
        dqk = QK_CH // H
        dv = V_CH // H
        lat = layer_norm(latent_q, ln_lat_g, ln_lat_b)
        inp = layer_norm(input_kv, ln_in_g, ln_in_b)
        Q = (lat @ W_Q).reshape(B, Lq, H, dqk)
        K = (inp @ W_K).reshape(B, Lkv, H, dqk)
        V = (inp @ W_V).reshape(B, Lkv, H, dv)
        scale = 1.0 / np.sqrt(dqk).astype(np.float32)
        attn = jnp.einsum('bqhd,bkhd->bhqk', Q, K) * scale
        attn = jax.nn.softmax(attn, axis=-1)
        out = jnp.einsum('bhqk,bkhd->bqhd', attn, V).reshape(B, Lq, V_CH)
        return out @ W_O

    def _L0_ffn_ref(x, U1, V1, b1, U2, V2, b2):
        import jax, jax.numpy as jnp
        import numpy as np
        D_MODEL, D_FF, RANK = (256, 1024, 64)
        B, S = (4, 1024)
        P = jnp.einsum('bsd,dr->bsr', x, U1)
        H = jax.nn.gelu(jnp.einsum('bsr,rf->bsf', P, V1) + b1)
        Q = jnp.einsum('bsf,fr->bsr', H, U2)
        return jnp.einsum('bsr,rd->bsd', Q, V2) + b2

    def _L1_attn_ref(x, qkv_w, qkv_b, out_w, out_b):
        import jax, jax.numpy as jnp
        import numpy as np
        D_MODEL = 256
        N_HEADS = 16
        D_HEAD = D_MODEL // N_HEADS
        M_SLOPE = 0.5
        BATCH = 2
        SEQ = 512

        def _alibi_bias(n_heads, seq_len, m, dtype):
            slopes = m ** jnp.arange(n_heads, dtype=dtype)
            pos = jnp.arange(seq_len, dtype=dtype)
            dist = jnp.abs(pos[:, None] - pos[None, :])
            return -dist[None, :, :] * slopes[:, None, None]
        batch, seq_len, d_model = x.shape
        qkv = x @ qkv_w.T + qkv_b
        qkv = qkv.reshape(batch, seq_len, N_HEADS, 3 * D_HEAD).transpose(0, 2, 1, 3)
        q, k, v = jnp.split(qkv, 3, axis=-1)
        scale = jnp.sqrt(jnp.asarray(D_HEAD, dtype=x.dtype))
        scores = jnp.einsum('bhid,bhjd->bhij', q, k) / scale
        scores = scores + _alibi_bias(N_HEADS, seq_len, M_SLOPE, x.dtype)[None]
        attn = jax.nn.softmax(scores, axis=-1)
        out = jnp.einsum('bhij,bhjd->bhid', attn, v)
        out = out.transpose(0, 2, 1, 3).reshape(batch, seq_len, d_model)
        return out @ out_w.T + out_b

    def _L1_xattn_ref(x, context, context_mask, Wq, Wk, Wv, Wo):
        import jax, jax.numpy as jnp
        import numpy as np
        DIM = 256
        CTX_DIM = 192
        HEADS = 16
        B, N, _ = x.shape
        M = context.shape[1]
        hd = DIM // HEADS
        scale = hd ** (-0.5)
        q = (x @ Wq).reshape(B, N, HEADS, hd).transpose(0, 2, 1, 3)
        k = (context @ Wk).reshape(B, M, HEADS, hd).transpose(0, 2, 1, 3)
        v = (context @ Wv).reshape(B, M, HEADS, hd).transpose(0, 2, 1, 3)
        scores = jnp.einsum('bhid,bhjd->bhij', q, k) * scale
        max_neg = -jnp.finfo(scores.dtype).max
        scores = jnp.where(context_mask[:, None, None, :], scores, max_neg)
        attn = jax.nn.softmax(scores, axis=-1)
        out = jnp.einsum('bhij,bhjd->bhid', attn, v)
        out = out.transpose(0, 2, 1, 3).reshape(B, N, DIM)
        return out @ Wo

    def _L1_ffn_ref(x, router_w, router_b, w_up, w_down, shared_w_up, shared_w_down):
        import jax, jax.numpy as jnp
        import numpy as np
        QMAX = 127.0

        def _quant_dequant(w):
            scale = jnp.max(jnp.abs(w), axis=-1, keepdims=True) / QMAX
            scale = jnp.maximum(scale, 1e-08)
            q = jnp.clip(jnp.round(w / scale), -QMAX, QMAX)
            return q * scale
        B, S, D = x.shape
        E = router_w.shape[0]
        TOPK = 2
        xt = x.reshape(-1, D)
        logits = xt @ router_w.T + router_b
        probs = jax.nn.softmax(logits, axis=-1)
        top_vals, top_idx = jax.lax.top_k(probs, TOPK)
        top_vals = top_vals / jnp.sum(top_vals, axis=-1, keepdims=True)
        combine = jnp.sum(jax.nn.one_hot(top_idx, E, dtype=xt.dtype) * top_vals[..., None], axis=1)
        h = jnp.einsum('td,efd->tef', xt, w_up)
        y = jnp.einsum('tef,edf->ted', jax.nn.silu(h), w_down)
        out = jnp.einsum('ted,te->td', y, combine)
        hs = jnp.einsum('td,sfd->tsf', xt, shared_w_up)
        out = out + jnp.einsum('tsf,sdf->td', jax.nn.silu(hs), shared_w_down)
        return out.reshape(B, S, D)
    x = _layernorm(x + _L0_attn_ref(x, L0_attn_Wqkv, L0_attn_bqkv, L0_attn_Wr, L0_attn_br), axis=-1)
    x = _layernorm(x + _L0_xattn_ref(x, ctx_768, L0_xattn_W_Q, L0_xattn_W_K, L0_xattn_W_V, L0_xattn_W_O, L0_xattn_ln_lat_g, L0_xattn_ln_lat_b, L0_xattn_ln_in_g, L0_xattn_ln_in_b), axis=-1)
    x = _layernorm(x + _L0_ffn_ref(x, L0_ffn_U1, L0_ffn_V1, L0_ffn_b1, L0_ffn_U2, L0_ffn_V2, L0_ffn_b2), axis=-1)
    x = _layernorm(x + _L1_attn_ref(x, L1_attn_qkv_w, L1_attn_qkv_b, L1_attn_out_w, L1_attn_out_b), axis=-1)
    x = _layernorm(x + _L1_xattn_ref(x, ctx_768, mask_BxS2_bf1, L1_xattn_Wq, L1_xattn_Wk, L1_xattn_Wv, L1_xattn_Wo), axis=-1)
    x = _layernorm(x + _L1_ffn_ref(x, L1_ffn_router_w, L1_ffn_router_b, L1_ffn_w_up, L1_ffn_w_down, L1_ffn_shared_w_up, L1_ffn_shared_w_down), axis=-1)
    return x

_drawn_inputs = setup_inputs


def setup_inputs(seed=0):
    import zlib

    import numpy as np

    out = dict(_drawn_inputs(seed))
    spreads = {'L0_xattn_ln_lat_g': (1.0, 0.2),
     'L0_xattn_ln_lat_b': (0.0, 0.1),
     'L0_xattn_ln_in_g': (1.0, 0.2),
     'L0_xattn_ln_in_b': (0.0, 0.1),
     'L0_ffn_b1': (0.0, 0.308),
     'L0_ffn_b2': (0.0, 0.1),
     'L1_attn_qkv_b': (0.0, 0.1),
     'L1_attn_out_b': (0.0, 0.1),
     'L1_ffn_router_b': (0.0, 0.1)}
    factors = {'L0_attn_br': 3.387, 'L0_ffn_U1': 4.082, 'L0_ffn_V1': 3.685, 'L0_ffn_V2': 2.945}
    for name, (base, spread) in spreads.items():
        noise = np.random.default_rng([zlib.crc32(name.encode()), seed]).standard_normal(out[name].shape)
        drawn = base * np.exp(spread * noise) if base else spread * noise
        out[name] = jnp.asarray(drawn.astype(out[name].dtype))
    for name, factor in factors.items():
        out[name] = (out[name] * factor).astype(out[name].dtype)
    return out
```

```python
from contextlib import ExitStack

import concourse.bass as bass
from concourse import mybir
from concourse.alu_op_type import AluOpType as ALU

ACT = mybir.ActivationFunctionType
AX = mybir.AxisListType.X
F32, BF16, U8 = mybir.dt.float32, mybir.dt.bfloat16, mybir.dt.uint8

B, T, D = 16, 100, 256
S, DC = 361, 192
G = 4
GT = G * T
C = D // 128
CK = DC // 2
JT = [(0, 128), (128, 128), (256, S - 256)]
FF, RANK = 1024, 64
E, F = 8, 512
NE = E + 1
FC = F // 128
NR = 257
REL0 = 128
HALO = 28
BIG = 3.3895313892515355e38
EPS = 1e-5
PIECES = [0, 0, 1, 0, 2, 1]
WPIECES = [0, 1, 0, 2, 0, 1]
NSTACK = 16 * len(PIECES)
WSLOTS = 3
LAG = 2

USES = {
    "pk0": dict(X0=1, S0=4, P1=3, X1=1, C1=2 + 9, X2=1, F2=1, X3=1, S3=4, P4=2, X4=1, C4=2 + 6, X5=1, M5=1),
    "pk1": dict(X0=1, S0=4, P1=4, X1=1, C1=12, X2=1, X3=1, S3=4, P4=3, X4=1, C4=9, X5=1, M5=E),
    "pa": dict(S0=7 + 32, C1=32, S3=16, C4=64, M5=2),
    "pb": dict(S0=6 + 16, C1=24, F2=8, S3=16, C4=48, M5=NE * FC),
    "po": dict(S0=4, C1=4, F2=1, S3=4, C4=4),
    "ps": dict(S0=4, C1=12, F2=4, S3=12, C4=12, M5=5),
    "pv": dict(S0=16, C1=8, S3=16, C4=16),
}
DEPTH = {"pa": 2, "pb": 2, "pk0": 1, "pk1": 1, "po": 1, "ps": 1}


def nth(ring, phase, i):
    before = 0
    for name, uses in USES[ring].items():
        if name == phase:
            assert i < uses, (ring, phase, i)
            return before + i + 1
        before += uses
    raise KeyError(phase)


class Self:
    heads, scale, hgs, keys, tiles = 16, 0.25, 4, T, [(0, T)]

    def __init__(self, phase, relative):
        self.p, self.relative = phase, relative


class Cross:
    keys, tiles, relative = S, JT, False

    def __init__(self, phase, pre, heads, scale, masked):
        self.p, self.pre, self.heads, self.scale, self.masked = phase, pre, heads, scale, masked
        self.hgs = heads // 4


SELF0, SELF3 = Self("S0", True), Self("S3", False)
CROSS1 = Cross("C1", "P1", 8, float(32 ** -0.5), False)
CROSS4 = Cross("C4", "P4", 16, 0.25, True)


def decoder(nc, a, out):
    with ExitStack() as ctx:
        def sb(name, shape, dt=F32):
            return ctx.enter_context(nc.sbuf_tensor(name, shape, dt))

        def sem(name):
            return ctx.enter_context(nc.semaphore(name))

        wqkv = {0: sb("wqkv0", [128, C, 3 * D]), 3: sb("wqkv3", [128, C, 3 * D])}
        bqk = {0: sb("bqk0", [128, 4]), 3: sb("bqk3", [128, 4])}
        bv = {0: sb("bv0", [T, D]), 3: sb("bv3", [T, D])}
        wq = {1: sb("wq1", [128, C, D]), 4: sb("wq4", [128, C, D])}
        wk = {1: sb("wk1", [CK, 2, D]), 4: sb("wk4", [CK, 2, D])}
        wv = {1: sb("wv1", [CK, 2, D]), 4: sb("wv4", [CK, 2, D])}
        wo = {1: sb("wo1", [128, C, D]), 3: sb("wo3", [128, C, D]), 4: sb("wo4", [128, C, D])}
        bo3 = sb("bo3", [T, D])
        lat_gb = sb("lat_gb", [128, 4])
        in_gb = sb("in_gb", [CK, 4])
        u1, v1 = sb("u1", [128, C, 128]), sb("v1", [128, FF])
        u2, v2 = sb("u2", [128, FF // 128, 128]), sb("v2", [128, D])
        b1c, one64 = sb("b1c", [128, FF // 128]), sb("one64", [128, 1])
        rw, rb = sb("rw", [128, C, E]), sb("rb", [T, E])
        rank8 = sb("rank8", [T, E])
        sele = sb("sele", [128, E, 128])
        ident = sb("ident", [128, 128])
        identb = sb("identb", [128, 128], BF16)
        mask16, mask32 = sb("mask16", [128, 8]), sb("mask32", [128, 4])
        negones = sb("negones", [T, 128], BF16)
        ones32 = sb("ones32", [128, 32])
        neghalf = sb("neghalf", [128, 4])
        alibi = sb("alibi", [T, 16, T], BF16)
        wstack = sb("wstack", [NSTACK + 3, NR], BF16)
        rowmask = sb("rowmask", [T, B * S], U8)
        colmask = sb("colmask", [128, 3, B], U8)
        experts = sb("experts", [128, WSLOTS, 2048])

        x = sb("x", [T, G, D])
        z = sb("z", [T, G, D])
        xT = sb("xT", [128, C, GT])
        qT = sb("qT", [128, C, GT])
        kT = sb("kT", [128, C, GT])
        kTb = sb("kTb", [128, C, GT], BF16)
        v16 = sb("v16", [T, G, 16, 32])
        qbd = sb("qbd", [128, 2, 16 * T])
        qbdb = sb("qbdb", [128, 2, 16 * T + HALO], BF16)
        shift = sb("shift", [T, 2, 16])
        dshift = sb("dshift", [T, 4, 4 * T], BF16)
        pT = sb("pT", [128, 3, 3, 4 * T])
        oT = sb("oT", [128, 4, T])
        rec = sb("rec", [T, 16])
        o = sb("o", [T, D])
        onT = sb("onT", [128, C, T])
        y = sb("y", [T, 2, D])
        bn6 = sb("bn6", [128, 3, 6])
        mv = sb("mv", [128, 4, 3, 2])
        vare = sb("vare", [128, 4, 3])
        rstd = sb("rstd", [128, 4, 3])
        UNION = 51200
        union = sb("union", [128, UNION // 4])

        def region(start, parts, shape, dt):
            size, n = (4 if dt == F32 else 2), 1
            for s in shape:
                n *= s
            assert start % 4 == 0 and start + n * size <= UNION
            v = union[0:parts, start // 4:(start + n * size) // 4]
            if dt != F32:
                v = v.bitcast(dt)
            if len(shape) > 1:
                names = "abcd"[:len(shape)]
                v = v.rearrange(f"p ({' '.join(names)}) -> p {' '.join(names)}",
                                **{k: s for k, s in zip(names, shape)})
            return v

        pos = region(0, T, [16 * G, T], F32)
        qstack = region(25600, NSTACK + 3, [16, GT], BF16)
        s0 = region(38400, T, [2, 16, T], F32)
        kxT = region(0, 128, [2, C, S], F32)
        kxTb = region(5776, 128, [2, C, S + 1], BF16)
        vx = region(8672, 128, [2, 3, 512], F32)
        cT = region(20960, CK, [2, 2, S], F32)
        cx = region(26736, 128, [2, 3, DC], F32)
        rowbias = region(31344, T, [2, S], F32)
        colbias = region(34232, 128, [2, 4], F32)
        hid = region(34304, 128, [8, GT], F32)
        ptok = region(0, 128, [GT], F32)
        qtok = region(1600, 128, [GT], F32)
        comb = region(0, T, [12, G, E], F32)
        ctop = region(1536, 128, [GT], F32)
        yT = region(3200, 128, [C, GT], F32)

        masked = sb("masked", [T, 2, S])
        pieces = pT[:, 0].rearrange("p a n -> p (a n)").bitcast(BF16).rearrange("p (s c t) -> p s c t", s=3, c=C)
        rest = pT[:, 1, 0:C, :]
        qp_dram = nc.dram_tensor("q_pieces", (3, D, GT), BF16).ap()

        banks = {r: [ctx.enter_context(nc.psum_tensor(f"{r}_{i}", [128, 512], F32)) for i in range(n)]
                 for r, n in DEPTH.items()}

        def bank(ring, n):
            return banks[ring][(n - 1) % DEPTH[ring]]

        w_const, w_self0, w_cross1 = sem("w_const"), sem("w_self0"), sem("w_cross1")
        w_ffn, w_self3, w_cross4, w_router = sem("w_ffn"), sem("w_self3"), sem("w_cross4"), sem("w_router")
        made = sem("made")
        group_sems = []

        def gsem(name):
            s = sem(name)
            group_sems.append(s)
            return s

        full = {r: gsem(f"{r}_full") for r in DEPTH}
        done = {r: gsem(f"{r}_done") for r in DEPTH}
        pv_done = gsem("pv_done")
        x_in, y_out = gsem("x_in"), gsem("y_out")
        cx_in = [gsem("cx_in0"), gsem("cx_in1")]
        cT_in = [gsem("cT_in0"), gsem("cT_in1")]
        pieces_out, qstack_in = gsem("pieces_out"), gsem("qstack_in")
        expert_in = [gsem(f"expert_in{i}") for i in range(WSLOTS)]
        expert_used = gsem("expert_used")
        pieces_made = gsem("pieces_made")
        kTb_made = gsem("kTb_made")
        qbdb_made = gsem("qbdb_made")
        qbd_made = gsem("qbd_made")
        dshift_made = gsem("dshift_made")
        var_made = gsem("var_made")
        rstd_made = gsem("rstd_made")
        ln_done = gsem("ln_done")
        z_made = gsem("z_made")
        cz_made = gsem("cz_made")
        bias_made = gsem("bias_made")
        gated = gsem("gated")
        logit_made, exp_made = gsem("logit_made"), gsem("exp_made")
        comb_made = gsem("comb_made")
        dve_step, pool_step = gsem("dve_step"), gsem("pool_step")

        LN = {"S0": 0, "C1": 4, "F2": 8, "S3": 12, "C4": 16, "M5": 20}
        asked = []
        for ph in ("S0",):
            asked += [(ph, b) for b in range(G)]
        asked += [("cx", 0)] + [("z", b) for b in range(G)] + [("cx", 1)]
        asked += [("cx", 2), ("cx", 3)] + [("C1", b) for b in range(G)]
        for ph in ("F2", "S3", "C4", "M5"):
            asked += [(ph, b) for b in range(G)]
        ASK = {k: i for i, k in enumerate(asked)}
        QBD = {"S0": 0, "C1": 4, "S3": 8, "C4": 12}
        QBDB = {"C1": 0, "S3": 4, "C4": 8}
        KTB = {"C1": 0, "S3": 4, "C4": 5}

        def hg_of(L, b, hg):
            return {"S0": 0, "C1": 16, "S3": 24, "C4": 40}[L.p] + b * L.hgs + hg

        def pa_max(L, b, i):
            if L.p == "S0":
                return nth("pa", "S0", 7 + 8 * b + 4 + i)
            return nth("pa", L.p, b * (4 if L.p == "S3" else L.heads) + i)

        def pb_exp(L, b, hg, jt):
            n = len(L.tiles)
            return nth("pb", L.p, (6 if L.p == "S0" else 0) + (b * L.hgs + hg) * n + jt)

        def kv_fill(L, b, ring, i):
            per = USES[ring][L.pre]
            if b == 0:
                return nth(ring, L.pre, i)
            return nth(ring, L.p, (2 if ring == "pk0" else 0) + (b - 1) * per + i)

        with nc.Block() as block:
            @block.sync
            def _(sync):
                for t, n in ((ident, "ident"), (mask16, "mask16"), (mask32, "mask32"), (one64, "one64"),
                             (neghalf, "neghalf"), (rank8, "rank8"), (alibi, "alibi")):
                    sync.dma_start(t[:], a[n]).then_inc(w_const, 16)
                sync.dma_start(union[0:NSTACK + 3, 0:NR], a["wr_stack"]).then_inc(w_const, 16)
                sync.dma_start(union[0:NSTACK + 3, 300:303], a["w_pick"]).then_inc(w_const, 16)
                sync.dma_start(wqkv[0][:], a["wqkv0"]).then_inc(w_self0, 16)
                sync.dma_start(bqk[0][:], a["bqk0"]).then_inc(w_self0, 16)
                sync.dma_start(bv[0][:], a["bv0"].partition_broadcast(T)).then_inc(w_self0, 16)

            @block.scalar
            def _(act):
                for t, n in ((wq[1], "wq1"), (wk[1], "wk1"), (wv[1], "wv1"), (wo[1], "wo1"),
                             (lat_gb, "lat_gb"), (in_gb, "in_gb")):
                    act.dma_start(t[:], a[n]).then_inc(w_cross1, 16)
                for t, n in ((u1, "u1"), (v1, "v1"), (u2, "u2"), (v2, "v2"), (b1c, "b1c")):
                    act.dma_start(t[:], a[n]).then_inc(w_ffn, 16)
                act.dma_start(wqkv[3][:], a["wqkv3"]).then_inc(w_self3, 16)
                act.dma_start(bqk[3][:], a["bqk3"]).then_inc(w_self3, 16)
                act.dma_start(bv[3][:], a["bv3"].partition_broadcast(T)).then_inc(w_self3, 16)
                act.dma_start(bo3[:], a["bo3"].partition_broadcast(T)).then_inc(w_self3, 16)
                act.dma_start(wo[3][:], a["wo3"]).then_inc(w_self3, 16)
                for t, n in ((wq[4], "wq4"), (wk[4], "wk4"), (wv[4], "wv4"), (wo[4], "wo4")):
                    act.dma_start(t[:], a[n]).then_inc(w_cross4, 16)
                act.dma_start(colmask[:, 0:2, :], a["maskT"][0:256, :].rearrange("(j p) b -> p j b", p=128)).then_inc(w_cross4, 16)
                act.dma_start(colmask[0:S - 256, 2, :], a["maskT"][256:S, :]).then_inc(w_cross4, 16)
                act.dma_start(rowmask[:], a["mask"].rearrange("b s -> (b s)").partition_broadcast(T)).then_inc(w_cross4, 16)
                act.dma_start(rw[:], a["rw"]).then_inc(w_router, 16)
                act.dma_start(sele[:], a["sele"]).then_inc(w_router, 16)
                act.dma_start(rb[:], a["rb"].partition_broadcast(T)).then_inc(w_router, 16)

            @block.vector
            def _(dve):
                nc.vector.memset(negones[:], -1.0).then_inc(made, 1)
                nc.vector.memset(ones32[:], 1.0).then_inc(made, 1)
                nc.vector.memset(v16[:], 1.0).then_inc(made, 1)
                nc.vector.memset(qbdb[:], 0.0).then_inc(made, 1)
                nc.vector.memset(mv[:], 1.0).then_inc(made, 1)
                dve.wait_ge(w_const, 144)
                nc.vector.tensor_copy(identb[:], ident[:]).then_inc(made, 1)
                R = NSTACK + 3
                w = union[0:R, 0:NR]
                pick = union[0:R, 300:303]
                hb = union[0:R, 400:400 + 130].bitcast(BF16)[:, 0:NR]
                mb = union[0:R, 600:600 + 130].bitcast(BF16)[:, 0:NR]
                lb = union[0:R, 800:800 + 130].bitcast(BF16)[:, 0:NR]
                r = union[0:R, 1000:1000 + NR]
                r2 = union[0:R, 1300:1300 + NR]
                nc.vector.tensor_copy(hb, w).then_inc(made, 1)
                dve.wait_ge(made, 7)
                nc.vector.tensor_tensor(r, w, hb, ALU.subtract).then_inc(made, 1)
                dve.wait_ge(made, 8)
                nc.vector.tensor_copy(mb, r).then_inc(made, 1)
                dve.wait_ge(made, 9)
                nc.vector.tensor_tensor(r2, r, mb, ALU.subtract).then_inc(made, 1)
                dve.wait_ge(made, 10)
                nc.vector.tensor_copy(lb, r2).then_inc(made, 1)
                dve.wait_ge(made, 11)
                nc.vector.tensor_scalar(r, hb, pick[:, 0:1], None, ALU.mult).then_inc(made, 1)
                dve.wait_ge(made, 12)
                nc.vector.scalar_tensor_tensor(out=r2, in0=mb, scalar=pick[:, 1:2], in1=r, op0=ALU.mult, op1=ALU.add).then_inc(made, 1)
                dve.wait_ge(made, 13)
                nc.vector.scalar_tensor_tensor(out=wstack[:], in0=lb, scalar=pick[:, 2:3], in1=r2, op0=ALU.mult, op1=ALU.add).then_inc(made, 1)
                dve.wait_ge(made, 14)

        with nc.Fori(0, B // G, 1) as g:
            with nc.Block() as block:

                @block.sync
                def _(sync):
                    sync.dma_start(x[:], a["x"][bass.ds(g * G, G)].rearrange("b t d -> t b d")).then_inc(x_in, 16)
                    for e in range(WSLOTS):
                        sync.dma_start(experts[:, e, :], a["experts"][e]).then_inc(expert_in[e], 16)
                    sync.wait_ge(pieces_made, 1)
                    sync.dma_start(qp_dram.rearrange("s (c p) t -> p s c t", p=128), pieces[:]).then_inc(pieces_out, 16)
                    sync.wait_ge(pieces_out, 16)
                    for s, piece in enumerate(PIECES):
                        sync.dma_start(qstack[16 * s:16 * s + 16], qp_dram[piece].rearrange("(h d) t -> d h t", d=16)).then_inc(qstack_in, 16)
                    for b in range(G):
                        if b < 2:
                            sync.wait_ge(full["pa"], nth("pa", "S0", 6))
                        else:
                            sync.wait_ge(full["pk1"], kv_fill(CROSS1, b - 2, "pk1", 0))
                            sync.wait_ge(full["pk0"], kv_fill(CROSS1, b - 2, "pk0", 0))
                        src = a["ctx"][bass.ds(g * G + b, 1)].rearrange("a s d -> (a s) d")
                        sync.dma_start(cx[:, b % 2, 0:2, :], src[0:256, :].rearrange("(j p) d -> p j d", p=128)).then_inc(cx_in[b % 2], 16)
                        sync.dma_start(cx[0:S - 256, b % 2, 2, :], src[256:S, :]).then_inc(cx_in[b % 2], 16)
                    for b in range(G):
                        L, u = (CROSS1, b + 2) if b < 2 else (CROSS4, b - 2)
                        sync.wait_ge(full["pk1"], kv_fill(L, u, "pk1", USES["pk1"][L.pre] - 1))
                        src = a["ctxT"][bass.ds(g * G + b, 1)].rearrange("a d s -> (a d) s")
                        sync.dma_start(cT[:, b % 2, :, :], src.rearrange("(k p) s -> p k s", p=CK)).then_inc(cT_in[b % 2], 16)
                    for e in range(WSLOTS, NE):
                        sync.wait_ge(expert_used, e - WSLOTS + 1)
                        sync.dma_start(experts[:, e % WSLOTS, :], a["experts"][e]).then_inc(expert_in[e % WSLOTS], 16)
                    for b in range(G):
                        sync.wait_ge(ln_done, LN["M5"] + b + 1)
                        sync.dma_start(out[bass.ds(g * G + b, 1)].rearrange("a t d -> (a t) d"), x[:, b, :]).then_inc(y_out, 16)
                    sync.wait_ge(y_out, 16 * G)

                @block.tensor
                def _(pe):
                    mm = nc.tensor.matmul

                    def claim(ring, n):
                        if n > DEPTH[ring]:
                            pe.wait_ge(done[ring], n - DEPTH[ring])
                        return bank(ring, n)

                    def transpose_x(ph, src, ready, counts):
                        for c, ring in enumerate(("pk0", "pk1")):
                            n = nth(ring, ph, 0)
                            p = claim(ring, n)
                            for b in range(G):
                                if c == 0:
                                    pe.wait_ge(ready, counts[b])
                                last = nc.tensor.transpose(p[:, b * T:(b + 1) * T], src[:, b, c * 128:(c + 1) * 128], ident[0:T, 0:T])
                            last.then_inc(full[ring], 1)

                    def wait_xT(ph):
                        pe.wait_ge(done["pk0"], nth("pk0", ph, 0))
                        pe.wait_ge(done["pk1"], nth("pk1", ph, 0))

                    def project_T(ring, n, w, col):
                        p = claim(ring, n)
                        for k in range(C):
                            last = mm(p[:, 0:GT], w[:, k, col:col + 128], xT[:, k, :], start=(k == 0), stop=(k == C - 1))
                        last.then_inc(full[ring], 1)

                    def self_project(li, L):
                        for i in range(4):
                            project_T("pk0", nth("pk0", L.p, i), wqkv[li], 128 * i)
                            n = nth("pk1", L.p, i)
                            p = claim("pk1", n)
                            for k in range(C):
                                last = mm(p[0:T, 0:D], xT[:, k, i * T:(i + 1) * T], wqkv[li][:, k, 2 * D:3 * D], start=(k == 0), stop=(k == C - 1))
                            last.then_inc(full["pk1"], 1)

                    def positions():
                        pe.wait_ge(qstack_in, 16 * len(PIECES))
                        pe.wait_ge(pool_step, 1)
                        for k in range(13):
                            ring = "pa" if k % 2 == 0 else "pb"
                            n = nth(ring, "S0", k // 2)
                            p = claim(ring, n)
                            for i in range(8 * k, min(8 * k + 8, T)):
                                u = i - 8 * k
                                rhs = qstack.rearrange("r h (b t) -> r h b t", b=G)[:, :, :, i]
                                last = mm(p[:, 64 * u:64 * u + 64], wstack[:, REL0 - i:REL0 - i + 128], rhs, start=True, stop=True)
                            last.then_inc(full[ring], 1)

                    def context(L, li, b):
                        s = b % 2
                        first = 0
                        if L is CROSS1:
                            pe.wait_ge(cz_made, b + 1)
                            for c, ring in enumerate(("pk0", "pk1")):
                                n = kv_fill(L, b, ring, 0)
                                p = claim(ring, n)
                                for j, (j0, J) in enumerate(JT):
                                    last = nc.tensor.transpose(p[0:CK, j0:j0 + J], cx[0:J, s, j, c * CK:(c + 1) * CK], ident[0:J, 0:J])
                                last.then_inc(full[ring], 1)
                            pe.wait_ge(done["pk0"], kv_fill(L, b, "pk0", 0))
                            pe.wait_ge(done["pk1"], kv_fill(L, b, "pk1", 0))
                            first = 1
                        else:
                            pe.wait_ge(cT_in[s], 16 * (b // 2 + 1))
                        for i in range(3):
                            if i < C:
                                n = kv_fill(L, b, "pk0", first + i)
                                p = claim("pk0", n)
                                for k in range(2):
                                    last = mm(p[:, 0:S], wk[li][:, k, i * 128:(i + 1) * 128], cT[:, s, k, :], start=(k == 0), stop=(k == 1))
                                last.then_inc(full["pk0"], 1)
                            n = kv_fill(L, b, "pk1", first + i)
                            p = claim("pk1", n)
                            j0, J = JT[i]
                            for k in range(2):
                                last = mm(p[0:J, 0:D], cT[:, s, k, j0:j0 + J], wv[li][:, k, :], start=(k == 0), stop=(k == 1))
                            last.then_inc(full["pk1"], 1)

                    def max_scores(L, b):
                        s = b % 2
                        if L.relative:
                            pe.wait_ge(qbd_made, QBD[L.p] + b + 1)
                            pe.wait_ge(done["pk0"], nth("pk0", "S0", 3))
                            for hg in range(4):
                                n = nth("pa", "S0", 7 + 8 * b + hg)
                                p = claim("pa", n)
                                mm(p[0:T, 0:4 * T], kT[:, hg // 2, b * T:(b + 1) * T], qbd[:, s, hg * 4 * T:(hg + 1) * 4 * T],
                                   start=True, stop=True).then_inc(full["pa"], 1)
                            for hg in range(4):
                                pe.wait_ge(done["pa"], nth("pa", "S0", 7 + 8 * b + hg))
                                n = pa_max(L, b, hg)
                                p = claim("pa", n)
                                for h in range(4):
                                    last = nc.tensor.transpose(p[0:T, h * T:(h + 1) * T], s0[:, s, 4 * hg + h, :], ident[0:T, 0:T])
                                last.then_inc(full["pa"], 1)
                            return
                        pe.wait_ge(qbdb_made, QBDB[L.p] + b + 1)
                        pe.wait_ge(kTb_made, KTB[L.p] + (1 if isinstance(L, Self) else b + 1))
                        if isinstance(L, Self):
                            for hg in range(4):
                                p = claim("pa", pa_max(L, b, hg))
                                mm(p[:, 0:4 * T], identb[0:T, :], alibi[:, 4 * hg:4 * hg + 4, :].rearrange("p h t -> p (h t)"), start=True, stop=True)
                                for h in range(4 * hg, 4 * hg + 4):
                                    u = h - 4 * hg
                                    last = mm(p[:, u * T:(u + 1) * T], qbdb[:, s, h * T:h * T + 128], kTb[:, h // 8, b * T:(b + 1) * T],
                                              start=False, stop=True, skip_group_check=True)
                                last.then_inc(full["pa"], 1)
                        else:
                            for h in range(L.heads):
                                p = claim("pa", pa_max(L, b, h))
                                mm(p[:, 0:S], qbdb[:, s, h * T:h * T + 128], kxTb[:, s, h // (L.heads // C), 0:S],
                                   start=True, stop=True).then_inc(full["pa"], 1)

                    def exp_scores(L, b, hg):
                        s, d = b % 2, hg_of(L, b, hg)
                        if not L.relative:
                            pe.wait_ge(qbd_made, QBD[L.p] + b + 1)
                        for j, (j0, J) in enumerate(L.tiles):
                            n = pb_exp(L, b, hg, j)
                            p = claim("pb", n)[0:J, 0:4 * T]
                            if L.relative:
                                mm(p, ident[0:T, 0:T], s0[:, s, 4 * hg:4 * hg + 4, :].rearrange("p h t -> p (h t)"), start=True, stop=False)
                            else:
                                chunk = 4 * hg // (L.heads // C)
                                keys = kT[:, chunk, b * T:(b + 1) * T] if isinstance(L, Self) else kxT[:, s, chunk, j0:j0 + J]
                                mm(p, keys, qbd[:, s, hg * 4 * T:(hg + 1) * 4 * T], start=True, stop=False)
                                if isinstance(L, Self):
                                    mm(p, identb[0:T, 0:T], alibi[:, 4 * hg:4 * hg + 4, :].rearrange("p h t -> p (h t)"), start=False, stop=False)
                            if j == 0:
                                pe.wait_ge(dshift_made, d + 1)
                            mm(p, negones[:, 0:J], dshift[:, d % 4, :], start=False, stop=True).then_inc(full["pb"], 1)

                    def times_v(L, b, hg):
                        d = hg_of(L, b, hg)
                        slot, p = d % 3, bank("po", 1)
                        if hg == 0:
                            n = nth("po", L.p, b)
                            if n > 1:
                                pe.wait_ge(done["po"], n - 1)
                            if isinstance(L, Self):
                                pe.wait_ge(done["pk1"], nth("pk1", L.p, G - 1))
                            else:
                                pe.wait_ge(done["pk1"], kv_fill(L, b, "pk1", USES["pk1"][L.pre] - 1))
                        last_tile = len(L.tiles) - 1
                        for j, (j0, J) in enumerate(L.tiles):
                            pe.wait_ge(done["pb"], pb_exp(L, b, hg, j))
                            for u in range(4):
                                h = 4 * hg + u
                                if isinstance(L, Self):
                                    v = v16[:, b, h, :]
                                else:
                                    v = vx[0:J, b % 2, j, 32 * h:32 * h + 32]
                                last = mm(p[32 * u:32 * u + 32, hg * T:(hg + 1) * T], v, pT[0:J, slot, j, u * T:(u + 1) * T],
                                          start=(j == 0), stop=(j == last_tile), skip_group_check=True)
                        if L is CROSS1:
                            for j, (j0, J) in enumerate(L.tiles):
                                for u in range(4):
                                    last = mm(p[32 * u:32 * u + 32, (2 + hg) * T:(3 + hg) * T], ones32[0:J, :], pT[0:J, slot, j, u * T:(u + 1) * T],
                                              start=(j == 0), stop=(j == last_tile), skip_group_check=True)
                        last.then_inc(pv_done, 1)

                    def epilogue(L, li, b, part):
                        per = 1 if L.relative else 3
                        if part == 0:
                            n = nth("ps", L.p, per * b)
                            p = claim("ps", n)
                            pe.wait_ge(done["po"], nth("po", L.p, b))
                            for i in range(4):
                                last = nc.tensor.transpose(p[0:T, i * 128:(i + 1) * 128], oT[:, i, :], ident[:, :])
                            last.then_inc(full["ps"], 1)
                        elif L.relative:
                            return
                        elif part == 1:
                            n = nth("ps", L.p, per * b + 1)
                            p = claim("ps", n)
                            for c in range(C):
                                last = nc.tensor.transpose(p[:, c * T:(c + 1) * T], o[:, c * 128:(c + 1) * 128], ident[0:T, 0:T])
                            last.then_inc(full["ps"], 1)
                        else:
                            n = nth("ps", L.p, per * b + 2)
                            p = claim("ps", n)
                            for c in range(C):
                                last = mm(p[0:T, 0:D], onT[:, c, :], wo[li][:, c, :], start=(c == 0), stop=(c == C - 1))
                            last.then_inc(full["ps"], 1)

                    def attention(L, li):
                        max_scores(L, 0)
                        for b in range(G):
                            if b + 1 < G:
                                if isinstance(L, Cross):
                                    context(L, li, b + 1)
                                max_scores(L, b + 1)
                            exp_scores(L, b, 0)
                            for hg in range(L.hgs):
                                if hg + 1 < L.hgs:
                                    exp_scores(L, b, hg + 1)
                                if b > 0 and hg < 3:
                                    epilogue(L, li, b - 1, hg)
                                times_v(L, b, hg)
                            if b > 0 and L.hgs < 3:
                                epilogue(L, li, b - 1, 2)
                        for part in range(3):
                            epilogue(L, li, G - 1, part)

                    pe.wait_ge(w_const, 144)
                    pe.wait_ge(w_self0, 48)
                    pe.wait_ge(made, 14)
                    pe.wait_ge(x_in, 16)
                    transpose_x("X0", x, x_in, [16] * G)
                    wait_xT("X0")
                    self_project(0, SELF0)
                    positions()
                    attention(SELF0, 0)
                    pe.wait_ge(w_cross1, 96)
                    context(CROSS1, 1, 0)
                    transpose_x("X1", z, z_made, [b + 1 for b in range(G)])
                    wait_xT("X1")
                    for i in range(C):
                        project_T("pk0", nth("pk0", "C1", i), wq[1], 128 * i)
                    attention(CROSS1, 1)
                    pe.wait_ge(w_ffn, 80)
                    transpose_x("X2", x, ln_done, [LN["C1"] + b + 1 for b in range(G)])
                    wait_xT("X2")
                    project_T("pk0", nth("pk0", "F2", 0), u1, 0)
                    pe.wait_ge(done["pk0"], nth("pk0", "F2", 0))
                    NF = FF // 128
                    n_po = nth("po", "F2", 0)
                    for i in range(NF + LAG):
                        if i < NF:
                            n = nth("pb", "F2", i)
                            mm(claim("pb", n)[:, 0:GT], v1[:, i * 128:(i + 1) * 128], ptok, start=True, stop=True).then_inc(full["pb"], 1)
                        if i >= LAG:
                            f = i - LAG
                            if f == 0:
                                claim("po", n_po)
                            pe.wait_ge(done["pb"], nth("pb", "F2", f))
                            last = mm(bank("po", 1)[:, 0:GT], u2[:, f, :], hid[:, f, :], start=(f == 0), stop=(f == NF - 1))
                    last.then_inc(full["po"], 1)
                    pe.wait_ge(done["po"], n_po)
                    for b in range(G):
                        p = claim("ps", nth("ps", "F2", b))
                        mm(p[0:T, 0:D], qtok[:, b * T:(b + 1) * T], v2[:], start=True, stop=True).then_inc(full["ps"], 1)
                    pe.wait_ge(w_self3, 80)
                    transpose_x("X3", x, ln_done, [LN["F2"] + b + 1 for b in range(G)])
                    wait_xT("X3")
                    self_project(3, SELF3)
                    attention(SELF3, 3)
                    pe.wait_ge(w_cross4, 112)
                    context(CROSS4, 4, 0)
                    transpose_x("X4", x, ln_done, [LN["S3"] + b + 1 for b in range(G)])
                    wait_xT("X4")
                    for i in range(C):
                        project_T("pk0", nth("pk0", "C4", i), wq[4], 128 * i)
                    attention(CROSS4, 4)
                    pe.wait_ge(w_router, 48)
                    transpose_x("X5", x, ln_done, [LN["C4"] + b + 1 for b in range(G)])
                    wait_xT("X5")
                    n = nth("ps", "M5", 0)
                    p = claim("ps", n)
                    for b in range(G):
                        for k in range(C):
                            last = mm(p[0:T, b * E:(b + 1) * E], xT[:, k, b * T:(b + 1) * T], rw[:, k, :], start=(k == 0), stop=(k == C - 1))
                    last.then_inc(full["ps"], 1)
                    yb = [claim("pa", nth("pa", "M5", i)) for i in range(C)]
                    chunks = NE * FC
                    for i in range(chunks + LAG):
                        if i < chunks:
                            e, f = divmod(i, FC)
                            if f == 0:
                                pe.wait_ge(expert_in[e % WSLOTS], 16 * (e // WSLOTS + 1))
                            w = experts[:, e % WSLOTS, 0:C * F].rearrange("p (c f) -> p c f", c=C)
                            project_T("pb", nth("pb", "M5", i), w, f * 128)
                        if i >= LAG:
                            e, f = divmod(i - LAG, FC)
                            u = i - LAG
                            if e == 0:
                                pe.wait_ge(done["pb"], nth("pb", "M5", u))
                            else:
                                pe.wait_ge(gated, u - FC + 1)
                            w = experts[:, e % WSLOTS, C * F:].rearrange("p (f d) -> p f d", f=FC)
                            for c in range(C):
                                last = mm(yb[c][:, 0:GT], w[:, f, c * 128:(c + 1) * 128], hid[:, u % 8, :], start=(u == 0), stop=(u == chunks - 1))
                                if u == chunks - 1:
                                    last.then_inc(full["pa"], 1)
                            if f == FC - 1 and e + WSLOTS < NE:
                                last.then_inc(expert_used, 1)
                        if i == FC:
                            pe.wait_ge(comb_made, 1)
                            p = claim("pk0", nth("pk0", "M5", 0))
                            for b in range(G):
                                last = nc.tensor.transpose(p[0:E, b * T:(b + 1) * T], comb[:, 11, b, :], ident[0:T, 0:T])
                            last.then_inc(full["pk0"], 1)
                            pe.wait_ge(done["pk0"], nth("pk0", "M5", 0))
                        if i % FC == 0 and 0 < i < chunks:
                            e = i // FC - 1
                            if e > 0:
                                pe.wait_ge(gated, FC * e)
                            else:
                                pe.wait_ge(done["pk1"], nth("pk1", "X5", 0))
                            mm(bank("pk1", 1)[:, 0:GT], sele[:, e, :], ctop, start=True, stop=True).then_inc(full["pk1"], 1)
                    for i in range(C):
                        pe.wait_ge(done["pa"], nth("pa", "M5", i))
                    for b in range(G):
                        p = claim("ps", nth("ps", "M5", 1 + b))
                        for c in range(C):
                            last = nc.tensor.transpose(p[0:T, c * 128:(c + 1) * 128], yT[:, c, b * T:(b + 1) * T], ident[:, :])
                        last.then_inc(full["ps"], 1)

                @block.scalar
                def _(act):
                    fn = nc.scalar.activation

                    def copy_xT(ph):
                        n = nth("pk0", ph, 0)
                        act.wait_ge(full["pk0"], n)
                        fn(xT[:, 0, :], bank("pk0", n)[:, 0:GT], ACT.Copy).then_inc(done["pk0"], 1)

                    def project_q(L):
                        for c in range(C):
                            n = nth("pk0", L.p, c)
                            act.wait_ge(full["pk0"], n)
                            fn(qT[:, c, :], bank("pk0", n)[:, 0:GT], ACT.Copy).then_inc(done["pk0"], 1)

                    def self_project(li, L):
                        for i in range(4):
                            n = nth("pk0", L.p, i)
                            act.wait_ge(full["pk0"], n)
                            dst = (qT if i < C else kT)[:, i % C, :]
                            fn(dst, bank("pk0", n)[:, 0:GT], ACT.Identity, bias=bqk[li][:, i:i + 1]).then_inc(done["pk0"], 1)

                    def context(L, b):
                        s, first = b % 2, 0
                        if L is CROSS1:
                            n = kv_fill(L, b, "pk0", 0)
                            act.wait_ge(full["pk0"], n)
                            fn(cT[:, s, 0, :], bank("pk0", n)[0:CK, 0:S], ACT.Identity, bias=in_gb[:, 2:3], scale=in_gb[:, 0:1]).then_inc(done["pk0"], 1)
                            first = 1
                        for c in range(C):
                            n = kv_fill(L, b, "pk0", first + c)
                            act.wait_ge(full["pk0"], n)
                            fn(kxT[:, s, c, :], bank("pk0", n)[:, 0:S], ACT.Copy).then_inc(done["pk0"], 1)

                    def attention(L):
                        for b in range(G):
                            if isinstance(L, Cross) and b + 1 < G:
                                context(L, b + 1)
                            for hg in range(L.hgs):
                                d = hg_of(L, b, hg)
                                if d >= 3:
                                    act.wait_ge(pv_done, d - 2)
                                for j, (j0, J) in enumerate(L.tiles):
                                    n = pb_exp(L, b, hg, j)
                                    act.wait_ge(full["pb"], n)
                                    src, dst = bank("pb", n)[0:J, 0:4 * T], pT[0:J, d % 3, j, :]
                                    scale = 1.0 if L.relative else L.scale
                                    if L is CROSS4:
                                        if hg == 0 and j == 0:
                                            act.wait_ge(bias_made, 3 * b + 3)
                                        fn(dst, src, ACT.Exp, bias=colbias[0:J, b % 2, j:j + 1], scale=scale).then_inc(done["pb"], 1)
                                    else:
                                        fn(dst, src, ACT.Exp, scale=scale).then_inc(done["pb"], 1)
                            act.wait_ge(pv_done, hg_of(L, b, L.hgs - 1) + 1)
                            fn(oT[:].rearrange("p h t -> p (h t)"), bank("po", 1)[:, 0:4 * T], ACT.Copy).then_inc(done["po"], 1)

                    copy_xT("X0")
                    act.wait_ge(w_self0, 48)
                    self_project(0, SELF0)
                    for k in range(1, 13, 2):
                        n = nth("pb", "S0", k // 2)
                        act.wait_ge(full["pb"], n)
                        fn(pos[:, :, 8 * k:8 * k + 8], bank("pb", n)[0:T, :].rearrange("p (i m) -> p m i", i=8), ACT.Copy).then_inc(done["pb"], 1)
                    attention(SELF0)
                    act.wait_ge(w_cross1, 96)
                    context(CROSS1, 0)
                    n = nth("pk0", "X1", 0)
                    act.wait_ge(full["pk0"], n)
                    fn(xT[:, 0, :], bank("pk0", n)[:, 0:GT], ACT.Identity, bias=lat_gb[:, 2:3], scale=lat_gb[:, 0:1]).then_inc(done["pk0"], 1)
                    project_q(CROSS1)
                    attention(CROSS1)
                    copy_xT("X2")
                    act.wait_ge(w_ffn, 80)
                    n = nth("pk0", "F2", 0)
                    act.wait_ge(full["pk0"], n)
                    fn(ptok, bank("pk0", n)[:, 0:GT], ACT.Copy).then_inc(done["pk0"], 1)
                    for i in range(FF // 128):
                        n = nth("pb", "F2", i)
                        act.wait_ge(full["pb"], n)
                        fn(hid[:, i, :], bank("pb", n)[:, 0:GT], ACT.Gelu_apprx_tanh, bias=b1c[:, i:i + 1]).then_inc(done["pb"], 1)
                    act.wait_ge(full["po"], 1)
                    fn(qtok, bank("po", 1)[:, 0:GT], ACT.Identity, bias=one64[:]).then_inc(done["po"], 1)
                    copy_xT("X3")
                    act.wait_ge(w_self3, 80)
                    self_project(3, SELF3)
                    attention(SELF3)
                    context(CROSS4, 0)
                    copy_xT("X4")
                    project_q(CROSS4)
                    attention(CROSS4)
                    copy_xT("X5")
                    act.wait_ge(logit_made, 1)
                    fn(comb[:, 2, :, :].rearrange("p b e -> p (b e)"), comb[:, 1, :, :].rearrange("p b e -> p (b e)"), ACT.Exp).then_inc(exp_made, 1)
                    for i in range(NE * FC):
                        if i == FC + 1:
                            n = nth("pk0", "M5", 0)
                            act.wait_ge(full["pk0"], n)
                            fn(ctop[0:E, :], bank("pk0", n)[0:E, 0:GT], ACT.Copy).then_inc(done["pk0"], 1)
                        n = nth("pb", "M5", i)
                        act.wait_ge(full["pb"], n)
                        fn(hid[:, i % 8, :], bank("pb", n)[:, 0:GT], ACT.Silu).then_inc(done["pb"], 1)

                @block.gpsimd
                def _(pool):
                    steps = [0]

                    def block_diagonal(L, b):
                        per = L.heads // C
                        m = mask16 if per == 8 else mask32
                        for c in range(C):
                            dst = qbd[:, b % 2, c * per * T:(c + 1) * per * T].rearrange("p (h t) -> p h t", h=per)
                            q = qT[:, c, b * T:(b + 1) * T].unsqueeze(1).broadcast_to([128, per, T])
                            ins = nc.gpsimd.tensor_tensor(dst, q, m[:].unsqueeze(2).broadcast_to([128, per, T]), ALU.mult)
                        ins.then_inc(qbd_made, 1)

                    def diagonal_shifts(L, b):
                        for hg in range(L.hgs):
                            d = hg_of(L, b, hg)
                            if d >= 4:
                                for_L, bb, hh = owner(d - 4)
                                pool.wait_ge(full["pb"], pb_exp(for_L, bb, hh, len(for_L.tiles) - 1))
                            pool.wait_ge(done["pa"], pa_max(L, b, 4 * hg + 3 if isinstance(L, Cross) else hg))
                            dst = dshift[:, d % 4, :].rearrange("p (h t) -> p h t", h=4)
                            i3 = ident[0:T, 0:T].unsqueeze(1).broadcast_to([T, 4, T])
                            m = shift[:, b % 2, 4 * hg:4 * hg + 4].unsqueeze(2).broadcast_to([T, 4, T])
                            nc.gpsimd.tensor_tensor(dst, i3, m, ALU.mult).then_inc(dshift_made, 1)

                    def owner(d):
                        for L in (SELF0, CROSS1, SELF3, CROSS4):
                            d0 = hg_of(L, 0, 0)
                            if d0 <= d < d0 + G * L.hgs:
                                return L, (d - d0) // L.hgs, (d - d0) % L.hgs

                    def inverse_std(what, b):
                        r = ASK[(what, b)]
                        P, n = (128, 3) if what == "cx" else (T, 1)
                        pool.wait_ge(var_made, r + 1)
                        nc.gpsimd.tensor_scalar(vare[0:P, r % 4, 0:n], mv[0:P, r % 4, 0:n, 1], EPS, None, ALU.add).then_inc(pool_step, 1)
                        steps[0] += 1
                        pool.wait_ge(pool_step, steps[0])
                        nc.gpsimd.tensor_tensor(rstd[0:P, r % 4, 0:n], vare[0:P, r % 4, 0:n], neghalf[0:P, 0:n], ALU.pow).then_inc(rstd_made, 1)

                    def attention(L):
                        ph = L.p
                        pool.wait_ge(done["pk0"], nth("pk0", ph, C - 1))
                        block_diagonal(L, 0)
                        if L.relative:
                            block_diagonal(L, 1)
                        diagonal_shifts(L, 0)
                        for b in range(G):
                            if L.relative:
                                if b + 2 < G:
                                    pool.wait_ge(full["pa"], nth("pa", "S0", 7 + 8 * b + 3))
                                    block_diagonal(L, b + 2)
                            elif b + 1 < G:
                                if b > 0:
                                    pool.wait_ge(full["pb"], pb_exp(L, b - 1, L.hgs - 1, len(L.tiles) - 1))
                                block_diagonal(L, b + 1)
                            if b + 1 < G:
                                diagonal_shifts(L, b + 1)
                            if L is CROSS1 and b + 2 < G:
                                inverse_std("cx", b + 2)
                            if b > 0:
                                inverse_std(ph, b - 1)
                        inverse_std(ph, G - 1)

                    pool.memset(qstack[NSTACK:NSTACK + 3], 1.0).then_inc(pool_step, 1)
                    steps[0] += 1
                    pool.wait_ge(pool_step, 1)
                    pool.wait_ge(w_const, 144)
                    attention(SELF0)
                    inverse_std("cx", 0)
                    for b in range(G):
                        inverse_std("z", b)
                    inverse_std("cx", 1)
                    attention(CROSS1)
                    for b in range(G):
                        inverse_std("F2", b)
                    attention(SELF3)
                    attention(CROSS4)
                    for b in range(G):
                        inverse_std("M5", b)

                @block.vector
                def _(dve):
                    v = nc.vector
                    steps = [0]

                    def then(ins):
                        ins.then_inc(dve_step, 1)
                        steps[0] += 1
                        dve.wait_ge(dve_step, steps[0])

                    def copy_xT(ph):
                        n = nth("pk1", ph, 0)
                        dve.wait_ge(full["pk1"], n)
                        v.tensor_copy(xT[:, 1, :], bank("pk1", n)[:, 0:GT]).then_inc(done["pk1"], 1)

                    def moments(src, what, b):
                        r = ASK[(what, b)]
                        then(v.bn_stats(bn6[0:T, 0, :], src))
                        v.bn_aggr(mv[0:T, r % 4, 0, :], bn6[0:T, 0, :]).then_inc(var_made, 1)

                    def normalised(dst, src, what, b, signal):
                        r = ASK[(what, b)]
                        dve.wait_ge(rstd_made, r + 1)
                        v.tensor_scalar(dst, src, mv[0:T, r % 4, 0, 0:1], rstd[0:T, r % 4, 0:1], ALU.subtract, ALU.mult).then_inc(signal, 1)

                    def add_x(src, b, ring_n=None):
                        ins = v.tensor_tensor(y[:, b % 2, :], src, x[:, b, :], ALU.add)
                        if ring_n is None:
                            then(ins)
                        else:
                            ins.then_inc(done["ps"], 1)
                            dve.wait_ge(done["ps"], ring_n)

                    def self_values(li, L):
                        for b in range(G):
                            n = nth("pk1", L.p, b)
                            dve.wait_ge(full["pk1"], n)
                            v.tensor_tensor(v16[:, b, :, 0:16], bank("pk1", n)[0:T, 0:D].rearrange("p (h d) -> p h d", h=16),
                                            bv[li][:].rearrange("p (h d) -> p h d", h=16), ALU.add).then_inc(done["pk1"], 1)

                    def context_stats(b):
                        s, r = b % 2, ASK[("cx", b)]
                        dve.wait_ge(cx_in[s], 32 * (b // 2 + 1))
                        for j, (j0, J) in enumerate(JT):
                            then(v.bn_stats(bn6[0:J, j, :], cx[0:J, s, j, :]))
                        for j, (j0, J) in enumerate(JT):
                            ins = v.bn_aggr(mv[0:J, r % 4, j, :], bn6[0:J, j, :])
                            if j < 2:
                                then(ins)
                        ins.then_inc(var_made, 1)

                    def context_normalised(b):
                        s, r = b % 2, ASK[("cx", b)]
                        dve.wait_ge(rstd_made, r + 1)
                        for j, (j0, J) in enumerate(JT):
                            ins = v.tensor_scalar(cx[0:J, s, j, :], cx[0:J, s, j, :], mv[0:J, r % 4, j, 0:1], rstd[0:J, r % 4, j:j + 1], ALU.subtract, ALU.mult)
                            if j < 2:
                                then(ins)
                        ins.then_inc(cz_made, 1)

                    def context(L, b):
                        s, first = b % 2, 0
                        if L is CROSS1:
                            n = kv_fill(L, b, "pk1", 0)
                            dve.wait_ge(full["pk1"], n)
                            v.tensor_scalar(cT[:, s, 1, :], bank("pk1", n)[0:CK, 0:S], in_gb[:, 1:2], in_gb[:, 3:4], ALU.mult, ALU.add).then_inc(done["pk1"], 1)
                            first = 1
                        for j, (j0, J) in enumerate(JT):
                            n = kv_fill(L, b, "pk1", first + j)
                            dve.wait_ge(full["pk1"], n)
                            src = bank("pk1", n)[0:J, 0:D]
                            if L is CROSS1:
                                ins = v.tensor_copy(vx[0:J, s, j, 0:D], src)
                            else:
                                ins = v.tensor_copy(vx[0:J, s, j, :].rearrange("p (h d) -> p h d", h=16)[:, :, 0:16], src.rearrange("p (h d) -> p h d", h=16))
                            ins.then_inc(done["pk1"], 1)
                        dve.wait_ge(done["pk0"], kv_fill(L, b, "pk0", USES["pk0"][L.pre] - 1))
                        v.tensor_copy(kxTb[:, s, :, 0:S], kxT[:, s, :, :]).then_inc(kTb_made, 1)

                    def mask_bias(b, batch):
                        row = rowmask[:, bass.ds(batch * S, S)]
                        v.tensor_scalar(rowbias[:, b % 2, :], row, 1.0, BIG, ALU.subtract, ALU.mult).then_inc(bias_made, 1)
                        for P, j0, j1 in ((128, 0, 2), (S - 256, 2, 3)):
                            col = colmask[0:P, j0:j1, bass.ds(batch, 1)].rearrange("p j a -> p (j a)")
                            v.tensor_scalar(colbias[0:P, b % 2, j0:j1], col, 1.0, BIG * CROSS4.scale, ALU.subtract, ALU.mult).then_inc(bias_made, 1)

                    def q_bf16(L, b):
                        per = L.heads // C
                        m = mask16 if per == 8 else mask32
                        if b == 0:
                            dve.wait_ge(done["pk0"], nth("pk0", L.p, C - 1))
                        for c in range(C):
                            dst = qbdb[:, b % 2, c * per * T:(c + 1) * per * T].rearrange("p (h t) -> p h t", h=per)
                            q = qT[:, c, b * T:(b + 1) * T].unsqueeze(1).broadcast_to([128, per, T])
                            ins = v.tensor_tensor(dst, q, m[:].unsqueeze(2).broadcast_to([128, per, T]), ALU.mult)
                        ins.then_inc(qbdb_made, 1)

                    def maxima(L, b):
                        s = b % 2
                        if L.relative:
                            for hg in range(4):
                                n = nth("pa", "S0", 7 + 8 * b + hg)
                                dve.wait_ge(full["pa"], n)
                                v.scalar_tensor_tensor(
                                    out=s0[:, s, 4 * hg:4 * hg + 4, :], in0=bank("pa", n)[0:T, 0:4 * T].rearrange("p (h t) -> p h t", h=4), scalar=L.scale,
                                    in1=pos.rearrange("p (h b) t -> p h b t", b=G)[:, 4 * hg:4 * hg + 4, b, :],
                                    op0=ALU.mult, op1=ALU.add).then_inc(done["pa"], 1)
                        for hg in range(L.hgs):
                            d = hg_of(L, b, hg)
                            if hg == 0 and b > 1:
                                dve.wait_ge(dshift_made, hg_of(L, b - 2, L.hgs - 1) + 1)
                            if isinstance(L, Self):
                                n = pa_max(L, b, hg)
                                dve.wait_ge(full["pa"], n)
                                v.tensor_reduce(shift[:, s, 4 * hg:4 * hg + 4], bank("pa", n)[0:T, 0:4 * T].rearrange("p (h t) -> p h t", h=4), AX, ALU.max).then_inc(done["pa"], 1)
                                continue
                            for h in range(4 * hg, 4 * hg + 4):
                                n = pa_max(L, b, h)
                                dve.wait_ge(full["pa"], n)
                                src, dst = bank("pa", n)[0:T, 0:S], shift[:, s, h:h + 1]
                                if L.masked:
                                    if h == 0:
                                        dve.wait_ge(bias_made, 3 * b + 3)
                                    v.tensor_tensor_reduce(masked[:, h % 2, :], src, rowbias[:, s, :], 1.0, -3.4e38, ALU.add, ALU.max, dst).then_inc(done["pa"], 1)
                                else:
                                    v.tensor_reduce(dst, src, AX, ALU.max).then_inc(done["pa"], 1)

                    def epilogue(L, b):
                        per = 1 if L.relative else 3
                        n = nth("ps", L.p, per * b)
                        dve.wait_ge(full["ps"], n)
                        p = bank("ps", n)[0:T, :]
                        H = L.heads
                        if L is CROSS1:
                            sums = p.rearrange("p (i r) -> p i r", r=32)[:, 8:16, 0]
                            heads = p[:, 0:D].rearrange("p (h d) -> p h d", h=H)
                        else:
                            sums = p.rearrange("p (i r) -> p i r", r=32)[:, :, 16]
                            heads = p.rearrange("p (i r) -> p i r", r=32)[:, :, 0:16]
                        then(v.reciprocal(rec[:, 0:H], sums))
                        v.tensor_tensor(o[:].rearrange("p (h d) -> p h d", h=H), heads, rec[:, 0:H].unsqueeze(2).broadcast_to([T, H, D // H]), ALU.mult).then_inc(done["ps"], 1)
                        dve.wait_ge(done["ps"], n)
                        if L.relative:
                            add_x(o[:], b)
                        else:
                            n = nth("ps", L.p, per * b + 1)
                            dve.wait_ge(full["ps"], n)
                            v.tensor_copy(onT[:].rearrange("p c t -> p (c t)"), bank("ps", n)[:, 0:C * T]).then_inc(done["ps"], 1)
                            n = nth("ps", L.p, per * b + 2)
                            dve.wait_ge(full["ps"], n)
                            add_x(bank("ps", n)[0:T, 0:D], b, n)
                            if L is SELF3:
                                then(v.tensor_tensor(y[:, b % 2, :], y[:, b % 2, :], bo3[:], ALU.add))
                        moments(y[:, b % 2, :], L.p, b)

                    def attention(L):
                        if not L.relative:
                            q_bf16(L, 0)
                            q_bf16(L, 1)
                        if L is CROSS4:
                            dve.wait_ge(w_cross4, 112)
                            mask_bias(0, g * G)
                            mask_bias(1, g * G + 1)
                        maxima(L, 0)
                        for b in range(G):
                            if b + 1 < G:
                                if isinstance(L, Cross):
                                    context(L, b + 1)
                                if L is CROSS4 and b > 0:
                                    dve.wait_ge(done["pb"], pb_exp(L, b - 1, L.hgs - 1, 2))
                                    mask_bias(b + 1, g * G + b + 1)
                                maxima(L, b + 1)
                            if b + 2 < G:
                                if not L.relative:
                                    dve.wait_ge(full["pa"], pa_max(L, b, (4 if isinstance(L, Self) else L.heads) - 1))
                                    q_bf16(L, b + 2)
                            if L is CROSS1 and b + 2 < G:
                                context_stats(b + 2)
                                context_normalised(b + 2)
                            if b > 0:
                                epilogue(L, b - 1)
                                normalised(x[:, b - 1, :], y[:, (b - 1) % 2, :], L.p, b - 1, ln_done)
                        epilogue(L, G - 1)
                        normalised(x[:, G - 1, :], y[:, (G - 1) % 2, :], L.p, G - 1, ln_done)

                    copy_xT("X0")
                    dve.wait_ge(w_self0, 48)
                    for b in range(G):
                        n = nth("pk1", "S0", b)
                        dve.wait_ge(full["pk1"], n)
                        v.tensor_tensor(v16[:, b, :, 0:16], bank("pk1", n)[0:T, 0:D].rearrange("p (h d) -> p h d", h=16),
                                        bv[0][:].rearrange("p (h d) -> p h d", h=16), ALU.add).then_inc(done["pk1"], 1)
                        if b == 1:
                            dve.wait_ge(done["pk0"], nth("pk0", "S0", C - 1))
                            then(v.tensor_copy(pieces[:, 0], qT[:]))
                            then(v.tensor_tensor(rest[:], qT[:], pieces[:, 0], ALU.subtract))
                            then(v.tensor_copy(pieces[:, 1], rest[:]))
                            then(v.tensor_tensor(rest[:], rest[:], pieces[:, 1], ALU.subtract))
                            v.tensor_copy(pieces[:, 2], rest[:]).then_inc(pieces_made, 1)
                    for k in range(0, 13, 2):
                        n = nth("pa", "S0", k // 2)
                        w = min(8, T - 8 * k)
                        dve.wait_ge(full["pa"], n)
                        v.tensor_copy(pos[:, :, 8 * k:8 * k + w], bank("pa", n)[0:T, 0:64 * w].rearrange("p (i m) -> p m i", i=w)).then_inc(done["pa"], 1)
                    dve.wait_ge(done["pa"], nth("pa", "S0", 6))
                    dve.wait_ge(done["pb"], nth("pb", "S0", 5))
                    attention(SELF0)
                    dve.wait_ge(w_cross1, 96)
                    context_stats(0)
                    context_normalised(0)
                    for b in range(G):
                        moments(x[:, b, :], "z", b)
                        normalised(z[:, b, :], x[:, b, :], "z", b, z_made)
                    context(CROSS1, 0)
                    n = nth("pk1", "X1", 0)
                    dve.wait_ge(full["pk1"], n)
                    v.tensor_scalar(xT[:, 1, :], bank("pk1", n)[:, 0:GT], lat_gb[:, 1:2], lat_gb[:, 3:4], ALU.mult, ALU.add).then_inc(done["pk1"], 1)
                    context_stats(1)
                    context_normalised(1)
                    attention(CROSS1)
                    copy_xT("X2")
                    for b in range(G):
                        n = nth("ps", "F2", b)
                        dve.wait_ge(full["ps"], n)
                        add_x(bank("ps", n)[0:T, 0:D], b, n)
                        moments(y[:, b % 2, :], "F2", b)
                        normalised(x[:, b, :], y[:, b % 2, :], "F2", b, ln_done)
                    copy_xT("X3")
                    dve.wait_ge(w_self3, 80)
                    self_values(3, SELF3)
                    dve.wait_ge(done["pk0"], nth("pk0", "S3", 3))
                    v.tensor_copy(kTb[:], kT[:]).then_inc(kTb_made, 1)
                    attention(SELF3)
                    then(v.memset(vx[:, :, :, :], 1.0))
                    context(CROSS4, 0)
                    copy_xT("X4")
                    attention(CROSS4)
                    copy_xT("X5")
                    n = nth("ps", "M5", 0)
                    dve.wait_ge(full["ps"], n)
                    dve.wait_ge(w_router, 48)
                    c = [comb[:, i, :, :] for i in range(12)]

                    def over_e(ap):
                        return ap.unsqueeze(2).broadcast_to([T, G, E])
                    v.tensor_tensor(c[0], bank("ps", n)[0:T, 0:G * E].rearrange("p (b e) -> p b e", b=G),
                                    rb[:].unsqueeze(1).broadcast_to([T, G, E]), ALU.add).then_inc(done["ps"], 1)
                    dve.wait_ge(done["ps"], n)
                    top = comb[:, 10, :, :].rearrange("p b e -> p (b e)")
                    then(v.tensor_reduce(top[:, 0:4], c[0], AX, ALU.max))
                    v.tensor_tensor(c[1], c[0], over_e(top[:, 0:4]), ALU.subtract).then_inc(logit_made, 1)
                    dve.wait_ge(exp_made, 1)
                    ranks = rank8[:].unsqueeze(1).broadcast_to([T, G, E])

                    def pick_first(src, dst, t):
                        then(v.tensor_reduce(top[:, t:t + 4], src, AX, ALU.max))
                        then(v.tensor_tensor(c[8], src, over_e(top[:, t:t + 4]), ALU.is_equal))
                        then(v.tensor_tensor(c[9], c[8], ranks, ALU.mult))
                        then(v.tensor_reduce(top[:, t + 4:t + 8], c[9], AX, ALU.max))
                        then(v.tensor_tensor(dst, c[9], over_e(top[:, t + 4:t + 8]), ALU.is_equal))
                    pick_first(c[2], c[3], 4)
                    then(v.scalar_tensor_tensor(out=c[4], in0=c[3], scalar=-2.0, in1=c[2], op0=ALU.mult, op1=ALU.add))
                    pick_first(c[4], c[5], 12)
                    then(v.tensor_tensor(c[6], c[3], c[5], ALU.add))
                    then(v.tensor_tensor(c[7], c[6], c[2], ALU.mult))
                    then(v.tensor_reduce(top[:, 20:24], c[7], AX, ALU.add))
                    then(v.reciprocal(top[:, 24:28], top[:, 20:24]))
                    then(v.memset(ctop[:, :], 0.0))
                    v.tensor_tensor(c[11], c[7], over_e(top[:, 24:28]), ALU.mult).then_inc(comb_made, 1)
                    for i in range(FC, NE * FC):
                        e = i // FC - 1
                        if i % FC == 0:
                            dve.wait_ge(full["pk1"], nth("pk1", "M5", e))
                        dve.wait_ge(done["pb"], nth("pb", "M5", i))
                        v.tensor_tensor(hid[:, i % 8, :], hid[:, i % 8, :], bank("pk1", 1)[:, 0:GT], ALU.mult).then_inc(gated, 1)
                    for i in range(C):
                        n = nth("pa", "M5", i)
                        dve.wait_ge(full["pa"], n)
                        v.tensor_copy(yT[:, i, :], bank("pa", n)[:, 0:GT]).then_inc(done["pa"], 1)
                    for b in range(G):
                        n = nth("ps", "M5", 1 + b)
                        dve.wait_ge(full["ps"], n)
                        add_x(bank("ps", n)[0:T, 0:D], b, n)
                        moments(y[:, b % 2, :], "M5", b)
                        normalised(x[:, b, :], y[:, b % 2, :], "M5", b, ln_done)

            nums = [s.num for s in group_sems]
            assert max(nums) - min(nums) == len(nums) - 1
            nc.gpsimd.sem_clear(range(min(nums), max(nums) + 1))
            nc.all_engine_barrier()


def kernel(**inputs):
    import numpy as np
    import ml_dtypes
    import concourse.bacc as bacc
    from concourse.bass_utils import run_bass_kernel_spmd

    i = {k: np.asarray(v) for k, v in inputs.items()}

    def rows(w, n):
        return w.reshape(n, w.shape[0] // n, w.shape[1]).transpose(1, 0, 2)

    def col(v, n):
        return v.reshape(n, -1).T

    def padded(w, r, c):
        out = np.zeros((r, c), w.dtype)
        out[:w.shape[0], :w.shape[1]] = w
        return out

    def qkv(w, bias):
        w = w.reshape(16, 3, 16, D).transpose(1, 0, 2, 3).reshape(3 * D, D).T
        bias = bias.reshape(16, 3, 16).transpose(1, 0, 2).reshape(3, D)
        return rows(w, C), col(bias[:2].reshape(-1), 4), bias[2]

    a = {"x": i["x"], "ctx": i["ctx_768"], "ctxT": i["ctx_768"].transpose(0, 2, 1)}
    a["wqkv0"], a["bqk0"], a["bv0"] = qkv(i["L0_attn_Wqkv"], i["L0_attn_bqkv"])
    a["wqkv3"], a["bqk3"], a["bv3"] = qkv(i["L1_attn_qkv_w"], i["L1_attn_qkv_b"])
    a["wr_stack"] = np.vstack([i["L0_attn_Wr"].T] * len(PIECES) + [i["L0_attn_br"][None]] * 3)
    a["wq1"], a["wq4"] = rows(i["L0_xattn_W_Q"], C), rows(i["L1_xattn_Wq"], C)
    a["wk1"], a["wk4"] = rows(i["L0_xattn_W_K"], 2), rows(i["L1_xattn_Wk"], 2)
    a["wv1"], a["wv4"] = rows(i["L0_xattn_W_V"], 2), rows(i["L1_xattn_Wv"], 2)
    a["wo1"], a["wo4"] = rows(i["L0_xattn_W_O"], C), rows(i["L1_xattn_Wo"], C)
    a["wo3"], a["bo3"] = rows(i["L1_attn_out_w"].T, C), i["L1_attn_out_b"]
    a["lat_gb"] = np.hstack([col(i["L0_xattn_ln_lat_g"], 2), col(i["L0_xattn_ln_lat_b"], 2)])
    a["in_gb"] = np.hstack([col(i["L0_xattn_ln_in_g"], 2), col(i["L0_xattn_ln_in_b"], 2)])
    a["u1"] = rows(padded(i["L0_ffn_U1"], D, 128), C)
    a["v1"] = padded(i["L0_ffn_V1"], 128, FF)
    a["u2"] = rows(padded(i["L0_ffn_U2"], FF, 128), FF // 128)
    a["v2"] = padded(np.vstack([i["L0_ffn_V2"], i["L0_ffn_b2"][None]]), 128, D)
    a["b1c"] = col(i["L0_ffn_b1"], FF // 128)
    a["rw"], a["rb"] = rows(i["L1_ffn_router_w"].T, C), i["L1_ffn_router_b"]
    up = np.concatenate([i["L1_ffn_shared_w_up"], i["L1_ffn_w_up"]])
    down = np.concatenate([i["L1_ffn_shared_w_down"], i["L1_ffn_w_down"]])
    a["experts"] = np.concatenate([
        up.transpose(0, 2, 1).reshape(NE, C, 128, F).transpose(0, 2, 1, 3).reshape(NE, 128, C * F),
        down.transpose(0, 2, 1).reshape(NE, FC, 128, D).transpose(0, 2, 1, 3).reshape(NE, 128, FC * D)], axis=2)
    a["mask"] = i["mask_BxS2_bf1"].view(np.uint8)
    a["maskT"] = a["mask"].T

    f32 = np.float32
    p = np.arange(128)
    a["ident"] = np.eye(128, dtype=f32)
    a["mask16"] = (p[:, None] // 16 == np.arange(8)).astype(f32)
    a["mask32"] = (p[:, None] // 32 == np.arange(4)).astype(f32)
    a["one64"] = (p[:, None] == RANK).astype(f32)
    a["neghalf"] = np.full((128, 4), -0.5, f32)
    a["rank8"] = np.tile(np.arange(E, 0, -1, dtype=f32), (T, 1))
    a["sele"] = np.repeat((p[:, None] == np.arange(E)).astype(f32)[:, :, None], 128, axis=2)
    t = np.arange(T)
    dist = np.abs(t[:, None] - t[None])
    slopes = 0.5 ** np.arange(16)
    a["alibi"] = (-4.0 * dist[:, None, :] * slopes[None, :, None]).astype(ml_dtypes.bfloat16)
    pick = np.zeros((NSTACK + 3, 3), f32)
    for s, w in enumerate(WPIECES):
        pick[16 * s:16 * s + 16, w] = 1
    pick[NSTACK:] = np.eye(3)
    a["w_pick"] = pick

    nc = bacc.Bacc("TRN2", target_bir_lowering=False, num_devices=1)
    arrays, aps = {}, {}
    for k, v in a.items():
        v = np.ascontiguousarray(v)
        arrays[f"in_{k}"] = v
        aps[k] = nc.dram_tensor(f"in_{k}", v.shape, mybir.dt.from_np(v.dtype), kind="ExternalInput").ap()
    out = nc.dram_tensor("out", (B, T, D), F32, kind="ExternalOutput").ap()
    decoder(nc, aps, out)
    r = run_bass_kernel_spmd(nc, [arrays], core_ids=[0])
    return r.results[0]["out"]
```

```python
from contextlib import ExitStack

import concourse.bass as bass
from concourse import mybir
from concourse.alu_op_type import AluOpType as ALU

ACT = mybir.ActivationFunctionType
AX = mybir.AxisListType.X
F32, BF16, U8 = mybir.dt.float32, mybir.dt.bfloat16, mybir.dt.uint8
F32R = mybir.dt.float32r

B, T, D = 16, 100, 256
S, DC = 361, 192
G = 4
GT = G * T
C = D // 128
CK = DC // 2
JT = [(0, 128), (128, 128), (256, S - 256)]
FF, RANK = 1024, 64
E, F = 8, 512
NE = E + 1
FC = F // 128
NR = 257
REL0 = 128
HALO = 28
BIG = 3.3895313892515355e38
EPS = 1e-5
PIECES = [0, 0, 1, 0, 2, 1]
WPIECES = [0, 1, 0, 2, 0, 1]
NSTACK = 16 * len(PIECES)
WSLOTS = 3
LAG = 3

USES = {
    "pk0": dict(X0=1, S0=4, P1=3, X1=1, C1=2 + 9, X2=1, F2=1, X3=1, S3=4, P4=2, X4=1, C4=2 + 6, X5=1, M5=1),
    "pk1": dict(X0=1, S0=4, P1=4, X1=1, C1=12, X2=1, X3=1, S3=4, P4=3, X4=1, C4=9, X5=1, M5=E),
    "pa": dict(S0=7 + 32, C1=32, F2=4, S3=16, C4=64, M5=2 + 4),
    "pb": dict(S0=6 + 16, C1=24, F2=8, S3=16, C4=48, M5=NE * FC),
    "po": dict(S0=4, C1=4, F2=1, S3=4, C4=4),
    "ps": dict(S0=4, C1=12, S3=12, C4=12, M5=1),
    "pv": dict(S0=16, C1=8, S3=16, C4=16),
}
DEPTH = {"pa": 2, "pb": 2, "pk0": 1, "pk1": 1, "po": 1, "ps": 1}


def nth(ring, phase, i):
    before = 0
    for name, uses in USES[ring].items():
        if name == phase:
            assert i < uses, (ring, phase, i)
            return before + i + 1
        before += uses
    raise KeyError(phase)


S0_STEPS = {(h, s): [(n, 0)] for h in range(4) for s, n in enumerate(("content", "rows"))}
S0_STEPS[1, 1] += [("out", 0)]
S0_STEPS[3, 1] += [("norm", 0)]
S3_STEPS = {(h, 0): [("rows", 0)] for h in range(4)}
for h in range(1, 4):
    S3_STEPS[h, 0] += [("out", h - 1)]
S3_STEPS[2, 1] = [("q", 0)]
S3_STEPS[3, 1] = [("norm", 0)]
C1_STEPS = {
    (0, 0): [("turn", 0), ("head", 0)], (0, 1): [("keys", 0), ("head", 1), ("stats", 0)],
    (0, 2): [("keys", 1), ("head", 2), ("head", 3)], (0, 3): [("keysb", 0), ("cz", 0), ("values", 0)],
    (1, 0): [("head", 0), ("out", 0), ("head", 1)], (1, 1): [("head", 2), ("out", 1), ("head", 3)],
    (1, 2): [("out", 2), ("values", 1), ("q", 0)], (1, 3): [("values", 2), ("norm", 0)],
}
C4_STEPS = {(h, s): [("head", s)] for h in range(4) for s in range(4)}
C4_STEPS[0, 0] += [("keys", 0)]
C4_STEPS[0, 1] += [("keys", 1)]
C4_STEPS[0, 3] += [("values", 0)]
C4_STEPS[1, 0] += [("out", 0)]
C4_STEPS[1, 1] += [("values", 1)]
C4_STEPS[1, 2] += [("values", 2), ("keysb", 0), ("mask", 0)]
C4_STEPS[1, 3] += [("q", 0)]
C4_STEPS[2, 1] += [("out", 1)]
C4_STEPS[3, 0] += [("out", 2)]
C4_STEPS[3, 3] += [("norm", 0)]
S0_LAST = {(1, 1): [("turn", 0)], (2, 0): [("keys", 0)], (2, 1): [("keys", 1), ("values", 0)],
           (3, 0): [("values", 1)], (3, 1): [("values", 2), ("keysb", 0)]}
S3_LAST = {(0, 0): [("keys", 0)], (0, 1): [("keys", 1)], (1, 0): [("values", 0)], (1, 1): [("values", 1)],
           (2, 0): [("values", 2), ("keysb", 0)]}


class Self:
    heads, scale, hgs, keys, tiles, lead = 16, 0.25, 4, T, [(0, T)], 2

    def __init__(self, phase, relative, steps, last, then):
        self.p, self.relative, self.steps, self.last, self.then = phase, relative, steps, last, then


class Cross:
    keys, tiles, relative, last = S, JT, False, {}

    def __init__(self, phase, pre, heads, scale, masked, lead, steps):
        self.p, self.pre, self.heads, self.scale, self.masked = phase, pre, heads, scale, masked
        self.hgs, self.lead, self.steps = heads // 4, lead, steps


CROSS1 = Cross("C1", "P1", 8, float(32 ** -0.5), False, 1, C1_STEPS)
CROSS4 = Cross("C4", "P4", 16, 0.25, True, 2, C4_STEPS)
SELF0, SELF3 = Self("S0", True, S0_STEPS, S0_LAST, CROSS1), Self("S3", False, S3_STEPS, S3_LAST, CROSS4)


def beside(L, b, hg, slot):
    found = []
    for name, i in L.steps.get((hg, slot), []):
        if name in ("turn", "keys", "values", "keysb", "mask"):
            found += [(name, i, L, b + 1)] if b + 1 < G else []
        elif name in ("stats", "cz", "q"):
            found += [(name, i, L, b + 2)] if b + 2 < G else []
        elif name in ("out", "norm"):
            found += [(name, i, L, b - 1)] if b > 0 else []
        else:
            ahead = 3 if name == "content" else L.lead
            bb, hh = divmod(b * L.hgs + hg + ahead, L.hgs)
            if bb < G:
                found += [(name, 4 * hh + i if name == "head" else hh, L, bb)]
    if b == G - 1:
        found += [(name, i, L.then, 0) for name, i in L.last.get((hg, slot), [])]
    return found


def decoder(nc, a, out):
    with ExitStack() as ctx:
        def sb(name, shape, dt=F32):
            return ctx.enter_context(nc.sbuf_tensor(name, shape, dt))

        def sb_both(name, shape):
            with nc.sbuf_tensor(name, shape, F32) as plain:
                pass
            return plain, sb(name + "_r", shape, F32R)

        def sem(name):
            return ctx.enter_context(nc.semaphore(name))

        wqkv = {0: sb("wqkv0", [128, C, 3 * D]), 3: sb("wqkv3", [128, C, 3 * D])}
        bqk = {0: sb("bqk0", [128, 4]), 3: sb("bqk3", [128, 4])}
        bv = {0: sb("bv0", [T, D]), 3: sb("bv3", [T, D])}
        wq = {1: sb("wq1", [128, C, D]), 4: sb("wq4", [128, C, D])}
        wk = {1: sb("wk1", [CK, 2, D]), 4: sb("wk4", [CK, 2, D])}
        wv = {1: sb("wv1", [CK, 2, D]), 4: sb("wv4", [CK, 2, D])}
        wo = {1: sb("wo1", [128, C, D]), 3: sb("wo3", [128, C, D]), 4: sb("wo4", [128, C, D])}
        bo3 = sb("bo3", [T, D])
        lat_gb = sb("lat_gb", [128, 4])
        in_gb = sb("in_gb", [CK, 4])
        u1, v1 = sb("u1", [128, C, 128]), sb("v1", [128, FF])
        u2, v2 = sb("u2", [128, FF // 128, 128]), sb("v2", [128, D])
        b1c, one64 = sb("b1c", [128, FF // 128]), sb("one64", [128, 1])
        rw, rb = sb("rw", [128, C, E]), sb("rb", [T, E])
        rank8 = sb("rank8", [T, E])
        sele = sb("sele", [128, E, 128])
        ident = sb("ident", [128, 128])
        identb = sb("identb", [128, 128], BF16)
        mask16, mask32 = sb("mask16", [128, 8]), sb("mask32", [128, 4])
        negones = sb("negones", [T, 128], BF16)
        ones32 = sb("ones32", [128, 32])
        neghalf = sb("neghalf", [128, 4])
        alibi = sb("alibi", [T, 16, T], BF16)
        wstack = sb("wstack", [NSTACK + 3, NR], BF16)
        rowmask = sb("rowmask", [T, B * S], U8)
        colmask = sb("colmask", [128, 3, B], U8)
        experts, experts_r = sb_both("experts", [128, WSLOTS, 2048])

        x = sb("x", [T, G, D])
        z = sb("z", [T, G, D])
        xT = sb("xT", [128, C, GT])
        qT = sb("qT", [128, C, GT])
        kT = sb("kT", [128, C, GT])
        kTb = sb("kTb", [128, C, GT], BF16)
        v16 = sb("v16", [T, G, 16, 32])
        qbd, qbd_r = sb_both("qbd", [128, 2, 16 * T])
        qbdb = sb("qbdb", [128, 2, 16 * T + HALO], BF16)
        shift = sb("shift", [T, 2, 16])
        dshift = sb("dshift", [T, 4, 4 * T], BF16)
        pT = sb("pT", [128, 3, 3, 4 * T])
        oT = sb("oT", [128, 4, T])
        rec = sb("rec", [T, 16])
        o = sb("o", [T, D])
        onT = sb("onT", [128, C, T])
        y = sb("y", [T, 2, D])
        bn6, bn6_cx = sb("bn6", [128, 4, 6]), sb("bn6_cx", [128, 3, 6])
        mv = sb("mv", [128, 4, 3, 2])
        vare = sb("vare", [128, 4, 3])
        rstd = sb("rstd", [128, 4, 3])
        UNION = 51200
        union, union_r = sb_both("union", [128, UNION // 4])

        def region(start, parts, shape, dt):
            size, n = (2 if dt == BF16 else 4), 1
            for s in shape:
                n *= s
            assert start % 4 == 0 and start + n * size <= UNION
            v = (union_r if dt == F32R else union)[0:parts, start // 4:(start + n * size) // 4]
            if dt == BF16:
                v = v.bitcast(dt)
            if len(shape) > 1:
                names = "abcd"[:len(shape)]
                v = v.rearrange(f"p ({' '.join(names)}) -> p {' '.join(names)}",
                                **{k: s for k, s in zip(names, shape)})
            return v

        pos = region(0, T, [16 * G, T], F32)
        qstack = region(25600, NSTACK + 3, [16, GT], BF16)
        s0 = region(38400, T, [2, 16, T], F32)
        kxT = region(0, 128, [2, C, S], F32)
        kxTb = region(5776, 128, [2, C, S + 1], BF16)
        vx = region(8672, 128, [2, 3, 512], F32)
        cT = region(20960, CK, [2, 2, S], F32)
        cx = region(26736, 128, [2, 3, DC], F32)
        rowbias = region(31344, T, [2, S], F32)
        colbias = region(34232, 128, [2, 4], F32)
        hid = region(34304, 128, [8, GT], F32)
        ptok = region(0, 128, [GT], F32)
        qtok = region(1600, 128, [GT], F32)
        comb = region(0, T, [12, G, E], F32)
        ctop = region(1536, 128, [GT], F32)
        yT = region(3200, 128, [C, GT], F32)
        wh_slots = [region(6400, 128, [2, 1024], F32R), region(14592, 128, [2, 1024], F32R),
                    qbd_r[:].rearrange("p s n -> p (s n)")[:, 0:2048].rearrange("p (a n) -> p a n", a=2)]
        x_parts = region(22784, 128, [2, C, GT], F32R)
        hid_hi = region(40704, 128, [4, GT], F32R)
        hid_lo = region(34304, 128, [4, GT], F32R)

        masked = sb("masked", [T, 2, S])
        pieces = pT[:, 0].rearrange("p a n -> p (a n)").bitcast(BF16).rearrange("p (s c t) -> p s c t", s=3, c=C)
        rest = pT[:, 1, 0:C, :]
        qp_dram = nc.dram_tensor("q_pieces", (3, D, GT), BF16).ap()

        banks = {r: [ctx.enter_context(nc.psum_tensor(f"{r}_{i}", [128, 512], F32)) for i in range(n)]
                 for r, n in DEPTH.items()}

        def bank(ring, n):
            return banks[ring][(n - 1) % DEPTH[ring]]

        w_const, w_self0, w_cross1 = sem("w_const"), sem("w_self0"), sem("w_cross1")
        w_ffn, w_self3, w_cross4, w_router = sem("w_ffn"), sem("w_self3"), sem("w_cross4"), sem("w_router")
        made = sem("made")
        x_in, y_out = sem("x_in"), sem("y_out")
        group_sems = []

        def gsem(name):
            s = sem(name)
            group_sems.append(s)
            return s

        full = {r: gsem(f"{r}_full") for r in DEPTH}
        done = {r: gsem(f"{r}_done") for r in DEPTH}
        pv_done = gsem("pv_done")
        cx_in = [gsem("cx_in0"), gsem("cx_in1")]
        cT_in = [gsem("cT_in0"), gsem("cT_in1")]
        pieces_out, qstack_in = gsem("pieces_out"), gsem("qstack_in")
        half_in = [gsem(f"half_in{i}") for i in range(2 * WSLOTS)]
        down_used = gsem("down_used")
        half_hi, half_lo = gsem("half_hi"), gsem("half_lo")
        x_hi, x_lo = gsem("x_hi"), gsem("x_lo")
        hid_hi_made = gsem("hid_hi_made")
        hid_lo_made = gsem("hid_lo_made")
        pieces_made = gsem("pieces_made")
        kTb_made = gsem("kTb_made")
        qbdb_made = gsem("qbdb_made")
        qbd_made = gsem("qbd_made")
        dshift_made = gsem("dshift_made")
        var_made = gsem("var_made")
        rstd_made = gsem("rstd_made")
        ln_done = gsem("ln_done")
        z_made = gsem("z_made")
        cz_made = gsem("cz_made")
        bias_made = gsem("bias_made")
        gated = gsem("gated")
        logit_made, exp_made = gsem("logit_made"), gsem("exp_made")
        comb_made = gsem("comb_made")
        vx_ones = gsem("vx_ones")
        dve_step, pool_step = gsem("dve_step"), gsem("pool_step")

        LN = {"S0": 0, "C1": 4, "F2": 8, "S3": 12, "C4": 16, "M5": 20}
        asked = [("S0", 0), ("z", 0), ("cx", 0), ("S0", 1), ("z", 1), ("cx", 1), ("S0", 2), ("z", 2), ("S0", 3), ("z", 3)]
        asked += [("cx", 2), ("cx", 3)] + [("C1", b) for b in range(G)]
        for ph in ("F2", "S3", "C4", "M5"):
            asked += [(ph, b) for b in range(G)]
        ASK = {k: i for i, k in enumerate(asked)}
        QBD = {"S0": 0, "C1": 4, "S3": 8, "C4": 12}
        QBDB = {"C1": 0, "S3": 8, "C4": 16}
        KTB = {"C1": 0, "S3": 4, "C4": 5}

        def hg_of(L, b, hg):
            return {"S0": 0, "C1": 16, "S3": 24, "C4": 40}[L.p] + b * L.hgs + hg

        s0_fills = [("content", 0), ("content", 1), ("content", 2), ("rows", 0), ("rows", 1)]
        for u in range(4 * G):
            s0_fills += [("content", u + 3)] if u + 3 < 4 * G else []
            s0_fills += [("rows", u + 2)] if u + 2 < 4 * G else []

        def pa_content(b, hg):
            return nth("pa", "S0", 7 + s0_fills.index(("content", 4 * b + hg)))

        def pa_max(L, b, i):
            if L.p == "S0":
                return nth("pa", "S0", 7 + s0_fills.index(("rows", 4 * b + i)))
            return nth("pa", L.p, b * (4 if L.p == "S3" else L.heads) + i)

        def pb_exp(L, b, hg, jt):
            n = len(L.tiles)
            return nth("pb", L.p, (6 if L.p == "S0" else 0) + (b * L.hgs + hg) * n + jt)

        def half(k):
            return experts[:, k // 2 % WSLOTS, k % 2 * 1024:(k % 2 + 1) * 1024]

        def wait_half_used(engine, k):
            e = k // 2
            if k % 2:
                engine.wait_ge(down_used, e + 1)
            else:
                engine.wait_ge(full["pb"], nth("pb", "M5", e * FC + FC - 1))

        def half_parts(k):
            return wh_slots[k // 2 % WSLOTS][:, k % 2, :], experts_r[:, k // 2 % WSLOTS, k % 2 * 1024:(k % 2 + 1) * 1024]

        def kv_fill(L, b, ring, i):
            per = USES[ring][L.pre]
            if b == 0:
                return nth(ring, L.pre, i)
            return nth(ring, L.p, (2 if ring == "pk0" else 0) + (b - 1) * per + i)

        with nc.Block() as block:
            @block.sync
            def _(sync):
                sync.dma_start(z[:], a["x"][0:G].rearrange("b t d -> t b d")).then_inc(x_in, 16)
                sync.dma_start(ident[:], a["ident"]).then_inc(w_const, 16)
                sync.dma_start(wqkv[0][:], a["wqkv0"]).then_inc(w_self0, 16)
                sync.dma_start(bqk[0][:], a["bqk0"]).then_inc(w_self0, 16)
                sync.dma_start(bv[0][:], a["bv0"].partition_broadcast(T)).then_inc(w_self0, 16)
                sync.dma_start(union[0:NSTACK + 3, 0:NR], a["wr_stack"]).then_inc(w_const, 16)
                sync.dma_start(union[0:NSTACK + 3, 300:303], a["w_pick"]).then_inc(w_const, 16)
                for t, n in ((mask16, "mask16"), (mask32, "mask32"), (one64, "one64"), (neghalf, "neghalf"), (rank8, "rank8")):
                    sync.dma_start(t[:], a[n]).then_inc(w_const, 16)

            @block.scalar
            def _(act):
                act.wait_ge(w_self0, 48)
                for t, n in ((wq[1], "wq1"), (wk[1], "wk1"), (wv[1], "wv1"), (wo[1], "wo1"),
                             (lat_gb, "lat_gb"), (in_gb, "in_gb")):
                    act.dma_start(t[:], a[n]).then_inc(w_cross1, 16)
                for t, n in ((u1, "u1"), (v1, "v1"), (u2, "u2"), (v2, "v2"), (b1c, "b1c")):
                    act.dma_start(t[:], a[n]).then_inc(w_ffn, 16)
                act.dma_start(wqkv[3][:], a["wqkv3"]).then_inc(w_self3, 16)
                act.dma_start(bqk[3][:], a["bqk3"]).then_inc(w_self3, 16)
                act.dma_start(bv[3][:], a["bv3"].partition_broadcast(T)).then_inc(w_self3, 16)
                act.dma_start(bo3[:], a["bo3"].partition_broadcast(T)).then_inc(w_self3, 16)
                act.dma_start(wo[3][:], a["wo3"]).then_inc(w_self3, 16)
                act.dma_start(alibi[:], a["alibi"]).then_inc(w_self3, 16)
                for t, n in ((wq[4], "wq4"), (wk[4], "wk4"), (wv[4], "wv4"), (wo[4], "wo4")):
                    act.dma_start(t[:], a[n]).then_inc(w_cross4, 16)
                act.dma_start(colmask[:, 0:2, :], a["maskT"][0:256, :].rearrange("(j p) b -> p j b", p=128)).then_inc(w_cross4, 16)
                act.dma_start(colmask[0:S - 256, 2, :], a["maskT"][256:S, :]).then_inc(w_cross4, 16)
                act.dma_start(rowmask[:], a["mask"].rearrange("b s -> (b s)").partition_broadcast(T)).then_inc(w_cross4, 16)
                act.dma_start(rw[:], a["rw"]).then_inc(w_router, 16)
                act.dma_start(sele[:], a["sele"]).then_inc(w_router, 16)
                act.dma_start(rb[:], a["rb"].partition_broadcast(T)).then_inc(w_router, 16)

            @block.vector
            def _(dve):
                nc.vector.memset(negones[:], -1.0).then_inc(made, 1)
                nc.vector.memset(rec[:], 1.0).then_inc(y_out, 1)
                nc.vector.memset(ones32[:], 1.0).then_inc(made, 1)
                nc.vector.memset(v16[:], 1.0).then_inc(made, 1)
                nc.vector.memset(qbdb[:], 0.0).then_inc(made, 1)
                nc.vector.memset(mv[:], 1.0).then_inc(made, 1)
                dve.wait_ge(w_const, 128)
                nc.vector.tensor_copy(identb[:], ident[:]).then_inc(made, 1)
                R = NSTACK + 3
                w = union[0:R, 0:NR]
                pick = union[0:R, 300:303]
                hb = union[0:R, 400:400 + 130].bitcast(BF16)[:, 0:NR]
                mb = union[0:R, 600:600 + 130].bitcast(BF16)[:, 0:NR]
                lb = union[0:R, 800:800 + 130].bitcast(BF16)[:, 0:NR]
                r = union[0:R, 1000:1000 + NR]
                r2 = union[0:R, 1300:1300 + NR]
                nc.vector.tensor_copy(hb, w).then_inc(made, 1)
                dve.wait_ge(made, 7)
                nc.vector.tensor_tensor(r, w, hb, ALU.subtract).then_inc(made, 1)
                dve.wait_ge(made, 8)
                nc.vector.tensor_copy(mb, r).then_inc(made, 1)
                dve.wait_ge(made, 9)
                nc.vector.tensor_tensor(r2, r, mb, ALU.subtract).then_inc(made, 1)
                dve.wait_ge(made, 10)
                nc.vector.tensor_copy(lb, r2).then_inc(made, 1)
                dve.wait_ge(made, 11)
                nc.vector.tensor_scalar(r, hb, pick[:, 0:1], None, ALU.mult).then_inc(made, 1)
                dve.wait_ge(made, 12)
                nc.vector.scalar_tensor_tensor(out=r2, in0=mb, scalar=pick[:, 1:2], in1=r, op0=ALU.mult, op1=ALU.add).then_inc(made, 1)
                dve.wait_ge(made, 13)
                nc.vector.scalar_tensor_tensor(out=wstack[:], in0=lb, scalar=pick[:, 2:3], in1=r2, op0=ALU.mult, op1=ALU.add).then_inc(made, 1)
                dve.wait_ge(made, 14)

        with nc.Fori(0, B // G, 1) as g:
            with nc.Block() as block:

                @block.sync
                def _(sync):
                    for k in range(2 * WSLOTS):
                        sync.dma_start(half(k), a["experts"][k // 2][:, k % 2 * 1024:(k % 2 + 1) * 1024]).then_inc(half_in[k], 16)
                    sync.wait_ge(pieces_made, 1)
                    sync.dma_start(qp_dram.rearrange("s (c p) t -> p s c t", p=128), pieces[:]).then_inc(pieces_out, 16)
                    sync.wait_ge(pieces_out, 16)
                    for s, piece in enumerate(PIECES):
                        sync.dma_start(qstack[16 * s:16 * s + 16], qp_dram[piece].rearrange("(h d) t -> d h t", d=16)).then_inc(qstack_in, 16)
                    for b in range(G):
                        if b < 2:
                            sync.wait_ge(full["pa"], nth("pa", "S0", 6))
                        else:
                            sync.wait_ge(full["pk1"], kv_fill(CROSS1, b - 2, "pk1", 0))
                            sync.wait_ge(full["pk0"], kv_fill(CROSS1, b - 2, "pk0", 0))
                        src = a["ctx"][bass.ds(g * G + b, 1)].rearrange("a s d -> (a s) d")
                        sync.dma_start(cx[:, b % 2, 0:2, :], src[0:256, :].rearrange("(j p) d -> p j d", p=128)).then_inc(cx_in[b % 2], 16)
                        sync.dma_start(cx[0:S - 256, b % 2, 2, :], src[256:S, :]).then_inc(cx_in[b % 2], 16)
                    sync.wait_ge(full["pk0"], nth("pk0", "X1", 0))
                    sync.wait_ge(full["pk1"], nth("pk1", "X1", 0))
                    sync.dma_start(z[:], a["x"][bass.ds((g + 1) % (B // G) * G, G)].rearrange("b t d -> t b d")).then_inc(x_in, 16)
                    for b in range(G):
                        L, u = (CROSS1, b + 2) if b < 2 else (CROSS4, b - 2)
                        sync.wait_ge(full["pk1"], kv_fill(L, u, "pk1", USES["pk1"][L.pre] - 1))
                        src = a["ctxT"][bass.ds(g * G + b, 1)].rearrange("a d s -> (a d) s")
                        sync.dma_start(cT[:, b % 2, :, :], src.rearrange("(k p) s -> p k s", p=CK)).then_inc(cT_in[b % 2], 16)
                    for k in range(2 * WSLOTS, 2 * NE):
                        wait_half_used(sync, k - 2 * WSLOTS)
                        sync.dma_start(half(k), a["experts"][k // 2][:, k % 2 * 1024:(k % 2 + 1) * 1024]).then_inc(half_in[k % (2 * WSLOTS)], 16)
                    for b in range(G):
                        sync.wait_ge(ln_done, LN["M5"] + b + 1)
                        sync.dma_start(out[bass.ds(g * G + b, 1)].rearrange("a t d -> (a t) d"), x[:, b, :]).then_inc(y_out, 16)

                @block.tensor
                def _(pe):
                    mm = nc.tensor.matmul

                    def claim(ring, n):
                        if n > DEPTH[ring]:
                            pe.wait_ge(done[ring], n - DEPTH[ring])
                        return bank(ring, n)

                    def transpose_x(ph, src, ready, counts):
                        for b in range(G):
                            pe.wait_ge(ready, counts[b])
                            for c, ring in enumerate(("pk0", "pk1")):
                                n = nth(ring, ph, 0)
                                p = claim(ring, n) if b == 0 else bank(ring, n)
                                last = nc.tensor.transpose(p[:, b * T:(b + 1) * T], src[:, b, c * 128:(c + 1) * 128], ident[0:T, 0:T])
                                if b == G - 1:
                                    last.then_inc(full[ring], 1)

                    def wait_xT(ph):
                        pe.wait_ge(done["pk0"], nth("pk0", ph, 0))
                        pe.wait_ge(done["pk1"], nth("pk1", ph, 0))

                    def project_T(ring, n, w, col):
                        p = claim(ring, n)
                        for k in range(C):
                            last = mm(p[:, 0:GT], w[:, k, col:col + 128], xT[:, k, :], start=(k == 0), stop=(k == C - 1))
                        last.then_inc(full[ring], 1)

                    def self_project(li, L):
                        for i in range(4):
                            project_T("pk0", nth("pk0", L.p, i), wqkv[li], 128 * i)
                            n = nth("pk1", L.p, i)
                            p = claim("pk1", n)
                            for k in range(C):
                                last = mm(p[0:T, 0:D], xT[:, k, i * T:(i + 1) * T], wqkv[li][:, k, 2 * D:3 * D], start=(k == 0), stop=(k == C - 1))
                            last.then_inc(full["pk1"], 1)

                    def positions():
                        pe.wait_ge(qstack_in, 16 * len(PIECES))
                        pe.wait_ge(pool_step, 1)
                        for k in range(13):
                            ring = "pa" if k % 2 == 0 else "pb"
                            n = nth(ring, "S0", k // 2)
                            p = claim(ring, n)
                            for i in range(8 * k, min(8 * k + 8, T)):
                                u = i - 8 * k
                                rhs = qstack.rearrange("r h (b t) -> r h b t", b=G)[:, :, :, i]
                                last = mm(p[:, 64 * u:64 * u + 64], wstack[:, REL0 - i:REL0 - i + 128], rhs, start=True, stop=True)
                            last.then_inc(full[ring], 1)

                    def turn(L, b):
                        s = b % 2
                        pe.wait_ge(cz_made, b + 1)
                        for c, ring in enumerate(("pk0", "pk1")):
                            n = kv_fill(L, b, ring, 0)
                            p = claim(ring, n)
                            for j, (j0, J) in enumerate(JT):
                                last = nc.tensor.transpose(p[0:CK, j0:j0 + J], cx[0:J, s, j, c * CK:(c + 1) * CK], ident[0:J, 0:J])
                            last.then_inc(full[ring], 1)

                    def wait_context(L, b):
                        if L is CROSS1:
                            pe.wait_ge(done["pk0"], kv_fill(L, b, "pk0", 0))
                            pe.wait_ge(done["pk1"], kv_fill(L, b, "pk1", 0))
                        else:
                            pe.wait_ge(w_cross4, 112)
                            pe.wait_ge(cT_in[b % 2], 16 * (b // 2 + 1))

                    def keys(L, b, i):
                        wk_l = wk[1] if L is CROSS1 else wk[4]
                        if i == 0:
                            wait_context(L, b)
                        n = kv_fill(L, b, "pk0", (1 if L is CROSS1 else 0) + i)
                        p = claim("pk0", n)
                        for k in range(2):
                            last = mm(p[:, 0:S], wk_l[:, k, i * 128:(i + 1) * 128], cT[:, b % 2, k, :], start=(k == 0), stop=(k == 1))
                        last.then_inc(full["pk0"], 1)

                    def values(L, b, i):
                        wv_l = wv[1] if L is CROSS1 else wv[4]
                        n = kv_fill(L, b, "pk1", (1 if L is CROSS1 else 0) + i)
                        p = claim("pk1", n)
                        j0, J = JT[i]
                        for k in range(2):
                            last = mm(p[0:J, 0:D], cT[:, b % 2, k, j0:j0 + J], wv_l[:, k, :], start=(k == 0), stop=(k == 1))
                        last.then_inc(full["pk1"], 1)

                    def q_chunks(L, h):
                        return min(C, (h + 1) // (L.heads // C) + 1)

                    def content(b, hg):
                        pe.wait_ge(qbd_made, QBD["S0"] + b + 1)
                        mm(claim("pa", pa_content(b, hg))[0:T, 0:4 * T], kT[:, hg // 2, b * T:(b + 1) * T], qbd[:, b % 2, hg * 4 * T:(hg + 1) * 4 * T],
                           start=True, stop=True).then_inc(full["pa"], 1)

                    def rows(L, b, hg):
                        s = b % 2
                        if L.relative:
                            pe.wait_ge(done["pa"], pa_content(b, hg))
                            p = claim("pa", pa_max(L, b, hg))
                            for h in range(4):
                                last = nc.tensor.transpose(p[0:T, h * T:(h + 1) * T], s0[:, s, 4 * hg + h, :], ident[0:T, 0:T])
                            last.then_inc(full["pa"], 1)
                            return
                        pe.wait_ge(kTb_made, KTB[L.p] + 1)
                        pe.wait_ge(qbdb_made, QBDB[L.p] + 2 * b + q_chunks(L, 4 * hg + 3))
                        p = claim("pa", pa_max(L, b, hg))
                        mm(p[:, 0:4 * T], identb[0:T, :], alibi[:, 4 * hg:4 * hg + 4, :].rearrange("p h t -> p (h t)"), start=True, stop=True)
                        for u in range(4):
                            h = 4 * hg + u
                            last = mm(p[:, u * T:(u + 1) * T], qbdb[:, s, h * T:h * T + 128], kTb[:, h // 8, b * T:(b + 1) * T],
                                      start=False, stop=True, skip_group_check=True)
                        last.then_inc(full["pa"], 1)

                    def head(L, b, h):
                        pe.wait_ge(kTb_made, KTB[L.p] + b + 1)
                        pe.wait_ge(qbdb_made, QBDB[L.p] + 2 * b + q_chunks(L, h))
                        mm(claim("pa", pa_max(L, b, h))[:, 0:S], qbdb[:, b % 2, h * T:h * T + 128], kxTb[:, b % 2, h // (L.heads // C), 0:S],
                           start=True, stop=True).then_inc(full["pa"], 1)

                    def exp_scores(L, b, hg, j):
                        s, d = b % 2, hg_of(L, b, hg)
                        if not L.relative:
                            pe.wait_ge(qbd_made, QBD[L.p] + b + 1)
                        j0, J = L.tiles[j]
                        p = claim("pb", pb_exp(L, b, hg, j))[0:J, 0:4 * T]
                        if L.relative:
                            mm(p, ident[0:T, 0:T], s0[:, s, 4 * hg:4 * hg + 4, :].rearrange("p h t -> p (h t)"), start=True, stop=False)
                        else:
                            chunk = 4 * hg // (L.heads // C)
                            k = kT[:, chunk, b * T:(b + 1) * T] if isinstance(L, Self) else kxT[:, s, chunk, j0:j0 + J]
                            mm(p, k, qbd[:, s, hg * 4 * T:(hg + 1) * 4 * T], start=True, stop=False)
                            if isinstance(L, Self):
                                mm(p, identb[0:T, 0:T], alibi[:, 4 * hg:4 * hg + 4, :].rearrange("p h t -> p (h t)"), start=False, stop=False)
                        if j == 0:
                            pe.wait_ge(dshift_made, d + 1)
                        mm(p, negones[:, 0:J], dshift[:, d % 4, :], start=False, stop=True).then_inc(full["pb"], 1)

                    def times_v(L, b, hg):
                        d = hg_of(L, b, hg)
                        slot, p = d % 3, bank("po", 1)
                        if hg == 0:
                            n = nth("po", L.p, b)
                            if n > 1:
                                pe.wait_ge(done["po"], n - 1)
                            if isinstance(L, Self):
                                pe.wait_ge(done["pk1"], nth("pk1", L.p, G - 1))
                            else:
                                pe.wait_ge(done["pk1"], kv_fill(L, b, "pk1", USES["pk1"][L.pre] - 1))
                        last_tile = len(L.tiles) - 1
                        for j, (j0, J) in enumerate(L.tiles):
                            pe.wait_ge(done["pb"], pb_exp(L, b, hg, j))
                            for u in range(4):
                                h = 4 * hg + u
                                if isinstance(L, Self):
                                    v = v16[:, b, h, :]
                                else:
                                    v = vx[0:J, b % 2, j, 32 * h:32 * h + 32]
                                last = mm(p[32 * u:32 * u + 32, hg * T:(hg + 1) * T], v, pT[0:J, slot, j, u * T:(u + 1) * T],
                                          start=(j == 0), stop=(j == last_tile), skip_group_check=True)
                        if L is CROSS1:
                            for j, (j0, J) in enumerate(L.tiles):
                                for u in range(4):
                                    last = mm(p[32 * u:32 * u + 32, (2 + hg) * T:(3 + hg) * T], ones32[0:J, :], pT[0:J, slot, j, u * T:(u + 1) * T],
                                              start=(j == 0), stop=(j == last_tile), skip_group_check=True)
                        last.then_inc(pv_done, 1)

                    def epilogue(L, li, b, part):
                        per = 1 if L.relative else 3
                        if part == 0:
                            n = nth("ps", L.p, per * b)
                            p = claim("ps", n)
                            pe.wait_ge(done["po"], nth("po", L.p, b))
                            for i in range(4):
                                last = nc.tensor.transpose(p[0:T, i * 128:(i + 1) * 128], oT[:, i, :], ident[:, :])
                            last.then_inc(full["ps"], 1)
                        elif L.relative:
                            return
                        elif part == 1:
                            n = nth("ps", L.p, per * b + 1)
                            p = claim("ps", n)
                            for c in range(C):
                                last = nc.tensor.transpose(p[:, c * T:(c + 1) * T], o[:, c * 128:(c + 1) * 128], ident[0:T, 0:T])
                            last.then_inc(full["ps"], 1)
                        else:
                            n = nth("ps", L.p, per * b + 2)
                            p = claim("ps", n)
                            for c in range(C):
                                last = mm(p[0:T, 0:D], onT[:, c, :], wo[li][:, c, :], start=(c == 0), stop=(c == C - 1))
                            last.then_inc(full["ps"], 1)

                    def steps_beside(L, li, b, hg, slot):
                        for name, i, M, bb in beside(L, b, hg, slot):
                            if name == "turn":
                                turn(M, bb)
                            elif name == "keys":
                                keys(M, bb, i)
                            elif name == "values":
                                values(M, bb, i)
                            elif name == "content":
                                content(bb, i)
                            elif name == "rows":
                                rows(M, bb, i)
                            elif name == "head":
                                head(M, bb, i)
                            elif name == "out":
                                epilogue(M, li, bb, i)

                    def attention(L, li):
                        if L.relative:
                            pe.wait_ge(done["pk0"], nth("pk0", "S0", 3))
                            for hg in range(3):
                                content(0, hg)
                        for hg in range(L.lead):
                            if isinstance(L, Self):
                                rows(L, 0, hg)
                            else:
                                for h in range(4 * hg, 4 * hg + 4):
                                    head(L, 0, h)
                        for u in range(G * L.hgs):
                            b, hg = divmod(u, L.hgs)
                            for j in range(len(L.tiles)):
                                exp_scores(L, b, hg, j)
                                steps_beside(L, li, b, hg, j)
                            if u > 0:
                                times_v(L, (u - 1) // L.hgs, (u - 1) % L.hgs)
                            steps_beside(L, li, b, hg, len(L.tiles))
                        times_v(L, G - 1, L.hgs - 1)
                        for part in range(3):
                            epilogue(L, li, G - 1, part)

                    def three_products(parts):
                        return [(0, parts[0]), (1, parts[0]), (0, parts[1])]

                    pe.wait_ge(w_const, 128)
                    pe.wait_ge(w_self0, 48)
                    pe.wait_ge(made, 14)
                    transpose_x("X0", z, x_in, [(g + 1) * 16] * G)
                    wait_xT("X0")
                    self_project(0, SELF0)
                    positions()
                    pe.wait_ge(w_cross1, 96)
                    attention(SELF0, 0)
                    transpose_x("X1", z, z_made, [b + 1 for b in range(G)])
                    wait_xT("X1")
                    for i in range(C):
                        project_T("pk0", nth("pk0", "C1", i), wq[1], 128 * i)
                    attention(CROSS1, 1)
                    pe.wait_ge(w_ffn, 80)
                    transpose_x("X2", x, ln_done, [LN["C1"] + b + 1 for b in range(G)])
                    wait_xT("X2")
                    project_T("pk0", nth("pk0", "F2", 0), u1, 0)
                    pe.wait_ge(done["pk0"], nth("pk0", "F2", 0))
                    NF = FF // 128
                    n_po = nth("po", "F2", 0)
                    for i in range(NF + LAG):
                        if i < NF:
                            n = nth("pb", "F2", i)
                            mm(claim("pb", n)[:, 0:GT], v1[:, i * 128:(i + 1) * 128], ptok, start=True, stop=True).then_inc(full["pb"], 1)
                        if i >= LAG:
                            f = i - LAG
                            if f == 0:
                                claim("po", n_po)
                            pe.wait_ge(done["pb"], nth("pb", "F2", f))
                            last = mm(bank("po", 1)[:, 0:GT], u2[:, f, :], hid[:, f, :], start=(f == 0), stop=(f == NF - 1))
                    last.then_inc(full["po"], 1)
                    pe.wait_ge(done["po"], n_po)
                    for b in range(G):
                        p = claim("pa", nth("pa", "F2", b))
                        mm(p[0:T, 0:D], qtok[:, b * T:(b + 1) * T], v2[:], start=True, stop=True).then_inc(full["pa"], 1)
                    pe.wait_ge(w_self3, 96)
                    transpose_x("X3", x, ln_done, [LN["F2"] + b + 1 for b in range(G)])
                    wait_xT("X3")
                    self_project(3, SELF3)
                    attention(SELF3, 3)
                    transpose_x("X4", x, ln_done, [LN["S3"] + b + 1 for b in range(G)])
                    wait_xT("X4")
                    for i in range(C):
                        project_T("pk0", nth("pk0", "C4", i), wq[4], 128 * i)
                    attention(CROSS4, 4)
                    pe.wait_ge(w_router, 48)
                    transpose_x("X5", x, ln_done, [LN["C4"] + b + 1 for b in range(G)])
                    wait_xT("X5")
                    n = nth("ps", "M5", 0)
                    p = claim("ps", n)
                    for b in range(G):
                        for k in range(C):
                            last = mm(p[0:T, b * E:(b + 1) * E], xT[:, k, b * T:(b + 1) * T], rw[:, k, :], start=(k == 0), stop=(k == C - 1))
                    last.then_inc(full["ps"], 1)
                    pe.wait_ge(x_lo, 1)
                    yb = [claim("pa", nth("pa", "M5", i)) for i in range(C)]
                    chunks = NE * FC
                    for i in range(chunks + LAG):
                        if i < chunks:
                            e, f = divmod(i, FC)
                            if f == 0:
                                pe.wait_ge(half_lo, 2 * e + 1)
                            p = claim("pb", nth("pb", "M5", i))
                            steps = [(w.rearrange("p (c f) -> p c f", c=C)[:, c, f * 128:(f + 1) * 128], x_parts[:, x, c, :])
                                     for x, w in three_products(half_parts(2 * e)) for c in range(C)]
                            for k, (w, xs) in enumerate(steps):
                                last = mm(p[:, 0:GT], w, xs, start=(k == 0), stop=(k == len(steps) - 1))
                            last.then_inc(full["pb"], 1)
                        if i >= LAG:
                            u = i - LAG
                            e, f = divmod(u, FC)
                            pe.wait_ge(hid_lo_made, u + 1)
                            if f == 0:
                                pe.wait_ge(half_lo, 2 * e + 2)
                            h_parts = [hid_hi[:, u % 4, :], hid_lo[:, u % 4, :]]
                            steps = [(w.rearrange("p (f d) -> p f d", f=FC)[:, f, :], h_parts[x]) for x, w in three_products(half_parts(2 * e + 1))]
                            for k, (w, hs) in enumerate(steps):
                                for c in range(C):
                                    last = mm(yb[c][:, 0:GT], w[:, c * 128:(c + 1) * 128], hs, start=(u == 0 and k == 0), stop=(u == chunks - 1 and k == 2))
                                    if u == chunks - 1 and k == 2:
                                        last.then_inc(full["pa"], 1)
                            if f == FC - 1 and e + WSLOTS < NE:
                                last.then_inc(down_used, 1)
                        if i == FC:
                            pe.wait_ge(comb_made, 1)
                            p = claim("pk0", nth("pk0", "M5", 0))
                            for b in range(G):
                                last = nc.tensor.transpose(p[0:E, b * T:(b + 1) * T], comb[:, 11, b, :], ident[0:T, 0:T])
                            last.then_inc(full["pk0"], 1)
                            pe.wait_ge(done["pk0"], nth("pk0", "M5", 0))
                        if i % FC == 0 and 0 < i < chunks:
                            e = i // FC - 1
                            if e > 0:
                                pe.wait_ge(gated, FC * e)
                            else:
                                pe.wait_ge(done["pk1"], nth("pk1", "X5", 0))
                            mm(bank("pk1", 1)[:, 0:GT], sele[:, e, :], ctop, start=True, stop=True).then_inc(full["pk1"], 1)
                    for i in range(C):
                        pe.wait_ge(done["pa"], nth("pa", "M5", i))
                    for b in range(G):
                        p = claim("pa", nth("pa", "M5", C + b))
                        for c in range(C):
                            last = nc.tensor.transpose(p[0:T, c * 128:(c + 1) * 128], yT[:, c, b * T:(b + 1) * T], ident[:, :])
                        last.then_inc(full["pa"], 1)

                @block.scalar
                def _(act):
                    fn = nc.scalar.activation

                    def copy_xT(ph):
                        n = nth("pk0", ph, 0)
                        act.wait_ge(full["pk0"], n)
                        fn(xT[:, 0, :], bank("pk0", n)[:, 0:GT], ACT.Copy).then_inc(done["pk0"], 1)

                    def project_q(L):
                        for c in range(C):
                            n = nth("pk0", L.p, c)
                            act.wait_ge(full["pk0"], n)
                            fn(qT[:, c, :], bank("pk0", n)[:, 0:GT], ACT.Copy).then_inc(done["pk0"], 1)

                    def self_project(li, L):
                        for i in range(4):
                            n = nth("pk0", L.p, i)
                            act.wait_ge(full["pk0"], n)
                            dst = (qT if i < C else kT)[:, i % C, :]
                            fn(dst, bank("pk0", n)[:, 0:GT], ACT.Identity, bias=bqk[li][:, i:i + 1]).then_inc(done["pk0"], 1)

                    def steps_beside(L, b, hg, slot):
                        for name, i, M, bb in beside(L, b, hg, slot):
                            if name == "turn":
                                n = kv_fill(M, bb, "pk0", 0)
                                act.wait_ge(full["pk0"], n)
                                fn(cT[:, bb % 2, 0, :], bank("pk0", n)[0:CK, 0:S], ACT.Identity, bias=in_gb[:, 2:3], scale=in_gb[:, 0:1]).then_inc(done["pk0"], 1)
                            elif name == "keys":
                                n = kv_fill(M, bb, "pk0", (1 if M is CROSS1 else 0) + i)
                                act.wait_ge(full["pk0"], n)
                                fn(kxT[:, bb % 2, i, :], bank("pk0", n)[:, 0:S], ACT.Copy).then_inc(done["pk0"], 1)

                    def attention(L):
                        for u in range(G * L.hgs):
                            b, hg = divmod(u, L.hgs)
                            d = hg_of(L, b, hg)
                            if d >= 3:
                                act.wait_ge(pv_done, d - 2)
                            for j, (j0, J) in enumerate(L.tiles):
                                n = pb_exp(L, b, hg, j)
                                act.wait_ge(full["pb"], n)
                                src, dst = bank("pb", n)[0:J, 0:4 * T], pT[0:J, d % 3, j, :]
                                scale = 1.0 if L.relative else L.scale
                                if L is CROSS4:
                                    if hg == 0 and j == 0:
                                        act.wait_ge(bias_made, 3 * b + 3)
                                    fn(dst, src, ACT.Exp, bias=colbias[0:J, b % 2, j:j + 1], scale=scale).then_inc(done["pb"], 1)
                                else:
                                    fn(dst, src, ACT.Exp, scale=scale).then_inc(done["pb"], 1)
                                steps_beside(L, b, hg, j)
                            if b > 0 and hg == 0:
                                heads_out(L, b - 1)
                            steps_beside(L, b, hg, len(L.tiles))
                        heads_out(L, G - 1)

                    def heads_out(L, b):
                        act.wait_ge(pv_done, hg_of(L, b, L.hgs - 1) + 1)
                        fn(oT[:].rearrange("p h t -> p (h t)"), bank("po", 1)[:, 0:4 * T], ACT.Copy).then_inc(done["po"], 1)

                    def half_high(k):
                        if k >= 2 * WSLOTS:
                            wait_half_used(act, k - 2 * WSLOTS)
                        act.wait_ge(half_in[k % (2 * WSLOTS)], 16 * (k // (2 * WSLOTS) + 1))
                        fn(half_parts(k)[0], half(k), ACT.Copy).then_inc(half_hi, 1)

                    copy_xT("X0")
                    act.wait_ge(w_self0, 48)
                    self_project(0, SELF0)
                    for k in range(1, 13, 2):
                        n = nth("pb", "S0", k // 2)
                        act.wait_ge(full["pb"], n)
                        fn(pos[:, :, 8 * k:8 * k + 8], bank("pb", n)[0:T, :].rearrange("p (i m) -> p m i", i=8), ACT.Copy).then_inc(done["pb"], 1)
                    act.wait_ge(w_cross1, 96)
                    attention(SELF0)
                    n = nth("pk0", "X1", 0)
                    act.wait_ge(full["pk0"], n)
                    fn(xT[:, 0, :], bank("pk0", n)[:, 0:GT], ACT.Identity, bias=lat_gb[:, 2:3], scale=lat_gb[:, 0:1]).then_inc(done["pk0"], 1)
                    project_q(CROSS1)
                    attention(CROSS1)
                    copy_xT("X2")
                    act.wait_ge(w_ffn, 80)
                    n = nth("pk0", "F2", 0)
                    act.wait_ge(full["pk0"], n)
                    fn(ptok, bank("pk0", n)[:, 0:GT], ACT.Copy).then_inc(done["pk0"], 1)
                    for i in range(FF // 128):
                        n = nth("pb", "F2", i)
                        act.wait_ge(full["pb"], n)
                        fn(hid[:, i, :], bank("pb", n)[:, 0:GT], ACT.Gelu_apprx_tanh, bias=b1c[:, i:i + 1]).then_inc(done["pb"], 1)
                    act.wait_ge(full["po"], 1)
                    fn(qtok, bank("po", 1)[:, 0:GT], ACT.Identity, bias=one64[:]).then_inc(done["po"], 1)
                    copy_xT("X3")
                    act.wait_ge(w_self3, 96)
                    self_project(3, SELF3)
                    attention(SELF3)
                    copy_xT("X4")
                    project_q(CROSS4)
                    attention(CROSS4)
                    copy_xT("X5")
                    act.wait_ge(logit_made, 1)
                    fn(comb[:, 2, :, :].rearrange("p b e -> p (b e)"), comb[:, 1, :, :].rearrange("p b e -> p (b e)"), ACT.Exp).then_inc(exp_made, 1)
                    for k in range(4):
                        half_high(k)
                    for i in range(NE * FC + 1):
                        if i < NE * FC:
                            if i == FC + 1:
                                n = nth("pk0", "M5", 0)
                                act.wait_ge(full["pk0"], n)
                                fn(ctop[0:E, :], bank("pk0", n)[0:E, 0:GT], ACT.Copy).then_inc(done["pk0"], 1)
                            n = nth("pb", "M5", i)
                            act.wait_ge(full["pb"], n)
                            fn(hid[:, i % 4, :], bank("pb", n)[:, 0:GT], ACT.Silu).then_inc(done["pb"], 1)
                        if i > 0:
                            if i - 1 < FC:
                                act.wait_ge(done["pb"], nth("pb", "M5", i - 1))
                            else:
                                act.wait_ge(gated, i - FC)
                            fn(hid_hi[:, (i - 1) % 4, :], hid[:, (i - 1) % 4, :], ACT.Copy).then_inc(hid_hi_made, 1)
                        if i % FC in (1, 3) and i // FC + 2 <= NE:
                            k = 2 * (i // FC + 1) + (i % FC == 3)
                            if k >= 4:
                                half_high(k)

                @block.gpsimd
                def _(pool):
                    steps = [0]

                    def block_diagonal(L, b):
                        per = L.heads // C
                        m = mask16 if per == 8 else mask32
                        for c in range(C):
                            dst = qbd[:, b % 2, c * per * T:(c + 1) * per * T].rearrange("p (h t) -> p h t", h=per)
                            q = qT[:, c, b * T:(b + 1) * T].unsqueeze(1).broadcast_to([128, per, T])
                            ins = nc.gpsimd.tensor_tensor(dst, q, m[:].unsqueeze(2).broadcast_to([128, per, T]), ALU.mult)
                        ins.then_inc(qbd_made, 1)

                    def diagonal_shifts(L, b, hg):
                        d = hg_of(L, b, hg)
                        if d >= 4:
                            for_L, bb, hh = owner(d - 4)
                            pool.wait_ge(full["pb"], pb_exp(for_L, bb, hh, len(for_L.tiles) - 1))
                        pool.wait_ge(done["pa"], pa_max(L, b, 4 * hg + 3 if isinstance(L, Cross) else hg))
                        dst = dshift[:, d % 4, :].rearrange("p (h t) -> p h t", h=4)
                        i3 = ident[0:T, 0:T].unsqueeze(1).broadcast_to([T, 4, T])
                        m = shift[:, b % 2, 4 * hg:4 * hg + 4].unsqueeze(2).broadcast_to([T, 4, T])
                        nc.gpsimd.tensor_tensor(dst, i3, m, ALU.mult).then_inc(dshift_made, 1)

                    def owner(d):
                        for L in (SELF0, CROSS1, SELF3, CROSS4):
                            d0 = hg_of(L, 0, 0)
                            if d0 <= d < d0 + G * L.hgs:
                                return L, (d - d0) // L.hgs, (d - d0) % L.hgs

                    def inverse_std(what, b):
                        r = ASK[(what, b)]
                        P, n = (128, 3) if what == "cx" else (T, 1)
                        pool.wait_ge(var_made, r + 1)
                        nc.gpsimd.tensor_scalar(vare[0:P, r % 4, 0:n], mv[0:P, r % 4, 0:n, 1], EPS, None, ALU.add).then_inc(pool_step, 1)
                        steps[0] += 1
                        pool.wait_ge(pool_step, steps[0])
                        nc.gpsimd.tensor_tensor(rstd[0:P, r % 4, 0:n], vare[0:P, r % 4, 0:n], neghalf[0:P, 0:n], ALU.pow).then_inc(rstd_made, 1)

                    def attention(L):
                        ph = L.p
                        pool.wait_ge(done["pk0"], nth("pk0", ph, C - 1))
                        block_diagonal(L, 0)
                        for hg in range(L.lead):
                            diagonal_shifts(L, 0, hg)
                        if L.relative:
                            block_diagonal(L, 1)
                        for u in range(G * L.hgs):
                            b, hg = divmod(u, L.hgs)
                            if L is SELF0 and hg == 0 and b >= 2:
                                inverse_std("z", b - 2)
                            if L is SELF0 and hg == 1 and b >= 2:
                                inverse_std("cx", b - 2)
                            if L.hgs == 4 and b > 0 and hg == L.hgs - 1:
                                inverse_std(ph, b - 1)
                            if u + L.lead < G * L.hgs:
                                diagonal_shifts(L, (u + L.lead) // L.hgs, (u + L.lead) % L.hgs)
                            if L is CROSS1 and hg == 0 and b + 2 < G:
                                inverse_std("cx", b + 2)
                            if L is CROSS1 and b > 0 and hg == L.hgs - 1:
                                inverse_std(ph, b - 1)
                            if L.relative and hg == 0 and b + 2 < G:
                                pool.wait_ge(full["pa"], pa_content(b, 3))
                                block_diagonal(L, b + 2)
                            if not L.relative and hg == 0 and b + 1 < G:
                                if b > 0:
                                    pool.wait_ge(full["pb"], pb_exp(L, b - 1, L.hgs - 1, len(L.tiles) - 1))
                                block_diagonal(L, b + 1)
                        if L is not SELF0:
                            inverse_std(ph, G - 1)

                    pool.memset(qstack[NSTACK:NSTACK + 3], 1.0).then_inc(pool_step, 1)
                    steps[0] += 1
                    pool.wait_ge(pool_step, 1)
                    pool.wait_ge(w_const, 128)
                    attention(SELF0)
                    for what, b in (("z", 2), ("S0", 3), ("z", 3)):
                        inverse_std(what, b)
                    attention(CROSS1)
                    pool.wait_ge(pv_done, hg_of(CROSS1, G - 1, 1) + 1)
                    pool.memset(vx[:], 1.0).then_inc(vx_ones, 1)
                    for b in range(G):
                        inverse_std("F2", b)
                    attention(SELF3)
                    attention(CROSS4)
                    for k in range(2 * NE):
                        pool.wait_ge(half_hi, k + 1)
                        nc.gpsimd.tensor_tensor(half_parts(k)[1], half(k), half_parts(k)[0].bitcast(F32), ALU.subtract).then_inc(half_lo, 1)
                    for b in range(G):
                        inverse_std("M5", b)

                @block.vector
                def _(dve):
                    v = nc.vector
                    steps = [0]

                    def then(ins):
                        ins.then_inc(dve_step, 1)
                        steps[0] += 1
                        dve.wait_ge(dve_step, steps[0])

                    def copy_xT(ph):
                        n = nth("pk1", ph, 0)
                        dve.wait_ge(full["pk1"], n)
                        v.tensor_copy(xT[:, 1, :], bank("pk1", n)[:, 0:GT]).then_inc(done["pk1"], 1)

                    def moments(src, what, b):
                        r = ASK[(what, b)]
                        then(v.bn_stats(bn6[0:T, r % 4, :], src))
                        v.bn_aggr(mv[0:T, r % 4, 0, :], bn6[0:T, r % 4, :]).then_inc(var_made, 1)

                    def normalised(dst, src, what, b, signal):
                        r = ASK[(what, b)]
                        dve.wait_ge(rstd_made, r + 1)
                        v.tensor_scalar(dst, src, mv[0:T, r % 4, 0, 0:1], rstd[0:T, r % 4, 0:1], ALU.subtract, ALU.mult).then_inc(signal, 1)

                    def add_x(src, b, ring_n=None, ring="ps", residual=None):
                        ins = v.tensor_tensor(y[:, b % 2, :], src, (x if residual is None else residual)[:, b, :], ALU.add)
                        if ring_n is None:
                            then(ins)
                        else:
                            ins.then_inc(done[ring], 1)
                            dve.wait_ge(done[ring], ring_n)

                    def sums_and_norms(ph, first):
                        for b in range(G + 1):
                            if b < G:
                                n = nth("pa", ph, first + b)
                                if b > 1:
                                    dve.wait_ge(ln_done, LN[ph] + b - 1)
                                dve.wait_ge(full["pa"], n)
                                add_x(bank("pa", n)[0:T, 0:D], b, n, "pa")
                                moments(y[:, b % 2, :], ph, b)
                            if b > 0:
                                normalised(x[:, b - 1, :], y[:, (b - 1) % 2, :], ph, b - 1, ln_done)

                    def self_values(li, L):
                        for b in range(G):
                            n = nth("pk1", L.p, b)
                            dve.wait_ge(full["pk1"], n)
                            v.tensor_tensor(v16[:, b, :, 0:16], bank("pk1", n)[0:T, 0:D].rearrange("p (h d) -> p h d", h=16),
                                            bv[li][:].rearrange("p (h d) -> p h d", h=16), ALU.add).then_inc(done["pk1"], 1)

                    def context_stats(b):
                        s, r = b % 2, ASK[("cx", b)]
                        dve.wait_ge(cx_in[s], 32 * (b // 2 + 1))
                        for j, (j0, J) in enumerate(JT):
                            then(v.bn_stats(bn6_cx[0:J, j, :], cx[0:J, s, j, :]))
                        for j, (j0, J) in enumerate(JT):
                            ins = v.bn_aggr(mv[0:J, r % 4, j, :], bn6_cx[0:J, j, :])
                            if j < 2:
                                then(ins)
                        ins.then_inc(var_made, 1)

                    def context_normalised(b):
                        s, r = b % 2, ASK[("cx", b)]
                        dve.wait_ge(rstd_made, r + 1)
                        for j, (j0, J) in enumerate(JT):
                            ins = v.tensor_scalar(cx[0:J, s, j, :], cx[0:J, s, j, :], mv[0:J, r % 4, j, 0:1], rstd[0:J, r % 4, j:j + 1], ALU.subtract, ALU.mult)
                            if j < 2:
                                then(ins)
                        ins.then_inc(cz_made, 1)

                    def turned(L, b):
                        n = kv_fill(L, b, "pk1", 0)
                        dve.wait_ge(full["pk1"], n)
                        v.tensor_scalar(cT[:, b % 2, 1, :], bank("pk1", n)[0:CK, 0:S], in_gb[:, 1:2], in_gb[:, 3:4], ALU.mult, ALU.add).then_inc(done["pk1"], 1)

                    def values(L, b, i):
                        s, (j0, J) = b % 2, JT[i]
                        n = kv_fill(L, b, "pk1", (1 if L is CROSS1 else 0) + i)
                        dve.wait_ge(full["pk1"], n)
                        src = bank("pk1", n)[0:J, 0:D]
                        if L is CROSS1:
                            ins = v.tensor_copy(vx[0:J, s, i, 0:D], src)
                        else:
                            dve.wait_ge(vx_ones, 1)
                            ins = v.tensor_copy(vx[0:J, s, i, :].rearrange("p (h d) -> p h d", h=16)[:, :, 0:16], src.rearrange("p (h d) -> p h d", h=16))
                        ins.then_inc(done["pk1"], 1)

                    def keys_bf16(L, b):
                        dve.wait_ge(done["pk0"], kv_fill(L, b, "pk0", USES["pk0"][L.pre] - 1))
                        v.tensor_copy(kxTb[:, b % 2, :, 0:S], kxT[:, b % 2, :, :]).then_inc(kTb_made, 1)

                    def mask_bias(b, batch):
                        row = rowmask[:, bass.ds(batch * S, S)]
                        v.tensor_scalar(rowbias[:, b % 2, :], row, 1.0, BIG, ALU.subtract, ALU.mult).then_inc(bias_made, 1)
                        for P, j0, j1 in ((128, 0, 2), (S - 256, 2, 3)):
                            col = colmask[0:P, j0:j1, bass.ds(batch, 1)].rearrange("p j a -> p (j a)")
                            v.tensor_scalar(colbias[0:P, b % 2, j0:j1], col, 1.0, BIG * CROSS4.scale, ALU.subtract, ALU.mult).then_inc(bias_made, 1)

                    def q_bf16(L, b):
                        per = L.heads // C
                        m = mask16 if per == 8 else mask32
                        for c in range(C):
                            if b == 0:
                                dve.wait_ge(done["pk0"], nth("pk0", L.p, c))
                            dst = qbdb[:, b % 2, c * per * T:(c + 1) * per * T].rearrange("p (h t) -> p h t", h=per)
                            q = qT[:, c, b * T:(b + 1) * T].unsqueeze(1).broadcast_to([128, per, T])
                            v.tensor_tensor(dst, q, m[:].unsqueeze(2).broadcast_to([128, per, T]), ALU.mult).then_inc(qbdb_made, 1)

                    def content(b, hg):
                        n = pa_content(b, hg)
                        dve.wait_ge(full["pa"], n)
                        v.scalar_tensor_tensor(
                            out=s0[:, b % 2, 4 * hg:4 * hg + 4, :], in0=bank("pa", n)[0:T, 0:4 * T].rearrange("p (h t) -> p h t", h=4), scalar=SELF0.scale,
                            in1=pos.rearrange("p (h b) t -> p h b t", b=G)[:, 4 * hg:4 * hg + 4, b, :],
                            op0=ALU.mult, op1=ALU.add).then_inc(done["pa"], 1)

                    def wait_shift(L, b):
                        if b > 1:
                            dve.wait_ge(dshift_made, hg_of(L, b - 2, L.hgs - 1) + 1)

                    def row_maxima(L, b, hg):
                        if hg == 0:
                            wait_shift(L, b)
                        n = pa_max(L, b, hg)
                        dve.wait_ge(full["pa"], n)
                        v.tensor_reduce(shift[:, b % 2, 4 * hg:4 * hg + 4], bank("pa", n)[0:T, 0:4 * T].rearrange("p (h t) -> p h t", h=4), AX, ALU.max).then_inc(done["pa"], 1)

                    def head_maxima(L, b, h):
                        if h == 0:
                            wait_shift(L, b)
                            if L.masked:
                                dve.wait_ge(bias_made, 3 * b + 3)
                        n = pa_max(L, b, h)
                        dve.wait_ge(full["pa"], n)
                        src, dst = bank("pa", n)[0:T, 0:S], shift[:, b % 2, h:h + 1]
                        if L.masked:
                            v.tensor_tensor_reduce(masked[:, h % 2, :], src, rowbias[:, b % 2, :], 1.0, -3.4e38, ALU.add, ALU.max, dst).then_inc(done["pa"], 1)
                        else:
                            v.tensor_reduce(dst, src, AX, ALU.max).then_inc(done["pa"], 1)

                    def epilogue(L, b, part):
                        per = 1 if L.relative else 3
                        if part == 0:
                            n = nth("ps", L.p, per * b)
                            dve.wait_ge(full["ps"], n)
                            p = bank("ps", n)[0:T, :]
                            H = L.heads
                            if L is CROSS1:
                                sums = p.rearrange("p (i r) -> p i r", r=32)[:, 8:16, 0]
                                heads = p[:, 0:D].rearrange("p (h d) -> p h d", h=H)
                            else:
                                sums = p.rearrange("p (i r) -> p i r", r=32)[:, :, 16]
                                heads = p.rearrange("p (i r) -> p i r", r=32)[:, :, 0:16]
                            then(v.reciprocal(rec[:, 0:H], sums))
                            v.tensor_tensor(o[:].rearrange("p (h d) -> p h d", h=H), heads, rec[:, 0:H].unsqueeze(2).broadcast_to([T, H, D // H]), ALU.mult).then_inc(done["ps"], 1)
                            if L.relative:
                                dve.wait_ge(done["ps"], n)
                                add_x(o[:], b, residual=z)
                                moments(y[:, b % 2, :], L.p, b)
                        elif L.relative:
                            return
                        elif part == 1:
                            n = nth("ps", L.p, per * b + 1)
                            dve.wait_ge(full["ps"], n)
                            v.tensor_copy(onT[:].rearrange("p c t -> p (c t)"), bank("ps", n)[:, 0:C * T]).then_inc(done["ps"], 1)
                        else:
                            n = nth("ps", L.p, per * b + 2)
                            dve.wait_ge(full["ps"], n)
                            add_x(bank("ps", n)[0:T, 0:D], b, n)
                            if L is SELF3:
                                then(v.tensor_tensor(y[:, b % 2, :], y[:, b % 2, :], bo3[:], ALU.add))
                            moments(y[:, b % 2, :], L.p, b)

                    def steps_beside(L, b, hg, slot):
                        for name, i, M, bb in beside(L, b, hg, slot):
                            if name == "turn":
                                turned(M, bb)
                            elif name == "values":
                                values(M, bb, i)
                            elif name == "keysb":
                                keys_bf16(M, bb)
                            elif name == "content":
                                content(bb, i)
                            elif name == "rows":
                                row_maxima(M, bb, i)
                            elif name == "head":
                                head_maxima(M, bb, i)
                            elif name == "stats":
                                context_stats(bb)
                            elif name == "cz":
                                context_normalised(bb)
                            elif name == "q":
                                dve.wait_ge(full["pa"], pa_max(M, bb - 2, (4 if isinstance(M, Self) else M.heads) - 1))
                                q_bf16(M, bb)
                            elif name == "mask":
                                if bb > 1:
                                    dve.wait_ge(done["pb"], pb_exp(M, bb - 2, M.hgs - 1, 2))
                                mask_bias(bb, g * G + bb)
                            elif name == "out":
                                epilogue(M, bb, i)
                            elif name == "norm":
                                normalised(x[:, bb, :], y[:, bb % 2, :], M.p, bb, ln_done)

                    def attention(L):
                        if not L.relative:
                            q_bf16(L, 0)
                        else:
                            for hg in range(3):
                                content(0, hg)
                        for hg in range(L.lead):
                            if isinstance(L, Self):
                                row_maxima(L, 0, hg)
                            else:
                                for h in range(4 * hg, 4 * hg + 4):
                                    head_maxima(L, 0, h)
                        if not L.relative:
                            q_bf16(L, 1)
                        for u in range(G * L.hgs):
                            b, hg = divmod(u, L.hgs)
                            if L is SELF0 and b >= 2 and hg == 0:
                                context_stats(b - 2)
                            for slot in range(len(L.tiles) + 1):
                                steps_beside(L, b, hg, slot)
                            if L is SELF0 and b >= 2 and hg == 1:
                                normalised(z[:, b - 2, :], x[:, b - 2, :], "z", b - 2, z_made)
                                context_normalised(b - 2)
                            if L is SELF0 and b >= 1 and hg == 3:
                                dve.wait_ge(ln_done, b)
                                moments(x[:, b - 1, :], "z", b - 1)
                        if L is SELF0:
                            epilogue(L, G - 1, 0)
                            normalised(z[:, 2, :], x[:, 2, :], "z", 2, z_made)
                            normalised(x[:, 3, :], y[:, 1, :], "S0", 3, ln_done)
                            dve.wait_ge(ln_done, LN["C1"])
                            moments(x[:, 3, :], "z", 3)
                            normalised(z[:, 3, :], x[:, 3, :], "z", 3, z_made)
                            return
                        for part in range(3):
                            epilogue(L, G - 1, part)
                        normalised(x[:, G - 1, :], y[:, (G - 1) % 2, :], L.p, G - 1, ln_done)

                    dve.wait_ge(x_in, (g + 1) * 16)
                    dve.wait_ge(y_out, g * (16 * G) + 1)
                    copy_xT("X0")
                    dve.wait_ge(w_self0, 48)
                    for b in range(G):
                        n = nth("pk1", "S0", b)
                        dve.wait_ge(full["pk1"], n)
                        v.tensor_tensor(v16[:, b, :, 0:16], bank("pk1", n)[0:T, 0:D].rearrange("p (h d) -> p h d", h=16),
                                        bv[0][:].rearrange("p (h d) -> p h d", h=16), ALU.add).then_inc(done["pk1"], 1)
                        if b == 1:
                            dve.wait_ge(done["pk0"], nth("pk0", "S0", C - 1))
                            then(v.tensor_copy(pieces[:, 0], qT[:]))
                            then(v.tensor_tensor(rest[:], qT[:], pieces[:, 0], ALU.subtract))
                            then(v.tensor_copy(pieces[:, 1], rest[:]))
                            then(v.tensor_tensor(rest[:], rest[:], pieces[:, 1], ALU.subtract))
                            v.tensor_copy(pieces[:, 2], rest[:]).then_inc(pieces_made, 1)
                    for k in range(0, 13, 2):
                        n = nth("pa", "S0", k // 2)
                        w = min(8, T - 8 * k)
                        dve.wait_ge(full["pa"], n)
                        v.tensor_copy(pos[:, :, 8 * k:8 * k + w], bank("pa", n)[0:T, 0:64 * w].rearrange("p (i m) -> p m i", i=w)).then_inc(done["pa"], 1)
                    dve.wait_ge(done["pa"], nth("pa", "S0", 6))
                    dve.wait_ge(done["pb"], nth("pb", "S0", 5))
                    dve.wait_ge(w_cross1, 96)
                    attention(SELF0)
                    n = nth("pk1", "X1", 0)
                    dve.wait_ge(full["pk1"], n)
                    v.tensor_scalar(xT[:, 1, :], bank("pk1", n)[:, 0:GT], lat_gb[:, 1:2], lat_gb[:, 3:4], ALU.mult, ALU.add).then_inc(done["pk1"], 1)
                    attention(CROSS1)
                    copy_xT("X2")
                    sums_and_norms("F2", 0)
                    copy_xT("X3")
                    dve.wait_ge(w_self3, 96)
                    self_values(3, SELF3)
                    dve.wait_ge(done["pk0"], nth("pk0", "S3", 3))
                    v.tensor_copy(kTb[:], kT[:]).then_inc(kTb_made, 1)
                    attention(SELF3)
                    dve.wait_ge(w_cross4, 112)
                    mask_bias(0, g * G)
                    copy_xT("X4")
                    attention(CROSS4)
                    copy_xT("X5")
                    dve.wait_ge(done["pk0"], nth("pk0", "X5", 0))
                    dve.wait_ge(done["pk1"], nth("pk1", "X5", 0))
                    dve.wait_ge(pv_done, hg_of(CROSS4, G - 1, 3) + 1)
                    v.tensor_copy(x_parts[:, 0], xT[:]).then_inc(x_hi, 1)
                    dve.wait_ge(x_hi, 1)
                    v.tensor_tensor(x_parts[:, 1], xT[:], x_parts[:, 0].bitcast(F32), ALU.subtract).then_inc(x_lo, 1)
                    n = nth("ps", "M5", 0)
                    dve.wait_ge(full["ps"], n)
                    dve.wait_ge(w_router, 48)
                    c = [comb[:, i, :, :] for i in range(12)]

                    def over_e(ap):
                        return ap.unsqueeze(2).broadcast_to([T, G, E])
                    v.tensor_tensor(c[0], bank("ps", n)[0:T, 0:G * E].rearrange("p (b e) -> p b e", b=G),
                                    rb[:].unsqueeze(1).broadcast_to([T, G, E]), ALU.add).then_inc(done["ps"], 1)
                    dve.wait_ge(done["ps"], n)
                    top = comb[:, 10, :, :].rearrange("p b e -> p (b e)")
                    then(v.tensor_reduce(top[:, 0:4], c[0], AX, ALU.max))
                    v.tensor_tensor(c[1], c[0], over_e(top[:, 0:4]), ALU.subtract).then_inc(logit_made, 1)
                    dve.wait_ge(exp_made, 1)
                    ranks = rank8[:].unsqueeze(1).broadcast_to([T, G, E])

                    def pick_first(src, dst, t):
                        then(v.tensor_reduce(top[:, t:t + 4], src, AX, ALU.max))
                        then(v.tensor_tensor(c[8], src, over_e(top[:, t:t + 4]), ALU.is_equal))
                        then(v.tensor_tensor(c[9], c[8], ranks, ALU.mult))
                        then(v.tensor_reduce(top[:, t + 4:t + 8], c[9], AX, ALU.max))
                        then(v.tensor_tensor(dst, c[9], over_e(top[:, t + 4:t + 8]), ALU.is_equal))
                    pick_first(c[2], c[3], 4)
                    then(v.scalar_tensor_tensor(out=c[4], in0=c[3], scalar=-2.0, in1=c[2], op0=ALU.mult, op1=ALU.add))
                    pick_first(c[4], c[5], 12)
                    then(v.tensor_tensor(c[6], c[3], c[5], ALU.add))
                    then(v.tensor_tensor(c[7], c[6], c[2], ALU.mult))
                    then(v.tensor_reduce(top[:, 20:24], c[7], AX, ALU.add))
                    then(v.reciprocal(top[:, 24:28], top[:, 20:24]))
                    then(v.memset(ctop[:, :], 0.0))
                    v.tensor_tensor(c[11], c[7], over_e(top[:, 24:28]), ALU.mult).then_inc(comb_made, 1)
                    for i in range(NE * FC + 1):
                        if FC <= i < NE * FC:
                            e = i // FC - 1
                            if i % FC == 0:
                                dve.wait_ge(full["pk1"], nth("pk1", "M5", e))
                            dve.wait_ge(done["pb"], nth("pb", "M5", i))
                            v.tensor_tensor(hid[:, i % 4, :], hid[:, i % 4, :], bank("pk1", 1)[:, 0:GT], ALU.mult).then_inc(gated, 1)
                        if i > 0:
                            h = hid[:, (i - 1) % 4, :]
                            dve.wait_ge(hid_hi_made, i)
                            v.tensor_tensor(hid_lo[:, (i - 1) % 4, :], h, hid_hi[:, (i - 1) % 4, :].bitcast(F32), ALU.subtract).then_inc(hid_lo_made, 1)
                    for i in range(C):
                        n = nth("pa", "M5", i)
                        dve.wait_ge(full["pa"], n)
                        v.tensor_copy(yT[:, i, :], bank("pa", n)[:, 0:GT]).then_inc(done["pa"], 1)
                    sums_and_norms("M5", C)

            nums = [s.num for s in group_sems]
            assert max(nums) - min(nums) == len(nums) - 1
            nc.gpsimd.sem_clear(range(min(nums), max(nums) + 1))
            nc.all_engine_barrier()

        nc.sync.wait_ge(y_out, 16 * B + 1)
        nc.sync.wait_ge(x_in, 16 * (B // G + 1))


def kernel(**inputs):
    import numpy as np
    import ml_dtypes
    import concourse.bacc as bacc
    from concourse.bass_utils import run_bass_kernel_spmd

    i = {k: np.asarray(v) for k, v in inputs.items()}

    def rows(w, n):
        return w.reshape(n, w.shape[0] // n, w.shape[1]).transpose(1, 0, 2)

    def col(v, n):
        return v.reshape(n, -1).T

    def padded(w, r, c):
        out = np.zeros((r, c), w.dtype)
        out[:w.shape[0], :w.shape[1]] = w
        return out

    def qkv(w, bias):
        w = w.reshape(16, 3, 16, D).transpose(1, 0, 2, 3).reshape(3 * D, D).T
        bias = bias.reshape(16, 3, 16).transpose(1, 0, 2).reshape(3, D)
        return rows(w, C), col(bias[:2].reshape(-1), 4), bias[2]

    a = {"x": i["x"], "ctx": i["ctx_768"], "ctxT": i["ctx_768"].transpose(0, 2, 1)}
    a["wqkv0"], a["bqk0"], a["bv0"] = qkv(i["L0_attn_Wqkv"], i["L0_attn_bqkv"])
    a["wqkv3"], a["bqk3"], a["bv3"] = qkv(i["L1_attn_qkv_w"], i["L1_attn_qkv_b"])
    a["wr_stack"] = np.vstack([i["L0_attn_Wr"].T] * len(PIECES) + [i["L0_attn_br"][None]] * 3)
    a["wq1"], a["wq4"] = rows(i["L0_xattn_W_Q"], C), rows(i["L1_xattn_Wq"], C)
    a["wk1"], a["wk4"] = rows(i["L0_xattn_W_K"], 2), rows(i["L1_xattn_Wk"], 2)
    a["wv1"], a["wv4"] = rows(i["L0_xattn_W_V"], 2), rows(i["L1_xattn_Wv"], 2)
    a["wo1"], a["wo4"] = rows(i["L0_xattn_W_O"], C), rows(i["L1_xattn_Wo"], C)
    a["wo3"], a["bo3"] = rows(i["L1_attn_out_w"].T, C), i["L1_attn_out_b"]
    a["lat_gb"] = np.hstack([col(i["L0_xattn_ln_lat_g"], 2), col(i["L0_xattn_ln_lat_b"], 2)])
    a["in_gb"] = np.hstack([col(i["L0_xattn_ln_in_g"], 2), col(i["L0_xattn_ln_in_b"], 2)])
    a["u1"] = rows(padded(i["L0_ffn_U1"], D, 128), C)
    a["v1"] = padded(i["L0_ffn_V1"], 128, FF)
    a["u2"] = rows(padded(i["L0_ffn_U2"], FF, 128), FF // 128)
    a["v2"] = padded(np.vstack([i["L0_ffn_V2"], i["L0_ffn_b2"][None]]), 128, D)
    a["b1c"] = col(i["L0_ffn_b1"], FF // 128)
    a["rw"], a["rb"] = rows(i["L1_ffn_router_w"].T, C), i["L1_ffn_router_b"]
    up = np.concatenate([i["L1_ffn_shared_w_up"], i["L1_ffn_w_up"]])
    down = np.concatenate([i["L1_ffn_shared_w_down"], i["L1_ffn_w_down"]])
    a["experts"] = np.concatenate([
        up.transpose(0, 2, 1).reshape(NE, C, 128, F).transpose(0, 2, 1, 3).reshape(NE, 128, C * F),
        down.transpose(0, 2, 1).reshape(NE, FC, 128, D).transpose(0, 2, 1, 3).reshape(NE, 128, FC * D)], axis=2)
    a["mask"] = i["mask_BxS2_bf1"].view(np.uint8)
    a["maskT"] = a["mask"].T

    f32 = np.float32
    p = np.arange(128)
    a["ident"] = np.eye(128, dtype=f32)
    a["mask16"] = (p[:, None] // 16 == np.arange(8)).astype(f32)
    a["mask32"] = (p[:, None] // 32 == np.arange(4)).astype(f32)
    a["one64"] = (p[:, None] == RANK).astype(f32)
    a["neghalf"] = np.full((128, 4), -0.5, f32)
    a["rank8"] = np.tile(np.arange(E, 0, -1, dtype=f32), (T, 1))
    a["sele"] = np.repeat((p[:, None] == np.arange(E)).astype(f32)[:, :, None], 128, axis=2)
    t = np.arange(T)
    dist = np.abs(t[:, None] - t[None])
    slopes = 0.5 ** np.arange(16)
    a["alibi"] = (-4.0 * dist[:, None, :] * slopes[None, :, None]).astype(ml_dtypes.bfloat16)
    pick = np.zeros((NSTACK + 3, 3), f32)
    for s, w in enumerate(WPIECES):
        pick[16 * s:16 * s + 16, w] = 1
    pick[NSTACK:] = np.eye(3)
    a["w_pick"] = pick

    nc = bacc.Bacc("TRN2", target_bir_lowering=False, num_devices=1)
    arrays, aps = {}, {}
    for k, v in a.items():
        v = np.ascontiguousarray(v)
        arrays[f"in_{k}"] = v
        aps[k] = nc.dram_tensor(f"in_{k}", v.shape, mybir.dt.from_np(v.dtype), kind="ExternalInput").ap()
    out = nc.dram_tensor("out", (B, T, D), F32, kind="ExternalOutput").ap()
    decoder(nc, aps, out)
    r = run_bass_kernel_spmd(nc, [arrays], core_ids=[0])
    return r.results[0]["out"]
```

```python
from contextlib import ExitStack

import concourse.bass as bass
from concourse import mybir
from concourse.alu_op_type import AluOpType as ALU

ACT = mybir.ActivationFunctionType
AX = mybir.AxisListType.X
F32, BF16, U8 = mybir.dt.float32, mybir.dt.bfloat16, mybir.dt.uint8
F32R = mybir.dt.float32r

B, T, D = 16, 100, 256
S, DC = 361, 192
G = 4
GT = G * T
C = D // 128
CK = DC // 2
JT = [(0, 128), (128, 128), (256, S - 256)]
FF, RANK = 1024, 64
E, F = 8, 512
NE = E + 1
FC = F // 128
NR = 257
REL0 = 128
HALO = 28
BIG = 3.3895313892515355e38
EPS = 1e-5
PIECES = [0, 0, 1, 0, 2, 1]
WPIECES = [0, 1, 0, 2, 0, 1]
NSTACK = 16 * len(PIECES)
WSLOTS = 3
LAG = 3

USES = {
    "pk0": dict(X0=1, S0=3, P1=3, X1=1, C1=1 + 9, X2=1, F2=1, X3=1, S3=3, P4=4, X4=1, C4=1 + 4, X5=1, M5=1),
    "pk1": dict(X0=1, S0=1, X1=1, C1=1, X2=1, X3=1, S3=1, X4=1, C4=1, X5=1, M5=E),
    "pa": dict(S0=G + 7 + 32 + 1, C1=32 + 3, F2=4, S3=G + 16 + 3, C4=64 + 3, M5=1 + 2 + 4),
    "pb": dict(S0=6 + 16, C1=24, F2=8, S3=16, C4=48, M5=NE * FC),
    "po": dict(S0=4, C1=4, F2=1, S3=4, C4=4),
    "pv": dict(S0=16, C1=8, S3=16, C4=16),
}
DEPTH = {"pa": 3, "pb": 2, "pk0": 1, "pk1": 1, "po": 1}


def nth(ring, phase, i):
    before = 0
    for name, uses in USES[ring].items():
        if name == phase:
            assert i < uses, (ring, phase, i)
            return before + i + 1
        before += uses
    raise KeyError(phase)


S0_STEPS = {(h, s): [(n, 0)] for h in range(4) for s, n in enumerate(("content", "rows"))}
S0_STEPS[1, 1] += [("out", 0)]
S0_STEPS[3, 1] += [("norm", 0)]
S3_STEPS = {(h, 0): [("rows", 0)] for h in range(4)}
for h in range(1, 4):
    S3_STEPS[h, 0] += [("out", h - 1)]
S3_STEPS[1, 1] = [("qbd", 0)]
S3_STEPS[2, 1] = [("q", 0)]
S3_STEPS[3, 1] = [("norm", 0)]
C1_STEPS = {
    (0, 0): [("turn", 0), ("head", 0)], (0, 1): [("keys", 0), ("head", 1), ("stats", 0)],
    (0, 2): [("keys", 1), ("head", 2), ("head", 3)], (0, 3): [("keysb", 0), ("cz", 0), ("values", 0)],
    (1, 0): [("values", 1), ("head", 0), ("out", 0), ("head", 1)], (1, 1): [("head", 2), ("out", 1), ("head", 3)],
    (1, 2): [("out", 2)], (1, 3): [("values", 2), ("norm", 0)],
}
C4_STEPS = {(h, s): [("head", s)] for h in range(4) for s in range(4)}
C4_STEPS[0, 0] += [("keys", 0)]
C4_STEPS[0, 1] += [("split", 0)]
C4_STEPS[0, 2] += [("keys", 1), ("mask", 0)]
C4_STEPS[0, 3] += [("split", 1), ("values", 0)]
C4_STEPS[1, 0] += [("values", 1)]
C4_STEPS[1, 1] += [("values", 2)]
C4_STEPS[1, 3] += [("out", 0)]
C4_STEPS[2, 2] += [("out", 1)]
C4_STEPS[3, 0] += [("out", 2)]
C4_STEPS[3, 3] += [("norm", 0)]
S0_LAST = {(1, 1): [("turn", 0)], (2, 0): [("keys", 0)], (2, 1): [("keys", 1), ("values", 0)],
           (3, 0): [("values", 1)], (3, 1): [("values", 2), ("keysb", 0)]}
S3_LAST = {(0, 0): [("keys", 0)], (0, 1): [("keys", 1), ("split", 0)], (1, 0): [("split", 1), ("values", 0)],
           (1, 1): [("values", 1)], (2, 0): [("values", 2)]}

S0_TAIL = [("out", 0)]
S3_TAIL = [("out", 0), ("keys", 0), ("out", 1), ("keys", 1), ("out", 2), ("values", 0), ("split", 0), ("values", 1),
           ("norm", 0), ("split", 1), ("values", 2)]
CROSS_TAIL = [("out", 0), ("out", 1), ("out", 2), ("norm", 0)]


class Self:
    heads, scale, hgs, keys, tiles, lead = 16, 0.25, 4, T, [(0, T)], 2

    def __init__(self, phase, relative, steps, last, tail, then):
        self.p, self.relative, self.steps, self.last, self.tail, self.then = phase, relative, steps, last, tail, then


class Cross:
    keys, tiles, relative, last, tail, then = S, JT, False, {}, CROSS_TAIL, None

    def __init__(self, phase, pre, heads, scale, masked, lead, steps, early):
        self.p, self.pre, self.heads, self.scale, self.masked = phase, pre, heads, scale, masked
        self.hgs, self.lead, self.steps = heads // 4, lead, steps
        self.early = early


CROSS1 = Cross("C1", "P1", 8, float(32 ** -0.5), False, 1, C1_STEPS, 1)
CROSS4 = Cross("C4", "P4", 16, 0.25, True, 3, C4_STEPS, 2)
SELF0, SELF3 = Self("S0", True, S0_STEPS, S0_LAST, S0_TAIL, CROSS1), Self("S3", False, S3_STEPS, S3_LAST, S3_TAIL, CROSS4)


def beside(L, b, hg, slot):
    found = []
    for name, i in L.steps.get((hg, slot), []):
        if name in ("turn", "keys", "split", "values", "keysb"):
            found += [(name, i, L, b + 1)] if L.early <= b + 1 < G else []
        elif name in ("mask", "qbd"):
            found += [(name, i, L, b + 1)] if b + 1 < G else []
        elif name in ("stats", "cz", "q"):
            found += [(name, i, L, b + 2)] if b + 2 < G else []
        elif name in ("out", "norm"):
            found += [(name, i, L, b - 1)] if b > 0 else []
        else:
            ahead = 3 if name == "content" else L.lead
            bb, hh = divmod(b * L.hgs + hg + ahead, L.hgs)
            if bb < G:
                found += [(name, 4 * hh + i if name == "head" else hh, L, bb)]
    if b == G - 1:
        found += [(name, i, L.then, 0) for name, i in L.last.get((hg, slot), [])]
    return found


def tail_of(L):
    return [(name, i, L, G - 1) if name in ("out", "norm") else (name, i, L.then, 1) for name, i in L.tail]


def side_fills(L):
    steps = []
    for u in range(G * L.hgs):
        for slot in range(len(L.tiles) + 1):
            steps += beside(L, u // L.hgs, u % L.hgs, slot)
    fills = []
    for name, i, M, b in steps + tail_of(L):
        if name == "turn":
            fills.append(("context", M.p, b, 0))
        elif name == "values":
            fills.append(("context", M.p, b, i + (1 if M is CROSS1 else 0)))
        elif name == "out" and b < G - 1:
            fills.append(("out", M.p, b, i))
    return fills


SIDE = {L.p: (USES["pk1"][L.p], side_fills(L)) for L in (SELF0, CROSS1, SELF3, CROSS4)}
for phase, (_, fills) in SIDE.items():
    USES["pk1"][phase] += len(fills)


def side_fill(*what):
    for phase, (first, fills) in SIDE.items():
        if what in fills:
            return nth("pk1", phase, first + fills.index(what))
    raise KeyError(what)


def out_fill(L, b, part):
    if b < G - 1:
        return "pk1", side_fill("out", L.p, b, part)
    parts = 1 if L.relative else 3
    return "pa", nth("pa", L.p, USES["pa"][L.p] - parts + part)


def decoder(nc, a, out):
    with ExitStack() as ctx:
        def sb(name, shape, dt=F32):
            return ctx.enter_context(nc.sbuf_tensor(name, shape, dt))

        def sb_both(name, shape):
            with nc.sbuf_tensor(name, shape, F32) as plain:
                pass
            return plain, sb(name + "_r", shape, F32R)

        def sem(name):
            return ctx.enter_context(nc.semaphore(name))

        wqkv = {0: sb("wqkv0", [128, C, 3 * D]), 3: sb("wqkv3", [128, C, 3 * D])}
        bqk = {0: sb("bqk0", [128, 4]), 3: sb("bqk3", [128, 4])}
        bv = {0: sb("bv0", [T, D]), 3: sb("bv3", [T, D])}
        wq = {1: sb("wq1", [128, C, D]), 4: sb("wq4", [128, C, D])}
        wk = {1: sb("wk1", [CK, 2, D]), 4: sb("wk4", [CK, 2, D])}
        wv = {1: sb("wv1", [CK, 2, D]), 4: sb("wv4", [CK, 2, D])}
        wo = {1: sb("wo1", [128, C, D]), 3: sb("wo3", [128, C, D]), 4: sb("wo4", [128, C, D])}
        bo3 = sb("bo3", [T, D])
        lat_gb = sb("lat_gb", [128, 4])
        in_gb = sb("in_gb", [CK, 4])
        u1, v1 = sb("u1", [128, C, 128]), sb("v1", [128, FF])
        u2, v2 = sb("u2", [128, FF // 128, 128]), sb("v2", [128, D])
        b1c, one64 = sb("b1c", [128, FF // 128]), sb("one64", [128, 1])
        rw, rb = sb("rw", [128, C, E]), sb("rb", [T, E])
        rank8 = sb("rank8", [T, E])
        sele = sb("sele", [128, E, 128])
        ident = sb("ident", [128, 128])
        identb = sb("identb", [128, 128], BF16)
        mask16, mask32 = sb("mask16", [128, 8]), sb("mask32", [128, 4])
        negones = sb("negones", [T, 128], BF16)
        ones32 = sb("ones32", [128, 32])
        neghalf = sb("neghalf", [128, 4])
        alibi = sb("alibi", [T, 16, T], BF16)
        wstack = sb("wstack", [NSTACK + 3, NR], BF16)
        rowmask = sb("rowmask", [T, B * S], U8)
        colmask = sb("colmask", [128, 3, B], U8)
        experts, experts_r = sb_both("experts", [128, WSLOTS, 2048])

        x = sb("x", [T, G, D])
        z = sb("z", [T, G, D])
        xT = sb("xT", [128, C, GT])
        qT = sb("qT", [128, C, GT])
        kT = sb("kT", [128, C, GT])
        kTb = sb("kTb", [128, C, GT], BF16)
        v16 = sb("v16", [T, G, 16, 32])
        qbd, qbd_r = sb_both("qbd", [128, 2, 16 * T])
        qbdb = sb("qbdb", [128, 2, 16 * T + HALO], BF16)
        shift = sb("shift", [T, 2, 16])
        dshift = sb("dshift", [T, 4, 4 * T], BF16)
        pT = sb("pT", [128, 3, 3, 4 * T])
        oT = sb("oT", [128, 4, T])
        rec = sb("rec", [T, 16])
        o = sb("o", [T, D])
        onT = sb("onT", [128, C, T])
        y = sb("y", [T, 2, D])
        bn6, bn6_cx = sb("bn6", [128, 4, 6]), sb("bn6_cx", [128, 3, 6])
        mv = sb("mv", [128, 4, 3, 2])
        vare = sb("vare", [128, 4, 3])
        rstd = sb("rstd", [128, 4, 3])
        UNION = 51200
        union, union_r = sb_both("union", [128, UNION // 4])

        def region(start, parts, shape, dt):
            size, n = (2 if dt == BF16 else 4), 1
            for s in shape:
                n *= s
            assert start % 4 == 0 and start + n * size <= UNION
            v = (union_r if dt == F32R else union)[0:parts, start // 4:(start + n * size) // 4]
            if dt == BF16:
                v = v.bitcast(dt)
            if len(shape) > 1:
                names = "abcd"[:len(shape)]
                v = v.rearrange(f"p ({' '.join(names)}) -> p {' '.join(names)}",
                                **{k: s for k, s in zip(names, shape)})
            return v

        pos = region(0, T, [16 * G, T], F32)
        qstack = region(25600, NSTACK + 3, [16, GT], BF16)
        s0 = qbd[0:T].rearrange("p s (h t) -> p s h t", h=16)
        k_rest = region(0, 128, [C, S], F32)
        k_low = region(2888, 128, [2, C, S], BF16)
        q4stack = qbd[:].rearrange("p s n -> p (s n)").bitcast(BF16).rearrange("p (h t) -> p h t", h=16)
        k4stack = experts[:].rearrange("p s n -> p (s n)").bitcast(BF16)[:, 0:2 * 16 * (S + 1)].rearrange("p (s h k) -> p s h k", s=2, h=16)
        k0stack = experts[:].rearrange("p s n -> p (s n)").bitcast(BF16)[:, 0:16 * GT].rearrange("p (h t) -> p h t", h=16)
        kxT = region(0, 128, [2, C, S], F32)
        kxTb = region(5776, 128, [2, C, S + 1], BF16)
        vx = region(8672, 128, [2, 3, 512], F32)
        cT = region(20960, CK, [2, 2, S], F32)
        cx = region(42496, 128, [2, 3, DC], F32)
        rowbias = region(26736, T, [2, S], F32)
        colbias = region(29624, 128, [2, 4], F32)
        hid = region(29696, 128, [8, GT], F32)
        ptok = region(0, 128, [GT], F32)
        qtok = region(1600, 128, [GT], F32)
        comb = region(0, T, [12, G, E], F32)
        ctop = region(1536, 128, [GT], F32)
        yT = region(3200, 128, [C, GT], F32)
        wh_slots = [region(6400, 128, [2, 1024], F32R), region(14592, 128, [2, 1024], F32R),
                    qbd_r[:].rearrange("p s n -> p (s n)")[:, 0:2048].rearrange("p (a n) -> p a n", a=2)]
        x_parts = region(22784, 128, [2, C, GT], F32R)
        hid_hi = region(36096, 128, [4, GT], F32R)
        hid_lo = region(29696, 128, [4, GT], F32R)

        masked = region(29696, T, [DEPTH["pa"], S], F32)
        pieces = pT[:, 0].rearrange("p a n -> p (a n)").bitcast(BF16).rearrange("p (s c t) -> p s c t", s=3, c=C)
        rest = pT[:, 1, 0:C, :]
        k0_pieces = pT[:, 2].rearrange("p a n -> p (a n)").bitcast(BF16).rearrange("p (s c t) -> p s c t", s=3, c=C)
        k0_dram = nc.dram_tensor("k0_pieces", (3, D, GT), BF16).ap()
        kp_dram = nc.dram_tensor("k_pieces", (2, 3, D, S), BF16).ap()
        qp_dram = nc.dram_tensor("q_pieces", (3, D, GT), BF16).ap()

        banks = {r: [ctx.enter_context(nc.psum_tensor(f"{r}_{i}", [128, 512], F32)) for i in range(n)]
                 for r, n in DEPTH.items()}

        def bank(ring, n):
            return banks[ring][(n - 1) % DEPTH[ring]]

        w_const, w_self0, w_cross1 = sem("w_const"), sem("w_self0"), sem("w_cross1")
        w_ffn, w_self3, w_cross4, w_router = sem("w_ffn"), sem("w_self3"), sem("w_cross4"), sem("w_router")
        made = sem("made")
        x_in, y_out = sem("x_in"), sem("y_out")
        group_sems = []

        def gsem(name):
            s = sem(name)
            group_sems.append(s)
            return s

        full = {r: gsem(f"{r}_full") for r in DEPTH}
        done = {r: gsem(f"{r}_done") for r in DEPTH}
        pv_done = gsem("pv_done")
        cx_in = [gsem("cx_in0"), gsem("cx_in1")]
        cT_in = [gsem("cT_in0"), gsem("cT_in1")]
        pieces_out, qstack_in = gsem("pieces_out"), gsem("qstack_in")
        half_in = [gsem(f"half_in{i}") for i in range(2 * WSLOTS)]
        down_used = gsem("down_used")
        half_hi, half_lo = gsem("half_hi"), gsem("half_lo")
        x_hi, x_lo = gsem("x_hi"), gsem("x_lo")
        hid_hi_made = gsem("hid_hi_made")
        hid_lo_made = gsem("hid_lo_made")
        pieces_made = gsem("pieces_made")
        q_high, q_mid = gsem("q_high"), gsem("q_mid")
        q_rest = gsem("q_rest")
        k0_made, k0_out, k0_in = gsem("k0_made"), gsem("k0_out"), gsem("k0_in")
        k_high, k_mid = gsem("k_high"), gsem("k_mid")
        k_split = gsem("k_split")
        k_out, k4_in = gsem("k_out"), [gsem("k4_in0"), gsem("k4_in1")]
        q4_in = [gsem("q4_in0"), gsem("q4_in1")]
        kTb_made = gsem("kTb_made")
        qbdb_made = gsem("qbdb_made")
        qbd_made = gsem("qbd_made")
        dshift_made = gsem("dshift_made")
        var_made = gsem("var_made")
        rstd_made = gsem("rstd_made")
        ln_done = gsem("ln_done")
        z_made = gsem("z_made")
        cz_made = gsem("cz_made")
        bias_made = gsem("bias_made")
        gated = gsem("gated")
        logit_made, exp_made = gsem("logit_made"), gsem("exp_made")
        comb_made = gsem("comb_made")
        vx_ones = gsem("vx_ones")
        dve_step, pool_step = gsem("dve_step"), gsem("pool_step")

        LN = {"S0": 0, "C1": 4, "F2": 8, "S3": 12, "C4": 16, "M5": 20}
        asked = [("S0", 0), ("z", 0), ("S0", 1), ("cx", 0), ("z", 1), ("S0", 2), ("cx", 1), ("z", 2), ("S0", 3), ("z", 3)]
        asked += [("cx", 2), ("cx", 3)] + [("C1", b) for b in range(G)]
        for ph in ("F2", "S3", "C4", "M5"):
            asked += [(ph, b) for b in range(G)]
        ASK = {k: i for i, k in enumerate(asked)}
        QBD = {"C1": 0, "S3": 4}
        QBDB = {"C1": 0, "S3": 8, "C4": 16}
        KTB = {"C1": 0, "S3": 4}

        def hg_of(L, b, hg):
            return {"S0": 0, "C1": 16, "S3": 24, "C4": 40}[L.p] + b * L.hgs + hg

        s0_fills = [("content", 0), ("content", 1), ("content", 2), ("rows", 0), ("rows", 1)]
        for u in range(4 * G):
            s0_fills += [("content", u + 3)] if u + 3 < 4 * G else []
            s0_fills += [("rows", u + 2)] if u + 2 < 4 * G else []

        def pa_content(b, hg):
            return nth("pa", "S0", G + 7 + s0_fills.index(("content", 4 * b + hg)))

        def pa_max(L, b, i):
            if L.p == "S0":
                return nth("pa", "S0", G + 7 + s0_fills.index(("rows", 4 * b + i)))
            return nth("pa", L.p, G + 4 * b + i if L.p == "S3" else L.heads * b + i)

        def pb_exp(L, b, hg, jt):
            n = len(L.tiles)
            return nth("pb", L.p, (6 if L.p == "S0" else 0) + (b * L.hgs + hg) * n + jt)

        def q_fill(L, c):
            ring = ("pk0", "pk1")[c]
            return ring, nth(ring, L.p, 0)

        def k_fill(L, c):
            return nth("pk0", L.p, 1 + c)

        def v_fill(L, b):
            return nth("pa", L.p, b)

        def q_operands(L, b, c, dst):
            per = L.heads // C
            m = mask16 if per == 8 else mask32
            return (dst[:, b % 2, c * per * T:(c + 1) * per * T].rearrange("p (h t) -> p h t", h=per),
                    qT[:, c, b * T:(b + 1) * T].unsqueeze(1).broadcast_to([128, per, T]), m[:].unsqueeze(2).broadcast_to([128, per, T]))

        def half(k):
            return experts[:, k // 2 % WSLOTS, k % 2 * 1024:(k % 2 + 1) * 1024]

        def wait_half_used(engine, k):
            e = k // 2
            if k % 2:
                engine.wait_ge(down_used, e + 1)
            else:
                engine.wait_ge(full["pb"], nth("pb", "M5", e * FC + FC - 1))

        def half_parts(k):
            return wh_slots[k // 2 % WSLOTS][:, k % 2, :], experts_r[:, k // 2 % WSLOTS, k % 2 * 1024:(k % 2 + 1) * 1024]

        def kv_fill(L, b, ring, i):
            if ring == "pk1":
                return side_fill("context", L.p, b, i)
            per = USES[ring][L.pre] // L.early
            if b < L.early:
                return nth(ring, L.pre, b * per + i)
            return nth(ring, L.p, 1 + (b - L.early) * per + i)

        def last_values(L, b):
            return kv_fill(L, b, "pk1", 3 if L is CROSS1 else 2)

        with nc.Block() as block:
            @block.sync
            def _(sync):
                sync.dma_start(z[:], a["x"][0:G].rearrange("b t d -> t b d")).then_inc(x_in, 16)
                sync.dma_start(ident[:], a["ident"]).then_inc(w_const, 16)
                sync.dma_start(wqkv[0][:], a["wqkv0"]).then_inc(w_self0, 16)
                sync.dma_start(bqk[0][:], a["bqk0"]).then_inc(w_self0, 16)
                sync.dma_start(bv[0][:], a["bv0"].partition_broadcast(T)).then_inc(w_self0, 16)
                sync.dma_start(union[0:NSTACK + 3, 0:NR], a["wr_stack"]).then_inc(w_const, 16)
                sync.dma_start(union[0:NSTACK + 3, 300:303], a["w_pick"]).then_inc(w_const, 16)
                for t, n in ((mask16, "mask16"), (mask32, "mask32"), (one64, "one64"), (neghalf, "neghalf"), (rank8, "rank8")):
                    sync.dma_start(t[:], a[n]).then_inc(w_const, 16)

            @block.scalar
            def _(act):
                act.wait_ge(w_self0, 48)
                for t, n in ((wq[1], "wq1"), (wk[1], "wk1"), (wv[1], "wv1"), (wo[1], "wo1"),
                             (lat_gb, "lat_gb"), (in_gb, "in_gb")):
                    act.dma_start(t[:], a[n]).then_inc(w_cross1, 16)
                for t, n in ((u1, "u1"), (v1, "v1"), (u2, "u2"), (v2, "v2"), (b1c, "b1c")):
                    act.dma_start(t[:], a[n]).then_inc(w_ffn, 16)
                act.dma_start(wqkv[3][:], a["wqkv3"]).then_inc(w_self3, 16)
                act.dma_start(bqk[3][:], a["bqk3"]).then_inc(w_self3, 16)
                act.dma_start(bv[3][:], a["bv3"].partition_broadcast(T)).then_inc(w_self3, 16)
                act.dma_start(bo3[:], a["bo3"].partition_broadcast(T)).then_inc(w_self3, 16)
                act.dma_start(wo[3][:], a["wo3"]).then_inc(w_self3, 16)
                act.dma_start(alibi[:], a["alibi"]).then_inc(w_self3, 16)
                for t, n in ((wq[4], "wq4"), (wk[4], "wk4"), (wv[4], "wv4"), (wo[4], "wo4")):
                    act.dma_start(t[:], a[n]).then_inc(w_cross4, 16)
                act.dma_start(colmask[:, 0:2, :], a["maskT"][0:256, :].rearrange("(j p) b -> p j b", p=128)).then_inc(w_cross4, 16)
                act.dma_start(colmask[0:S - 256, 2, :], a["maskT"][256:S, :]).then_inc(w_cross4, 16)
                act.dma_start(rowmask[:], a["mask"].rearrange("b s -> (b s)").partition_broadcast(T)).then_inc(w_cross4, 16)
                act.dma_start(rw[:], a["rw"]).then_inc(w_router, 16)
                act.dma_start(sele[:], a["sele"]).then_inc(w_router, 16)
                act.dma_start(rb[:], a["rb"].partition_broadcast(T)).then_inc(w_router, 16)

            @block.vector
            def _(dve):
                nc.vector.memset(negones[:], -1.0).then_inc(made, 1)
                nc.vector.memset(rec[:], 1.0).then_inc(y_out, 1)
                nc.vector.memset(ones32[:], 1.0).then_inc(made, 1)
                nc.vector.memset(v16[:], 1.0).then_inc(made, 1)
                nc.vector.memset(qbdb[:], 0.0).then_inc(made, 1)
                nc.vector.memset(mv[:], 1.0).then_inc(made, 1)
                dve.wait_ge(w_const, 128)
                nc.vector.tensor_copy(identb[:], ident[:]).then_inc(made, 1)
                R = NSTACK + 3
                w = union[0:R, 0:NR]
                pick = union[0:R, 300:303]
                hb = union[0:R, 400:400 + 130].bitcast(BF16)[:, 0:NR]
                mb = union[0:R, 600:600 + 130].bitcast(BF16)[:, 0:NR]
                lb = union[0:R, 800:800 + 130].bitcast(BF16)[:, 0:NR]
                r = union[0:R, 1000:1000 + NR]
                r2 = union[0:R, 1300:1300 + NR]
                nc.vector.tensor_copy(hb, w).then_inc(made, 1)
                dve.wait_ge(made, 7)
                nc.vector.tensor_tensor(r, w, hb, ALU.subtract).then_inc(made, 1)
                dve.wait_ge(made, 8)
                nc.vector.tensor_copy(mb, r).then_inc(made, 1)
                dve.wait_ge(made, 9)
                nc.vector.tensor_tensor(r2, r, mb, ALU.subtract).then_inc(made, 1)
                dve.wait_ge(made, 10)
                nc.vector.tensor_copy(lb, r2).then_inc(made, 1)
                dve.wait_ge(made, 11)
                nc.vector.tensor_scalar(r, hb, pick[:, 0:1], None, ALU.mult).then_inc(made, 1)
                dve.wait_ge(made, 12)
                nc.vector.scalar_tensor_tensor(out=r2, in0=mb, scalar=pick[:, 1:2], in1=r, op0=ALU.mult, op1=ALU.add).then_inc(made, 1)
                dve.wait_ge(made, 13)
                nc.vector.scalar_tensor_tensor(out=wstack[:], in0=lb, scalar=pick[:, 2:3], in1=r2, op0=ALU.mult, op1=ALU.add).then_inc(made, 1)
                dve.wait_ge(made, 14)

        with nc.Fori(0, B // G, 1) as g:
            with nc.Block() as block:

                @block.sync
                def _(sync):
                    def load_cT(b):
                        src = a["ctxT"][bass.ds(g * G + b, 1)].rearrange("a d s -> (a d) s")
                        sync.dma_start(cT[:, b % 2, :, :], src.rearrange("(k p) s -> p k s", p=CK)).then_inc(cT_in[b % 2], 16)

                    for c in range(C):
                        sync.wait_ge(pieces_made, c + 1)
                        sync.dma_start(qp_dram[:, c * 128:(c + 1) * 128, :].rearrange("s p t -> p s t"), pieces[:, :, c, :]).then_inc(pieces_out, 16)
                    sync.wait_ge(pieces_out, 16 * C)
                    for s, piece in enumerate(PIECES):
                        sync.dma_start(qstack[16 * s:16 * s + 16], qp_dram[piece].rearrange("(h d) t -> d h t", d=16)).then_inc(qstack_in, 16)
                    sync.wait_ge(k0_made, C)
                    sync.dma_start(k0_dram.rearrange("s (c p) t -> p s c t", p=128), k0_pieces[:]).then_inc(k0_out, 16)
                    sync.wait_ge(k0_out, 16)
                    for s, piece in enumerate(WPIECES):
                        sync.dma_start(k0stack[16 * s:16 * s + 16], k0_dram[piece].rearrange("(h d) t -> d h t", d=16)).then_inc(k0_in, 16)
                    for b in range(G):
                        if b < 2:
                            sync.wait_ge(full["pa"], nth("pa", "S0", G + 6))
                        else:
                            sync.wait_ge(full["pk1"], kv_fill(CROSS1, b - 2, "pk1", 0))
                            sync.wait_ge(full["pk0"], kv_fill(CROSS1, b - 2, "pk0", 0))
                        src = a["ctx"][bass.ds(g * G + b, 1)].rearrange("a s d -> (a s) d")
                        sync.dma_start(cx[:, b % 2, 0:2, :], src[0:256, :].rearrange("(j p) d -> p j d", p=128)).then_inc(cx_in[b % 2], 16)
                        sync.dma_start(cx[0:S - 256, b % 2, 2, :], src[256:S, :]).then_inc(cx_in[b % 2], 16)
                    sync.wait_ge(full["pk0"], nth("pk0", "X1", 0))
                    sync.wait_ge(full["pk1"], nth("pk1", "X1", 0))
                    sync.dma_start(z[:], a["x"][bass.ds((g + 1) % (B // G) * G, G)].rearrange("b t d -> t b d")).then_inc(x_in, 16)
                    for b in range(2):
                        sync.wait_ge(full["pk1"], last_values(CROSS1, b + 2))
                        load_cT(b)
                    for b in range(G):
                        sync.wait_ge(k_split, 2 * b + 2)
                        sync.dma_start(kp_dram[b % 2, 0].rearrange("(c p) k -> p c k", p=128), kxTb[:, b % 2, :, 0:S]).then_inc(k_out, 16)
                        for i in range(2):
                            sync.dma_start(kp_dram[b % 2, 1 + i].rearrange("(c p) k -> p c k", p=128), k_low[:, i]).then_inc(k_out, 16)
                        sync.wait_ge(k_out, 48 * (b + 1))
                        if b > 1:
                            sync.wait_ge(full["pb"], pb_exp(CROSS4, b - 2, 3, 2))
                        for s, piece in enumerate(WPIECES):
                            sync.dma_start(k4stack[16 * s:16 * s + 16, b % 2, :, 0:S], kp_dram[b % 2, piece].rearrange("(h d) k -> d h k", d=16)).then_inc(k4_in[b % 2], 16)
                        if b < 2:
                            sync.wait_ge(full["pk1"], kv_fill(CROSS4, b, "pk1", 2))
                            load_cT(b + 2)
                        if b == 1:
                            sync.wait_ge(pieces_made, C + 1)
                            sync.wait_ge(qstack_in, 16 * len(PIECES))
                            sync.dma_start(qp_dram.rearrange("s (c p) t -> p s c t", p=128), pieces[:]).then_inc(pieces_out, 16)
                            sync.wait_ge(pieces_out, 16 * C + 16)
                            for part, (t0, t1) in enumerate(((0, T), (T, GT))):
                                for s, piece in enumerate(PIECES):
                                    sync.dma_start(q4stack[16 * s:16 * s + 16, :, t0:t1], qp_dram[piece].rearrange("(h d) t -> d h t", d=16)[:, :, t0:t1]).then_inc(q4_in[part], 16)
                    sync.wait_ge(full["pb"], pb_exp(CROSS4, G - 1, 3, 2))
                    for k in range(2 * WSLOTS):
                        sync.dma_start(half(k), a["experts"][k // 2][:, k % 2 * 1024:(k % 2 + 1) * 1024]).then_inc(half_in[k], 16)
                    for k in range(2 * WSLOTS, 2 * NE):
                        wait_half_used(sync, k - 2 * WSLOTS)
                        sync.dma_start(half(k), a["experts"][k // 2][:, k % 2 * 1024:(k % 2 + 1) * 1024]).then_inc(half_in[k % (2 * WSLOTS)], 16)
                    for b in range(G):
                        sync.wait_ge(ln_done, LN["M5"] + b + 1)
                        sync.dma_start(out[bass.ds(g * G + b, 1)].rearrange("a t d -> (a t) d"), x[:, b, :]).then_inc(y_out, 16)

                @block.tensor
                def _(pe):
                    mm = nc.tensor.matmul

                    def claim(ring, n):
                        if n > DEPTH[ring]:
                            pe.wait_ge(done[ring], n - DEPTH[ring])
                        return bank(ring, n)

                    def transpose_x(ph, src, ready, counts, batches):
                        for b in batches:
                            pe.wait_ge(ready, counts[b])
                            for c, ring in enumerate(("pk0", "pk1")):
                                n = nth(ring, ph, 0)
                                p = claim(ring, n) if b == 0 else bank(ring, n)
                                last = nc.tensor.transpose(p[:, b * T:(b + 1) * T], src[:, b, c * 128:(c + 1) * 128], ident[0:T, 0:T])
                                if b == G - 1:
                                    last.then_inc(full[ring], 1)

                    def wait_xT(ph):
                        pe.wait_ge(done["pk0"], nth("pk0", ph, 0))
                        pe.wait_ge(done["pk1"], nth("pk1", ph, 0))

                    def project_T(ring, n, w, col):
                        p = claim(ring, n)
                        for k in range(C):
                            last = mm(p[:, 0:GT], w[:, k, col:col + 128], xT[:, k, :], start=(k == 0), stop=(k == C - 1))
                        last.then_inc(full[ring], 1)

                    def self_project(li, L):
                        for c in range(C):
                            project_T(*q_fill(L, c), wqkv[li], 128 * c)
                        for c in range(C):
                            project_T("pk0", k_fill(L, c), wqkv[li], 128 * (C + c))
                        for i in range(G):
                            n = v_fill(L, i)
                            p = claim("pa", n)
                            for k in range(C):
                                last = mm(p[0:T, 0:D], xT[:, k, i * T:(i + 1) * T], wqkv[li][:, k, 2 * D:3 * D], start=(k == 0), stop=(k == C - 1))
                            last.then_inc(full["pa"], 1)

                    def positions():
                        pe.wait_ge(qstack_in, 16 * len(PIECES))
                        pe.wait_ge(pool_step, 1)
                        for k in range(13):
                            ring = "pa" if k % 2 == 0 else "pb"
                            n = nth(ring, "S0", k // 2 + (G if ring == "pa" else 0))
                            p = claim(ring, n)
                            for i in range(8 * k, min(8 * k + 8, T)):
                                u = i - 8 * k
                                rhs = qstack.rearrange("r h (b t) -> r h b t", b=G)[:, :, :, i]
                                last = mm(p[:, 64 * u:64 * u + 64], wstack[:, REL0 - i:REL0 - i + 128], rhs, start=True, stop=True)
                            last.then_inc(full[ring], 1)

                    def turn(L, b):
                        s = b % 2
                        pe.wait_ge(cz_made, b + 1)
                        for c, ring in enumerate(("pk0", "pk1")):
                            n = kv_fill(L, b, ring, 0)
                            p = claim(ring, n)
                            for j, (j0, J) in enumerate(JT):
                                last = nc.tensor.transpose(p[0:CK, j0:j0 + J], cx[0:J, s, j, c * CK:(c + 1) * CK], ident[0:J, 0:J])
                            last.then_inc(full[ring], 1)

                    def wait_context(L, b):
                        if L is CROSS1:
                            pe.wait_ge(done["pk0"], kv_fill(L, b, "pk0", 0))
                            pe.wait_ge(done["pk1"], kv_fill(L, b, "pk1", 0))
                        else:
                            pe.wait_ge(w_cross4, 112)
                            pe.wait_ge(cT_in[b % 2], 16 * (b // 2 + 1))

                    def keys(L, b, i):
                        wk_l = wk[1] if L is CROSS1 else wk[4]
                        if i == 0:
                            wait_context(L, b)
                        n = kv_fill(L, b, "pk0", (1 if L is CROSS1 else 0) + i)
                        p = claim("pk0", n)
                        for k in range(2):
                            last = mm(p[:, 0:S], wk_l[:, k, i * 128:(i + 1) * 128], cT[:, b % 2, k, :], start=(k == 0), stop=(k == 1))
                        last.then_inc(full["pk0"], 1)

                    def values(L, b, i):
                        wv_l = wv[1] if L is CROSS1 else wv[4]
                        n = kv_fill(L, b, "pk1", (1 if L is CROSS1 else 0) + i)
                        p = claim("pk1", n)
                        j0, J = JT[i]
                        for k in range(2):
                            last = mm(p[0:J, 0:D], cT[:, b % 2, k, j0:j0 + J], wv_l[:, k, :], start=(k == 0), stop=(k == 1))
                        last.then_inc(full["pk1"], 1)

                    def q_chunks(L, h):
                        return min(C, (h + 1) // (L.heads // C) + 1)

                    def content(b, hg):
                        p = claim("pa", pa_content(b, hg))
                        for u in range(4):
                            h = 4 * hg + u
                            last = mm(p[0:T, u * T:(u + 1) * T], k0stack[0:NSTACK, h, b * T:(b + 1) * T], qstack[0:NSTACK, h, b * T:(b + 1) * T], start=True, stop=True)
                        last.then_inc(full["pa"], 1)

                    def rows(L, b, hg):
                        s = b % 2
                        if L.relative:
                            pe.wait_ge(done["pa"], pa_content(b, hg))
                            p = claim("pa", pa_max(L, b, hg))
                            for h in range(4):
                                last = nc.tensor.transpose(p[0:T, h * T:(h + 1) * T], s0[:, s, 4 * hg + h, :], ident[0:T, 0:T])
                            last.then_inc(full["pa"], 1)
                            return
                        pe.wait_ge(kTb_made, KTB[L.p] + 1)
                        pe.wait_ge(qbdb_made, QBDB[L.p] + 2 * b + q_chunks(L, 4 * hg + 3))
                        p = claim("pa", pa_max(L, b, hg))
                        mm(p[:, 0:4 * T], identb[0:T, :], alibi[:, 4 * hg:4 * hg + 4, :].rearrange("p h t -> p (h t)"), start=True, stop=True)
                        for u in range(4):
                            h = 4 * hg + u
                            last = mm(p[:, u * T:(u + 1) * T], qbdb[:, s, h * T:h * T + 128], kTb[:, h // 8, b * T:(b + 1) * T],
                                      start=False, stop=True, skip_group_check=True)
                        last.then_inc(full["pa"], 1)

                    def head(L, b, h):
                        if L is CROSS4:
                            pe.wait_ge(k_high, 2 * b + 2)
                        else:
                            pe.wait_ge(kTb_made, KTB[L.p] + b + 1)
                        pe.wait_ge(qbdb_made, QBDB[L.p] + 2 * b + q_chunks(L, h))
                        mm(claim("pa", pa_max(L, b, h))[:, 0:S], qbdb[:, b % 2, h * T:h * T + 128], kxTb[:, b % 2, h // (L.heads // C), 0:S],
                           start=True, stop=True).then_inc(full["pa"], 1)

                    def exp_scores(L, b, hg, j):
                        s, d = b % 2, hg_of(L, b, hg)
                        if L in (CROSS1, SELF3):
                            pe.wait_ge(qbd_made, QBD[L.p] + b + 1)
                        j0, J = L.tiles[j]
                        p = claim("pb", pb_exp(L, b, hg, j))[0:J, 0:4 * T]
                        if L.relative:
                            mm(p, ident[0:T, 0:T], s0[:, s, 4 * hg:4 * hg + 4, :].rearrange("p h t -> p (h t)"), start=True, stop=False)
                        elif L is CROSS4:
                            if hg == 0 and j == 0:
                                pe.wait_ge(k4_in[s], 16 * len(PIECES) * (b // 2 + 1))
                                if b < 2:
                                    pe.wait_ge(q4_in[b], 16 * len(PIECES))
                            if j == 0:
                                pe.wait_ge(dshift_made, d + 1)
                            mm(p, negones[:, 0:J], dshift[:, d % 4, :], start=True, stop=True)
                            for u in range(4):
                                h = 4 * hg + u
                                last = mm(p[:, u * T:(u + 1) * T], k4stack[0:NSTACK, s, h, j0:j0 + J], q4stack[0:NSTACK, h, b * T:(b + 1) * T],
                                          start=False, stop=True, skip_group_check=True)
                            last.then_inc(full["pb"], 1)
                            return
                        else:
                            chunk = 4 * hg // (L.heads // C)
                            k = kT[:, chunk, b * T:(b + 1) * T] if isinstance(L, Self) else kxT[:, s, chunk, j0:j0 + J]
                            mm(p, k, qbd[:, s, hg * 4 * T:(hg + 1) * 4 * T], start=True, stop=False)
                            if isinstance(L, Self):
                                mm(p, identb[0:T, 0:T], alibi[:, 4 * hg:4 * hg + 4, :].rearrange("p h t -> p (h t)"), start=False, stop=False)
                        if j == 0:
                            pe.wait_ge(dshift_made, d + 1)
                        mm(p, negones[:, 0:J], dshift[:, d % 4, :], start=False, stop=True).then_inc(full["pb"], 1)

                    def times_v(L, b, hg, j):
                        d = hg_of(L, b, hg)
                        slot, p = d % 3, bank("po", 1)
                        if hg == 0 and j == 0:
                            n = nth("po", L.p, b)
                            if n > 1:
                                pe.wait_ge(done["po"], n - 1)
                            if isinstance(L, Self):
                                pe.wait_ge(done["pa"], v_fill(L, G - 1))
                            else:
                                pe.wait_ge(done["pk1"], last_values(L, b))
                        J, last_tile = L.tiles[j][1], len(L.tiles) - 1
                        pe.wait_ge(done["pb"], pb_exp(L, b, hg, j))
                        for u in range(4):
                            h = 4 * hg + u
                            if isinstance(L, Self):
                                v = v16[:, b, h, :]
                            else:
                                v = vx[0:J, b % 2, j, 32 * h:32 * h + 32]
                            last = mm(p[32 * u:32 * u + 32, hg * T:(hg + 1) * T], v, pT[0:J, slot, j, u * T:(u + 1) * T],
                                      start=(j == 0), stop=(j == last_tile), skip_group_check=True)
                        if L is CROSS1:
                            for u in range(4):
                                last = mm(p[32 * u:32 * u + 32, (2 + hg) * T:(3 + hg) * T], ones32[0:J, :], pT[0:J, slot, j, u * T:(u + 1) * T],
                                          start=False, stop=(j == last_tile), skip_group_check=True)
                        if j == last_tile:
                            last.then_inc(pv_done, 1)

                    def epilogue(L, li, b, part):
                        if part == 0:
                            ring, n = out_fill(L, b, 0)
                            p = claim(ring, n)
                            pe.wait_ge(done["po"], nth("po", L.p, b))
                            for i in range(4):
                                last = nc.tensor.transpose(p[0:T, i * 128:(i + 1) * 128], oT[:, i, :], ident[:, :])
                            last.then_inc(full[ring], 1)
                        elif L.relative:
                            return
                        elif part == 1:
                            ring, n = out_fill(L, b, 1)
                            pe.wait_ge(done[ring], out_fill(L, b, 0)[1])
                            p = claim(ring, n)
                            for c in range(C):
                                last = nc.tensor.transpose(p[:, c * T:(c + 1) * T], o[:, c * 128:(c + 1) * 128], ident[0:T, 0:T])
                            last.then_inc(full[ring], 1)
                        else:
                            ring, n = out_fill(L, b, 2)
                            pe.wait_ge(done[ring], out_fill(L, b, 1)[1])
                            p = claim(ring, n)
                            for c in range(C):
                                last = mm(p[0:T, 0:D], onT[:, c, :], wo[li][:, c, :], start=(c == 0), stop=(c == C - 1))
                            last.then_inc(full[ring], 1)

                    def do(steps, li):
                        for name, i, M, bb in steps:
                            if name == "turn":
                                turn(M, bb)
                            elif name == "keys":
                                keys(M, bb, i)
                            elif name == "values":
                                values(M, bb, i)
                            elif name == "content":
                                content(bb, i)
                            elif name == "rows":
                                rows(M, bb, i)
                            elif name == "head":
                                head(M, bb, i)
                            elif name == "out":
                                epilogue(M, li, bb, i)

                    def attention(L, li, *x_next):
                        if L.relative:
                            pe.wait_ge(k0_in, 16 * len(WPIECES))
                            for hg in range(3):
                                content(0, hg)
                        for hg in range(L.lead):
                            if isinstance(L, Self):
                                rows(L, 0, hg)
                            else:
                                for h in range(4 * hg, 4 * hg + 4):
                                    head(L, 0, h)
                        for u in range(G * L.hgs):
                            b, hg = divmod(u, L.hgs)
                            for j in range(len(L.tiles)):
                                exp_scores(L, b, hg, j)
                                do(beside(L, b, hg, j), li)
                                if u > 0:
                                    times_v(L, (u - 1) // L.hgs, (u - 1) % L.hgs, j)
                            do(beside(L, b, hg, len(L.tiles)), li)
                        for j in range(len(L.tiles)):
                            times_v(L, G - 1, L.hgs - 1, j)
                        do(tail_of(L), li)
                        transpose_x(*x_next, range(G - 1))

                    def three_products(parts):
                        return [(0, parts[0]), (1, parts[0]), (0, parts[1])]

                    pe.wait_ge(w_const, 128)
                    pe.wait_ge(w_self0, 48)
                    pe.wait_ge(made, 14)
                    transpose_x("X0", z, x_in, [(g + 1) * 16] * G, range(G))
                    wait_xT("X0")
                    self_project(0, SELF0)
                    positions()
                    pe.wait_ge(w_cross1, 96)
                    attention(SELF0, 0, "X1", z, z_made, [b + 1 for b in range(G)])
                    transpose_x("X1", z, z_made, [b + 1 for b in range(G)], [3])
                    wait_xT("X1")
                    for i in range(C):
                        project_T(*q_fill(CROSS1, i), wq[1], 128 * i)
                    attention(CROSS1, 1, "X2", x, ln_done, [LN["C1"] + b + 1 for b in range(G)])
                    pe.wait_ge(w_ffn, 80)
                    transpose_x("X2", x, ln_done, [LN["C1"] + b + 1 for b in range(G)], [3])
                    wait_xT("X2")
                    project_T("pk0", nth("pk0", "F2", 0), u1, 0)
                    pe.wait_ge(done["pk0"], nth("pk0", "F2", 0))
                    NF = FF // 128
                    n_po = nth("po", "F2", 0)
                    for i in range(NF + LAG):
                        if i < NF:
                            n = nth("pb", "F2", i)
                            mm(claim("pb", n)[:, 0:GT], v1[:, i * 128:(i + 1) * 128], ptok, start=True, stop=True).then_inc(full["pb"], 1)
                        if i >= LAG:
                            f = i - LAG
                            if f == 0:
                                claim("po", n_po)
                            pe.wait_ge(done["pb"], nth("pb", "F2", f))
                            last = mm(bank("po", 1)[:, 0:GT], u2[:, f, :], hid[:, f, :], start=(f == 0), stop=(f == NF - 1))
                    last.then_inc(full["po"], 1)
                    pe.wait_ge(done["po"], n_po)
                    for b in range(G):
                        p = claim("pa", nth("pa", "F2", b))
                        mm(p[0:T, 0:D], qtok[:, b * T:(b + 1) * T], v2[:], start=True, stop=True).then_inc(full["pa"], 1)
                    pe.wait_ge(w_self3, 96)
                    transpose_x("X3", x, ln_done, [LN["F2"] + b + 1 for b in range(G)], range(G))
                    wait_xT("X3")
                    self_project(3, SELF3)
                    attention(SELF3, 3, "X4", x, ln_done, [LN["S3"] + b + 1 for b in range(G)])
                    transpose_x("X4", x, ln_done, [LN["S3"] + b + 1 for b in range(G)], [3])
                    wait_xT("X4")
                    for i in range(C):
                        project_T(*q_fill(CROSS4, i), wq[4], 128 * i)
                    attention(CROSS4, 4, "X5", x, ln_done, [LN["C4"] + b + 1 for b in range(G)])
                    pe.wait_ge(w_router, 48)
                    transpose_x("X5", x, ln_done, [LN["C4"] + b + 1 for b in range(G)], [3])
                    wait_xT("X5")
                    n = nth("pa", "M5", 0)
                    p = claim("pa", n)
                    for b in range(G):
                        for k in range(C):
                            last = mm(p[0:T, b * E:(b + 1) * E], xT[:, k, b * T:(b + 1) * T], rw[:, k, :], start=(k == 0), stop=(k == C - 1))
                    last.then_inc(full["pa"], 1)
                    pe.wait_ge(x_lo, 1)
                    yb = [claim("pa", nth("pa", "M5", 1 + i)) for i in range(C)]
                    chunks = NE * FC
                    for i in range(chunks + LAG):
                        if i < chunks:
                            e, f = divmod(i, FC)
                            if f == 0:
                                pe.wait_ge(half_lo, 2 * e + 1)
                            p = claim("pb", nth("pb", "M5", i))
                            steps = [(w.rearrange("p (c f) -> p c f", c=C)[:, c, f * 128:(f + 1) * 128], x_parts[:, x, c, :])
                                     for x, w in three_products(half_parts(2 * e)) for c in range(C)]
                            for k, (w, xs) in enumerate(steps):
                                last = mm(p[:, 0:GT], w, xs, start=(k == 0), stop=(k == len(steps) - 1))
                            last.then_inc(full["pb"], 1)
                        if i >= LAG:
                            u = i - LAG
                            e, f = divmod(u, FC)
                            pe.wait_ge(hid_lo_made, u + 1)
                            if f == 0:
                                pe.wait_ge(half_lo, 2 * e + 2)
                            h_parts = [hid_hi[:, u % 4, :], hid_lo[:, u % 4, :]]
                            steps = [(w.rearrange("p (f d) -> p f d", f=FC)[:, f, :], h_parts[x]) for x, w in three_products(half_parts(2 * e + 1))]
                            for k, (w, hs) in enumerate(steps):
                                for c in range(C):
                                    last = mm(yb[c][:, 0:GT], w[:, c * 128:(c + 1) * 128], hs, start=(u == 0 and k == 0), stop=(u == chunks - 1 and k == 2))
                                    if u == chunks - 1 and k == 2:
                                        last.then_inc(full["pa"], 1)
                            if f == FC - 1 and e + WSLOTS < NE:
                                last.then_inc(down_used, 1)
                        if i == FC:
                            pe.wait_ge(comb_made, 1)
                            p = claim("pk0", nth("pk0", "M5", 0))
                            for b in range(G):
                                last = nc.tensor.transpose(p[0:E, b * T:(b + 1) * T], comb[:, 11, b, :], ident[0:T, 0:T])
                            last.then_inc(full["pk0"], 1)
                            pe.wait_ge(done["pk0"], nth("pk0", "M5", 0))
                        if i % FC == 0 and 0 < i < chunks:
                            e = i // FC - 1
                            if e > 0:
                                pe.wait_ge(gated, FC * e)
                            else:
                                pe.wait_ge(done["pk1"], nth("pk1", "X5", 0))
                            mm(bank("pk1", 1)[:, 0:GT], sele[:, e, :], ctop, start=True, stop=True).then_inc(full["pk1"], 1)
                    for i in range(C):
                        pe.wait_ge(done["pa"], nth("pa", "M5", 1 + i))
                    for b in range(G):
                        p = claim("pa", nth("pa", "M5", 1 + C + b))
                        for c in range(C):
                            last = nc.tensor.transpose(p[0:T, c * 128:(c + 1) * 128], yT[:, c, b * T:(b + 1) * T], ident[:, :])
                        last.then_inc(full["pa"], 1)

                @block.scalar
                def _(act):
                    fn = nc.scalar.activation

                    def copy_xT(ph):
                        n = nth("pk0", ph, 0)
                        act.wait_ge(full["pk0"], n)
                        fn(xT[:, 0, :], bank("pk0", n)[:, 0:GT], ACT.Copy).then_inc(done["pk0"], 1)

                    def project_q(L):
                        for c in range(C):
                            ring, n = q_fill(L, c)
                            act.wait_ge(full[ring], n)
                            if L is CROSS4:
                                fn(pieces[:, 0, c, :], bank(ring, n)[:, 0:GT], ACT.Copy).then_inc(q_high, 1)
                            fn(qT[:, c, :], bank(ring, n)[:, 0:GT], ACT.Copy).then_inc(done[ring], 1)
                        if L is CROSS4:
                            act.wait_ge(q_rest, 1)
                            fn(pieces[:, 1], rest[:], ACT.Copy).then_inc(q_mid, 1)

                    def self_project(li, L):
                        for i in range(2 * C):
                            ring, n = q_fill(L, i) if i < C else ("pk0", k_fill(L, i - C))
                            act.wait_ge(full[ring], n)
                            dst = (qT if i < C else kT)[:, i % C, :]
                            fn(dst, bank(ring, n)[:, 0:GT], ACT.Identity, bias=bqk[li][:, i:i + 1]).then_inc(done[ring], 1)

                    def do(steps):
                        for name, i, M, bb in steps:
                            if name == "turn":
                                n = kv_fill(M, bb, "pk0", 0)
                                act.wait_ge(full["pk0"], n)
                                fn(cT[:, bb % 2, 0, :], bank("pk0", n)[0:CK, 0:S], ACT.Identity, bias=in_gb[:, 2:3], scale=in_gb[:, 0:1]).then_inc(done["pk0"], 1)
                            elif name == "keys" and M is CROSS4:
                                n = kv_fill(M, bb, "pk0", i)
                                act.wait_ge(full["pk0"], n)
                                if i == 0 and bb > 0:
                                    act.wait_ge(k_out, 48 * bb)
                                fn(kxTb[:, bb % 2, i, 0:S], bank("pk0", n)[:, 0:S], ACT.Copy).then_inc(k_high, 1)
                            elif name == "values":
                                J = JT[i][1]
                                n = kv_fill(M, bb, "pk1", (1 if M is CROSS1 else 0) + i)
                                act.wait_ge(full["pk1"], n)
                                src = bank("pk1", n)[0:J, 0:D]
                                if M is CROSS1:
                                    fn(vx[0:J, bb % 2, i, 0:D], src, ACT.Copy).then_inc(done["pk1"], 1)
                                else:
                                    act.wait_ge(vx_ones, 1)
                                    fn(vx[0:J, bb % 2, i, :].rearrange("p (h d) -> p h d", h=16)[:, :, 0:16], src.rearrange("p (h d) -> p h d", h=16),
                                       ACT.Copy).then_inc(done["pk1"], 1)
                            elif name == "split":
                                act.wait_ge(done["pk0"], kv_fill(M, bb, "pk0", i))
                                fn(k_low[:, 0, i, :], k_rest[:, i, :], ACT.Copy).then_inc(k_mid, 1)
                            elif name == "keys":
                                n = kv_fill(M, bb, "pk0", (1 if M is CROSS1 else 0) + i)
                                act.wait_ge(full["pk0"], n)
                                fn(kxT[:, bb % 2, i, :], bank("pk0", n)[:, 0:S], ACT.Copy).then_inc(done["pk0"], 1)

                    def attention(L):
                        for u in range(G * L.hgs):
                            b, hg = divmod(u, L.hgs)
                            d = hg_of(L, b, hg)
                            if d >= 3:
                                act.wait_ge(pv_done, d - 2)
                            for j, (j0, J) in enumerate(L.tiles):
                                n = pb_exp(L, b, hg, j)
                                act.wait_ge(full["pb"], n)
                                src, dst = bank("pb", n)[0:J, 0:4 * T], pT[0:J, d % 3, j, :]
                                scale = 1.0 if L.relative else L.scale
                                if L is CROSS4:
                                    if hg == 0 and j == 0:
                                        act.wait_ge(bias_made, 3 * b + 3)
                                    fn(dst, src, ACT.Exp, bias=colbias[0:J, b % 2, j:j + 1], scale=scale).then_inc(done["pb"], 1)
                                else:
                                    fn(dst, src, ACT.Exp, scale=scale).then_inc(done["pb"], 1)
                                do(beside(L, b, hg, j))
                            if b > 0 and hg == 0:
                                heads_out(L, b - 1)
                            do(beside(L, b, hg, len(L.tiles)))
                        heads_out(L, G - 1)
                        do(tail_of(L))

                    def heads_out(L, b):
                        act.wait_ge(pv_done, hg_of(L, b, L.hgs - 1) + 1)
                        fn(oT[:].rearrange("p h t -> p (h t)"), bank("po", 1)[:, 0:4 * T], ACT.Copy).then_inc(done["po"], 1)

                    def half_high(k):
                        if k >= 2 * WSLOTS:
                            wait_half_used(act, k - 2 * WSLOTS)
                        act.wait_ge(half_in[k % (2 * WSLOTS)], 16 * (k // (2 * WSLOTS) + 1))
                        fn(half_parts(k)[0], half(k), ACT.Copy).then_inc(half_hi, 1)

                    copy_xT("X0")
                    act.wait_ge(w_self0, 48)
                    self_project(0, SELF0)
                    for k in range(1, 13, 2):
                        n = nth("pb", "S0", k // 2)
                        act.wait_ge(full["pb"], n)
                        fn(pos[:, :, 8 * k:8 * k + 8], bank("pb", n)[0:T, :].rearrange("p (i m) -> p m i", i=8), ACT.Copy).then_inc(done["pb"], 1)
                    act.wait_ge(w_cross1, 96)
                    attention(SELF0)
                    n = nth("pk0", "X1", 0)
                    act.wait_ge(full["pk0"], n)
                    fn(xT[:, 0, :], bank("pk0", n)[:, 0:GT], ACT.Identity, bias=lat_gb[:, 2:3], scale=lat_gb[:, 0:1]).then_inc(done["pk0"], 1)
                    project_q(CROSS1)
                    attention(CROSS1)
                    copy_xT("X2")
                    act.wait_ge(w_ffn, 80)
                    n = nth("pk0", "F2", 0)
                    act.wait_ge(full["pk0"], n)
                    fn(ptok, bank("pk0", n)[:, 0:GT], ACT.Copy).then_inc(done["pk0"], 1)
                    for i in range(FF // 128):
                        n = nth("pb", "F2", i)
                        act.wait_ge(full["pb"], n)
                        fn(hid[:, i, :], bank("pb", n)[:, 0:GT], ACT.Gelu_apprx_tanh, bias=b1c[:, i:i + 1]).then_inc(done["pb"], 1)
                    act.wait_ge(full["po"], 1)
                    fn(qtok, bank("po", 1)[:, 0:GT], ACT.Identity, bias=one64[:]).then_inc(done["po"], 1)
                    copy_xT("X3")
                    act.wait_ge(w_self3, 96)
                    self_project(3, SELF3)
                    attention(SELF3)
                    copy_xT("X4")
                    project_q(CROSS4)
                    attention(CROSS4)
                    half_high(0)
                    copy_xT("X5")
                    act.wait_ge(done["pk1"], nth("pk1", "X5", 0))
                    act.wait_ge(done["pk0"], nth("pk0", "X5", 0))
                    fn(x_parts[:, 0], xT[:], ACT.Copy).then_inc(x_hi, 1)
                    half_high(1)
                    act.wait_ge(logit_made, 1)
                    fn(comb[:, 2, :, :].rearrange("p b e -> p (b e)"), comb[:, 1, :, :].rearrange("p b e -> p (b e)"), ACT.Exp).then_inc(exp_made, 1)
                    for k in range(2, 4):
                        half_high(k)
                    for i in range(NE * FC + 1):
                        if i < NE * FC:
                            if i == FC + 1:
                                n = nth("pk0", "M5", 0)
                                act.wait_ge(full["pk0"], n)
                                fn(ctop[0:E, :], bank("pk0", n)[0:E, 0:GT], ACT.Copy).then_inc(done["pk0"], 1)
                            n = nth("pb", "M5", i)
                            act.wait_ge(full["pb"], n)
                            fn(hid[:, i % 4, :], bank("pb", n)[:, 0:GT], ACT.Silu).then_inc(done["pb"], 1)
                        if i > 0:
                            if i - 1 < FC:
                                act.wait_ge(done["pb"], nth("pb", "M5", i - 1))
                            else:
                                act.wait_ge(gated, i - FC)
                            fn(hid_hi[:, (i - 1) % 4, :], hid[:, (i - 1) % 4, :], ACT.Copy).then_inc(hid_hi_made, 1)
                        if i % FC in (1, 3) and i // FC + 2 <= NE:
                            k = 2 * (i // FC + 1) + (i % FC == 3)
                            if k >= 4:
                                half_high(k)

                @block.gpsimd
                def _(pool):
                    steps = [0]

                    def block_diagonal(L, b):
                        for c in range(C):
                            ins = nc.gpsimd.tensor_tensor(*q_operands(L, b, c, qbd), ALU.mult)
                        ins.then_inc(qbd_made, 1)

                    def q_bf16(L, b):
                        if b > 1:
                            pool.wait_ge(full["pa"], pa_max(L, b - 2, L.heads - 1))
                        else:
                            pool.wait_ge(qbdb_made, QBDB[L.p] + 2)
                        for c in range(C):
                            nc.gpsimd.tensor_tensor(*q_operands(L, b, c, qbdb), ALU.mult).then_inc(qbdb_made, 1)

                    def diagonal_shifts(L, b, hg):
                        d = hg_of(L, b, hg)
                        if d >= 4:
                            for_L, bb, hh = owner(d - 4)
                            pool.wait_ge(full["pb"], pb_exp(for_L, bb, hh, len(for_L.tiles) - 1))
                        pool.wait_ge(done["pa"], pa_max(L, b, 4 * hg + 3 if isinstance(L, Cross) else hg))
                        dst = dshift[:, d % 4, :].rearrange("p (h t) -> p h t", h=4)
                        i3 = ident[0:T, 0:T].unsqueeze(1).broadcast_to([T, 4, T])
                        m = shift[:, b % 2, 4 * hg:4 * hg + 4].unsqueeze(2).broadcast_to([T, 4, T])
                        nc.gpsimd.tensor_tensor(dst, i3, m, ALU.mult).then_inc(dshift_made, 1)

                    def owner(d):
                        for L in (SELF0, CROSS1, SELF3, CROSS4):
                            d0 = hg_of(L, 0, 0)
                            if d0 <= d < d0 + G * L.hgs:
                                return L, (d - d0) // L.hgs, (d - d0) % L.hgs

                    def inverse_std(what, b):
                        r = ASK[(what, b)]
                        P, n = (128, 3) if what == "cx" else (T, 1)
                        pool.wait_ge(var_made, r + 1)
                        nc.gpsimd.tensor_scalar(vare[0:P, r % 4, 0:n], mv[0:P, r % 4, 0:n, 1], EPS, None, ALU.add).then_inc(pool_step, 1)
                        steps[0] += 1
                        pool.wait_ge(pool_step, steps[0])
                        nc.gpsimd.tensor_tensor(rstd[0:P, r % 4, 0:n], vare[0:P, r % 4, 0:n], neghalf[0:P, 0:n], ALU.pow).then_inc(rstd_made, 1)

                    def attention(L):
                        ph = L.p
                        for c in range(C):
                            ring, n = q_fill(L, c)
                            pool.wait_ge(done[ring], n)
                        if L is CROSS1:
                            block_diagonal(L, 0)
                        for hg in range(L.lead):
                            diagonal_shifts(L, 0, hg)
                        if isinstance(L, Cross):
                            q_bf16(L, 1)
                        for u in range(G * L.hgs):
                            b, hg = divmod(u, L.hgs)
                            if L is SELF0 and hg == 1 and b >= 2:
                                inverse_std("z", b - 2)
                            if L is SELF0 and hg == 2 and b > 0:
                                inverse_std("S0", b - 1)
                            if L is SELF0 and hg == 2 and b >= 2:
                                inverse_std("cx", b - 2)
                            if L is not SELF0 and L.hgs == 4 and b > 0 and hg == L.hgs - 1:
                                inverse_std(ph, b - 1)
                            if u + L.lead < G * L.hgs:
                                diagonal_shifts(L, (u + L.lead) // L.hgs, (u + L.lead) % L.hgs)
                            if L is CROSS1 and hg == 0 and b + 2 < G:
                                inverse_std("cx", b + 2)
                            if L is CROSS1 and b > 0 and hg == L.hgs - 1:
                                inverse_std(ph, b - 1)
                            if isinstance(L, Cross) and hg == 1 and b + 2 < G:
                                q_bf16(L, b + 2)
                            if L is CROSS1 and hg == 0 and b + 1 < G:
                                if b > 0:
                                    pool.wait_ge(full["pb"], pb_exp(L, b - 1, L.hgs - 1, len(L.tiles) - 1))
                                block_diagonal(L, b + 1)
                        if L is not SELF0:
                            inverse_std(ph, G - 1)

                    pool.memset(qstack[NSTACK:NSTACK + 3], 1.0).then_inc(pool_step, 1)
                    steps[0] += 1
                    pool.wait_ge(pool_step, 1)
                    pool.wait_ge(w_const, 128)
                    attention(SELF0)
                    for what, b in (("z", 2), ("S0", 3), ("z", 3)):
                        inverse_std(what, b)
                    attention(CROSS1)
                    pool.wait_ge(pv_done, hg_of(CROSS1, G - 1, 1) + 1)
                    pool.memset(vx[:], 1.0).then_inc(vx_ones, 1)
                    for b in range(G):
                        inverse_std("F2", b)
                    attention(SELF3)
                    attention(CROSS4)
                    for k in range(2 * NE):
                        pool.wait_ge(half_hi, k + 1)
                        nc.gpsimd.tensor_tensor(half_parts(k)[1], half(k), half_parts(k)[0].bitcast(F32), ALU.subtract).then_inc(half_lo, 1)
                    for b in range(G):
                        inverse_std("M5", b)

                @block.vector
                def _(dve):
                    v = nc.vector
                    steps = [0]

                    def then(ins):
                        ins.then_inc(dve_step, 1)
                        steps[0] += 1
                        dve.wait_ge(dve_step, steps[0])

                    def copy_xT(ph):
                        n = nth("pk1", ph, 0)
                        dve.wait_ge(full["pk1"], n)
                        v.tensor_copy(xT[:, 1, :], bank("pk1", n)[:, 0:GT]).then_inc(done["pk1"], 1)

                    def moments(src, what, b):
                        r = ASK[(what, b)]
                        then(v.bn_stats(bn6[0:T, r % 4, :], src))
                        v.bn_aggr(mv[0:T, r % 4, 0, :], bn6[0:T, r % 4, :]).then_inc(var_made, 1)

                    def normalised(dst, src, what, b, signal):
                        r = ASK[(what, b)]
                        dve.wait_ge(rstd_made, r + 1)
                        v.tensor_scalar(dst, src, mv[0:T, r % 4, 0, 0:1], rstd[0:T, r % 4, 0:1], ALU.subtract, ALU.mult).then_inc(signal, 1)

                    def split(src, c, ring, n, dst, made):
                        dve.wait_ge(done[ring], n)
                        then(v.tensor_copy(dst[:, 0, c], src[:, c]))
                        then(v.tensor_tensor(rest[:, c], src[:, c], dst[:, 0, c], ALU.subtract))
                        then(v.tensor_copy(dst[:, 1, c], rest[:, c]))
                        v.tensor_tensor(dst[:, 2, c], rest[:, c], dst[:, 1, c], ALU.subtract).then_inc(made, 1)

                    def add_x(src, b, ring_n=None, ring=None, residual=None):
                        ins = v.tensor_tensor(y[:, b % 2, :], src, (x if residual is None else residual)[:, b, :], ALU.add)
                        if ring_n is None:
                            then(ins)
                        else:
                            ins.then_inc(done[ring], 1)
                            dve.wait_ge(done[ring], ring_n)

                    def sums_and_norms(ph, first):
                        for b in range(G + 1):
                            if b < G:
                                n = nth("pa", ph, first + b)
                                if b > 1:
                                    dve.wait_ge(ln_done, LN[ph] + b - 1)
                                dve.wait_ge(full["pa"], n)
                                add_x(bank("pa", n)[0:T, 0:D], b, n, "pa")
                                moments(y[:, b % 2, :], ph, b)
                            if b > 0:
                                normalised(x[:, b - 1, :], y[:, (b - 1) % 2, :], ph, b - 1, ln_done)

                    def self_values(li, L):
                        for b in range(G):
                            n = v_fill(L, b)
                            dve.wait_ge(full["pa"], n)
                            v.tensor_tensor(v16[:, b, :, 0:16], bank("pa", n)[0:T, 0:D].rearrange("p (h d) -> p h d", h=16),
                                            bv[li][:].rearrange("p (h d) -> p h d", h=16), ALU.add).then_inc(done["pa"], 1)

                    def context_stats(b):
                        s, r = b % 2, ASK[("cx", b)]
                        dve.wait_ge(cx_in[s], 32 * (b // 2 + 1))
                        for j, (j0, J) in enumerate(JT):
                            ins = v.bn_stats(bn6_cx[0:J, j, :], cx[0:J, s, j, :])
                        then(ins)
                        for j, (j0, J) in enumerate(JT):
                            ins = v.bn_aggr(mv[0:J, r % 4, j, :], bn6_cx[0:J, j, :])
                        ins.then_inc(var_made, 1)

                    def context_normalised(b):
                        s, r = b % 2, ASK[("cx", b)]
                        dve.wait_ge(rstd_made, r + 1)
                        for j, (j0, J) in enumerate(JT):
                            ins = v.tensor_scalar(cx[0:J, s, j, :], cx[0:J, s, j, :], mv[0:J, r % 4, j, 0:1], rstd[0:J, r % 4, j:j + 1], ALU.subtract, ALU.mult)
                        ins.then_inc(cz_made, 1)

                    def turned(L, b):
                        n = kv_fill(L, b, "pk1", 0)
                        dve.wait_ge(full["pk1"], n)
                        v.tensor_scalar(cT[:, b % 2, 1, :], bank("pk1", n)[0:CK, 0:S], in_gb[:, 1:2], in_gb[:, 3:4], ALU.mult, ALU.add).then_inc(done["pk1"], 1)

                    def keys_bf16(L, b):
                        dve.wait_ge(done["pk0"], kv_fill(L, b, "pk0", 2))
                        v.tensor_copy(kxTb[:, b % 2, :, 0:S], kxT[:, b % 2, :, :]).then_inc(kTb_made, 1)

                    def mask_bias(b, batch):
                        row = rowmask[:, bass.ds(batch * S, S)]
                        v.tensor_scalar(rowbias[:, b % 2, :], row, 1.0, BIG, ALU.subtract, ALU.mult).then_inc(bias_made, 1)
                        for P, j0, j1 in ((128, 0, 2), (S - 256, 2, 3)):
                            col = colmask[0:P, j0:j1, bass.ds(batch, 1)].rearrange("p j a -> p (j a)")
                            v.tensor_scalar(colbias[0:P, b % 2, j0:j1], col, 1.0, BIG * CROSS4.scale, ALU.subtract, ALU.mult).then_inc(bias_made, 1)

                    def q_bf16(L, b, chunks=range(C)):
                        for c in chunks:
                            if b == 0:
                                ring, n = q_fill(L, c)
                                dve.wait_ge(done[ring], n)
                            v.tensor_tensor(*q_operands(L, b, c, qbdb), ALU.mult).then_inc(qbdb_made, 1)

                    def block_diagonal(L, b):
                        for c in range(C):
                            ring, n = q_fill(L, c)
                            dve.wait_ge(done[ring], n)
                            ins = v.tensor_tensor(*q_operands(L, b, c, qbd), ALU.mult)
                        ins.then_inc(qbd_made, 1)

                    def content(b, hg):
                        n = pa_content(b, hg)
                        dve.wait_ge(full["pa"], n)
                        v.scalar_tensor_tensor(
                            out=s0[:, b % 2, 4 * hg:4 * hg + 4, :], in0=bank("pa", n)[0:T, 0:4 * T].rearrange("p (h t) -> p h t", h=4), scalar=SELF0.scale,
                            in1=pos.rearrange("p (h b) t -> p h b t", b=G)[:, 4 * hg:4 * hg + 4, b, :],
                            op0=ALU.mult, op1=ALU.add).then_inc(done["pa"], 1)

                    def wait_shift(L, b):
                        if b > 1:
                            dve.wait_ge(dshift_made, hg_of(L, b - 2, L.hgs - 1) + 1)

                    def row_maxima(L, b, hg):
                        if hg == 0:
                            wait_shift(L, b)
                        n = pa_max(L, b, hg)
                        dve.wait_ge(full["pa"], n)
                        v.tensor_reduce(shift[:, b % 2, 4 * hg:4 * hg + 4], bank("pa", n)[0:T, 0:4 * T].rearrange("p (h t) -> p h t", h=4), AX, ALU.max).then_inc(done["pa"], 1)

                    def head_maxima(L, b, h):
                        if h == 0:
                            wait_shift(L, b)
                            if L.masked:
                                dve.wait_ge(bias_made, 3 * b + 3)
                        n = pa_max(L, b, h)
                        dve.wait_ge(full["pa"], n)
                        src, dst = bank("pa", n)[0:T, 0:S], shift[:, b % 2, h:h + 1]
                        if L.masked:
                            v.tensor_tensor_reduce(masked[:, n % DEPTH["pa"], :], src, rowbias[:, b % 2, :], 1.0, -3.4e38, ALU.add, ALU.max, dst).then_inc(done["pa"], 1)
                        else:
                            v.tensor_reduce(dst, src, AX, ALU.max).then_inc(done["pa"], 1)

                    def epilogue(L, b, part):
                        if part == 0:
                            ring, n = out_fill(L, b, 0)
                            dve.wait_ge(full[ring], n)
                            p = bank(ring, n)[0:T, :]
                            H = L.heads
                            if L is CROSS1:
                                sums = p.rearrange("p (i r) -> p i r", r=32)[:, 8:16, 0]
                                heads = p[:, 0:D].rearrange("p (h d) -> p h d", h=H)
                            else:
                                sums = p.rearrange("p (i r) -> p i r", r=32)[:, :, 16]
                                heads = p.rearrange("p (i r) -> p i r", r=32)[:, :, 0:16]
                            then(v.reciprocal(rec[:, 0:H], sums))
                            v.tensor_tensor(o[:].rearrange("p (h d) -> p h d", h=H), heads, rec[:, 0:H].unsqueeze(2).broadcast_to([T, H, D // H]), ALU.mult).then_inc(done[ring], 1)
                            if L.relative:
                                dve.wait_ge(done[ring], n)
                                add_x(o[:], b, residual=z)
                                moments(y[:, b % 2, :], L.p, b)
                        elif L.relative:
                            return
                        elif part == 1:
                            ring, n = out_fill(L, b, 1)
                            dve.wait_ge(full[ring], n)
                            v.tensor_copy(onT[:].rearrange("p c t -> p (c t)"), bank(ring, n)[:, 0:C * T]).then_inc(done[ring], 1)
                        else:
                            ring, n = out_fill(L, b, 2)
                            dve.wait_ge(full[ring], n)
                            add_x(bank(ring, n)[0:T, 0:D], b, n, ring)
                            if L is SELF3:
                                then(v.tensor_tensor(y[:, b % 2, :], y[:, b % 2, :], bo3[:], ALU.add))
                            moments(y[:, b % 2, :], L.p, b)

                    def do(steps):
                        for name, i, M, bb in steps:
                            if name == "turn":
                                turned(M, bb)
                            elif name == "keys" and M is CROSS4:
                                dve.wait_ge(k_high, 2 * bb + i + 1)
                                n = kv_fill(M, bb, "pk0", i)
                                v.tensor_tensor(k_rest[:, i, :], bank("pk0", n)[:, 0:S], kxTb[:, bb % 2, i, 0:S], ALU.subtract).then_inc(done["pk0"], 1)
                            elif name == "split":
                                dve.wait_ge(k_mid, 2 * bb + i + 1)
                                v.tensor_tensor(k_low[:, 1, i, :], k_rest[:, i, :], k_low[:, 0, i, :], ALU.subtract).then_inc(k_split, 1)
                            elif name == "keysb":
                                keys_bf16(M, bb)
                            elif name == "content":
                                content(bb, i)
                            elif name == "rows":
                                row_maxima(M, bb, i)
                            elif name == "head":
                                head_maxima(M, bb, i)
                            elif name == "stats":
                                context_stats(bb)
                            elif name == "cz":
                                context_normalised(bb)
                            elif name == "q" and M is SELF3:
                                dve.wait_ge(full["pa"], pa_max(M, bb - 2, 3))
                                q_bf16(M, bb)
                            elif name == "qbd":
                                if bb > 1:
                                    dve.wait_ge(full["pb"], pb_exp(M, bb - 2, 3, 0))
                                block_diagonal(M, bb)
                            elif name == "mask":
                                if bb > 1:
                                    dve.wait_ge(done["pb"], pb_exp(M, bb - 2, M.hgs - 1, 2))
                                mask_bias(bb, g * G + bb)
                            elif name == "out":
                                epilogue(M, bb, i)
                            elif name == "norm":
                                normalised(x[:, bb, :], y[:, bb % 2, :], M.p, bb, ln_done)

                    def attention(L):
                        if L is CROSS4:
                            q_bf16(L, 0, [0])
                            dve.wait_ge(q_high, C)
                            for c in range(C):
                                ring, n = q_fill(L, c)
                                dve.wait_ge(done[ring], n)
                            v.tensor_tensor(rest[:], qT[:], pieces[:, 0], ALU.subtract).then_inc(q_rest, 1)
                            q_bf16(L, 0, [1])
                            dve.wait_ge(q_mid, 1)
                            v.tensor_tensor(pieces[:, 2], rest[:], pieces[:, 1], ALU.subtract).then_inc(pieces_made, 1)
                        elif not L.relative:
                            q_bf16(L, 0)
                            if L is SELF3:
                                block_diagonal(L, 0)
                        else:
                            for hg in range(3):
                                content(0, hg)
                        for hg in range(L.lead):
                            if isinstance(L, Self):
                                row_maxima(L, 0, hg)
                            else:
                                for h in range(4 * hg, 4 * hg + 4):
                                    head_maxima(L, 0, h)
                        if L is SELF3:
                            q_bf16(L, 1)
                        for u in range(G * L.hgs):
                            b, hg = divmod(u, L.hgs)
                            for slot in range(len(L.tiles) + 1):
                                do(beside(L, b, hg, slot))
                            if L is SELF0 and b >= 2:
                                if hg == 0:
                                    dve.wait_ge(ln_done, b - 1)
                                    moments(x[:, b - 2, :], "z", b - 2)
                                elif hg == 1:
                                    context_stats(b - 2)
                                elif hg == 2:
                                    normalised(z[:, b - 2, :], x[:, b - 2, :], "z", b - 2, z_made)
                                elif b == 2:
                                    context_normalised(0)
                        if L is SELF0:
                            dve.wait_ge(ln_done, 3)
                            moments(x[:, 2, :], "z", 2)
                            epilogue(L, G - 1, 0)
                            context_normalised(1)
                            normalised(x[:, 3, :], y[:, 1, :], "S0", 3, ln_done)
                            dve.wait_ge(ln_done, LN["C1"])
                            moments(x[:, 3, :], "z", 3)
                            normalised(z[:, 2, :], x[:, 2, :], "z", 2, z_made)
                            normalised(z[:, 3, :], x[:, 3, :], "z", 3, z_made)
                            return
                        do(tail_of(L))

                    dve.wait_ge(x_in, (g + 1) * 16)
                    dve.wait_ge(y_out, g * (16 * G) + 1)
                    copy_xT("X0")
                    dve.wait_ge(w_self0, 48)
                    for c in range(C):
                        split(qT, c, *q_fill(SELF0, c), pieces, pieces_made)
                    dve.wait_ge(pieces_made, C)
                    for c in range(C):
                        split(kT, c, "pk0", k_fill(SELF0, c), k0_pieces, k0_made)
                    self_values(0, SELF0)
                    for k in range(0, 13, 2):
                        n = nth("pa", "S0", G + k // 2)
                        w = min(8, T - 8 * k)
                        dve.wait_ge(full["pa"], n)
                        v.tensor_copy(pos[:, :, 8 * k:8 * k + w], bank("pa", n)[0:T, 0:64 * w].rearrange("p (i m) -> p m i", i=w)).then_inc(done["pa"], 1)
                    dve.wait_ge(done["pa"], nth("pa", "S0", G + 6))
                    dve.wait_ge(done["pb"], nth("pb", "S0", 5))
                    dve.wait_ge(w_cross1, 96)
                    attention(SELF0)
                    n = nth("pk1", "X1", 0)
                    dve.wait_ge(full["pk1"], n)
                    v.tensor_scalar(xT[:, 1, :], bank("pk1", n)[:, 0:GT], lat_gb[:, 1:2], lat_gb[:, 3:4], ALU.mult, ALU.add).then_inc(done["pk1"], 1)
                    attention(CROSS1)
                    copy_xT("X2")
                    sums_and_norms("F2", 0)
                    copy_xT("X3")
                    dve.wait_ge(w_self3, 96)
                    dve.wait_ge(done["pk0"], k_fill(SELF3, C - 1))
                    v.tensor_copy(kTb[:], kT[:]).then_inc(kTb_made, 1)
                    self_values(3, SELF3)
                    attention(SELF3)
                    dve.wait_ge(w_cross4, 112)
                    mask_bias(0, g * G)
                    copy_xT("X4")
                    attention(CROSS4)
                    copy_xT("X5")
                    dve.wait_ge(done["pk0"], nth("pk0", "X5", 0))
                    dve.wait_ge(done["pk1"], nth("pk1", "X5", 0))
                    dve.wait_ge(pv_done, hg_of(CROSS4, G - 1, 3) + 1)
                    dve.wait_ge(x_hi, 1)
                    v.tensor_tensor(x_parts[:, 1], xT[:], x_parts[:, 0].bitcast(F32), ALU.subtract).then_inc(x_lo, 1)
                    n = nth("pa", "M5", 0)
                    dve.wait_ge(full["pa"], n)
                    dve.wait_ge(w_router, 48)
                    c = [comb[:, i, :, :] for i in range(12)]

                    def over_e(ap):
                        return ap.unsqueeze(2).broadcast_to([T, G, E])
                    v.tensor_tensor(c[0], bank("pa", n)[0:T, 0:G * E].rearrange("p (b e) -> p b e", b=G),
                                    rb[:].unsqueeze(1).broadcast_to([T, G, E]), ALU.add).then_inc(done["pa"], 1)
                    dve.wait_ge(done["pa"], n)
                    top = comb[:, 10, :, :].rearrange("p b e -> p (b e)")
                    then(v.tensor_reduce(top[:, 0:4], c[0], AX, ALU.max))
                    v.tensor_tensor(c[1], c[0], over_e(top[:, 0:4]), ALU.subtract).then_inc(logit_made, 1)
                    dve.wait_ge(exp_made, 1)
                    ranks = rank8[:].unsqueeze(1).broadcast_to([T, G, E])

                    def pick_first(src, dst, t):
                        then(v.tensor_reduce(top[:, t:t + 4], src, AX, ALU.max))
                        then(v.tensor_tensor(c[8], src, over_e(top[:, t:t + 4]), ALU.is_equal))
                        then(v.tensor_tensor(c[9], c[8], ranks, ALU.mult))
                        then(v.tensor_reduce(top[:, t + 4:t + 8], c[9], AX, ALU.max))
                        then(v.tensor_tensor(dst, c[9], over_e(top[:, t + 4:t + 8]), ALU.is_equal))
                    pick_first(c[2], c[3], 4)
                    then(v.scalar_tensor_tensor(out=c[4], in0=c[3], scalar=-2.0, in1=c[2], op0=ALU.mult, op1=ALU.add))
                    pick_first(c[4], c[5], 12)
                    then(v.tensor_tensor(c[6], c[3], c[5], ALU.add))
                    then(v.tensor_tensor(c[7], c[6], c[2], ALU.mult))
                    then(v.tensor_reduce(top[:, 20:24], c[7], AX, ALU.add))
                    then(v.reciprocal(top[:, 24:28], top[:, 20:24]))
                    then(v.memset(ctop[:, :], 0.0))
                    v.tensor_tensor(c[11], c[7], over_e(top[:, 24:28]), ALU.mult).then_inc(comb_made, 1)
                    for i in range(NE * FC + 1):
                        if FC <= i < NE * FC:
                            e = i // FC - 1
                            if i % FC == 0:
                                dve.wait_ge(full["pk1"], nth("pk1", "M5", e))
                            dve.wait_ge(done["pb"], nth("pb", "M5", i))
                            v.tensor_tensor(hid[:, i % 4, :], hid[:, i % 4, :], bank("pk1", 1)[:, 0:GT], ALU.mult).then_inc(gated, 1)
                        if i > 0:
                            h = hid[:, (i - 1) % 4, :]
                            dve.wait_ge(hid_hi_made, i)
                            v.tensor_tensor(hid_lo[:, (i - 1) % 4, :], h, hid_hi[:, (i - 1) % 4, :].bitcast(F32), ALU.subtract).then_inc(hid_lo_made, 1)
                    for i in range(C):
                        n = nth("pa", "M5", 1 + i)
                        dve.wait_ge(full["pa"], n)
                        v.tensor_copy(yT[:, i, :], bank("pa", n)[:, 0:GT]).then_inc(done["pa"], 1)
                    sums_and_norms("M5", 1 + C)

            nums = [s.num for s in group_sems]
            assert max(nums) - min(nums) == len(nums) - 1
            nc.gpsimd.sem_clear(range(min(nums), max(nums) + 1))
            nc.all_engine_barrier()

        nc.sync.wait_ge(y_out, 16 * B + 1)
        nc.sync.wait_ge(x_in, 16 * (B // G + 1))


def kernel(**inputs):
    import numpy as np
    import ml_dtypes
    import concourse.bacc as bacc
    from concourse.bass_utils import run_bass_kernel_spmd

    i = {k: np.asarray(v) for k, v in inputs.items()}

    def rows(w, n):
        return w.reshape(n, w.shape[0] // n, w.shape[1]).transpose(1, 0, 2)

    def col(v, n):
        return v.reshape(n, -1).T

    def padded(w, r, c):
        out = np.zeros((r, c), w.dtype)
        out[:w.shape[0], :w.shape[1]] = w
        return out

    def qkv(w, bias):
        w = w.reshape(16, 3, 16, D).transpose(1, 0, 2, 3).reshape(3 * D, D).T
        bias = bias.reshape(16, 3, 16).transpose(1, 0, 2).reshape(3, D)
        return rows(w, C), col(bias[:2].reshape(-1), 4), bias[2]

    a = {"x": i["x"], "ctx": i["ctx_768"], "ctxT": i["ctx_768"].transpose(0, 2, 1)}
    a["wqkv0"], a["bqk0"], a["bv0"] = qkv(i["L0_attn_Wqkv"], i["L0_attn_bqkv"])
    a["wqkv3"], a["bqk3"], a["bv3"] = qkv(i["L1_attn_qkv_w"], i["L1_attn_qkv_b"])
    a["wr_stack"] = np.vstack([i["L0_attn_Wr"].T] * len(PIECES) + [i["L0_attn_br"][None]] * 3)
    a["wq1"], a["wq4"] = rows(i["L0_xattn_W_Q"], C), rows(i["L1_xattn_Wq"], C)
    a["wk1"], a["wk4"] = rows(i["L0_xattn_W_K"], 2), rows(i["L1_xattn_Wk"], 2)
    a["wv1"], a["wv4"] = rows(i["L0_xattn_W_V"], 2), rows(i["L1_xattn_Wv"], 2)
    a["wo1"], a["wo4"] = rows(i["L0_xattn_W_O"], C), rows(i["L1_xattn_Wo"], C)
    a["wo3"], a["bo3"] = rows(i["L1_attn_out_w"].T, C), i["L1_attn_out_b"]
    a["lat_gb"] = np.hstack([col(i["L0_xattn_ln_lat_g"], 2), col(i["L0_xattn_ln_lat_b"], 2)])
    a["in_gb"] = np.hstack([col(i["L0_xattn_ln_in_g"], 2), col(i["L0_xattn_ln_in_b"], 2)])
    a["u1"] = rows(padded(i["L0_ffn_U1"], D, 128), C)
    a["v1"] = padded(i["L0_ffn_V1"], 128, FF)
    a["u2"] = rows(padded(i["L0_ffn_U2"], FF, 128), FF // 128)
    a["v2"] = padded(np.vstack([i["L0_ffn_V2"], i["L0_ffn_b2"][None]]), 128, D)
    a["b1c"] = col(i["L0_ffn_b1"], FF // 128)
    a["rw"], a["rb"] = rows(i["L1_ffn_router_w"].T, C), i["L1_ffn_router_b"]
    up = np.concatenate([i["L1_ffn_shared_w_up"], i["L1_ffn_w_up"]])
    down = np.concatenate([i["L1_ffn_shared_w_down"], i["L1_ffn_w_down"]])
    a["experts"] = np.concatenate([
        up.transpose(0, 2, 1).reshape(NE, C, 128, F).transpose(0, 2, 1, 3).reshape(NE, 128, C * F),
        down.transpose(0, 2, 1).reshape(NE, FC, 128, D).transpose(0, 2, 1, 3).reshape(NE, 128, FC * D)], axis=2)
    a["mask"] = i["mask_BxS2_bf1"].view(np.uint8)
    a["maskT"] = a["mask"].T

    f32 = np.float32
    p = np.arange(128)
    a["ident"] = np.eye(128, dtype=f32)
    a["mask16"] = (p[:, None] // 16 == np.arange(8)).astype(f32)
    a["mask32"] = (p[:, None] // 32 == np.arange(4)).astype(f32)
    a["one64"] = (p[:, None] == RANK).astype(f32)
    a["neghalf"] = np.full((128, 4), -0.5, f32)
    a["rank8"] = np.tile(np.arange(E, 0, -1, dtype=f32), (T, 1))
    a["sele"] = np.repeat((p[:, None] == np.arange(E)).astype(f32)[:, :, None], 128, axis=2)
    t = np.arange(T)
    dist = np.abs(t[:, None] - t[None])
    slopes = 0.5 ** np.arange(16)
    a["alibi"] = (-4.0 * dist[:, None, :] * slopes[None, :, None]).astype(ml_dtypes.bfloat16)
    pick = np.zeros((NSTACK + 3, 3), f32)
    for s, w in enumerate(WPIECES):
        pick[16 * s:16 * s + 16, w] = 1
    pick[NSTACK:] = np.eye(3)
    a["w_pick"] = pick

    nc = bacc.Bacc("TRN2", target_bir_lowering=False, num_devices=1)
    arrays, aps = {}, {}
    for k, v in a.items():
        v = np.ascontiguousarray(v)
        arrays[f"in_{k}"] = v
        aps[k] = nc.dram_tensor(f"in_{k}", v.shape, mybir.dt.from_np(v.dtype), kind="ExternalInput").ap()
    out = nc.dram_tensor("out", (B, T, D), F32, kind="ExternalOutput").ap()
    decoder(nc, aps, out)
    r = run_bass_kernel_spmd(nc, [arrays], core_ids=[0])
    return r.results[0]["out"]
```
